# Optimizing a Trainium2 kernel written in Bass

```python
import numpy as np
import jax
import jax.numpy as jnp

def _softmax(x, axis=-1):
    return jax.nn.softmax(x, axis=axis)

def _gelu(x):
    return jax.nn.gelu(x, approximate=True)

def _silu(x):
    return jax.nn.silu(x)

def _sigmoid(x):
    return jax.nn.sigmoid(x)

def _layernorm(x, axis=-1, eps=1e-05):
    m = jnp.mean(x, axis=axis, keepdims=True)
    v = jnp.var(x, axis=axis, keepdims=True)
    return (x - m) / jnp.sqrt(v + eps)

def _scatter_add(tgt, idx, src, axis=0):
    return tgt.at[idx].add(src)

def _segment_sum(src, seg, n):
    return jax.ops.segment_sum(src, seg, n)
kernel_name = 'mk_seq_preln_d1_jaxref_r8_71c02e'

def setup_inputs(seed: int=0):
    np.random.seed(seed)
    _w = jnp.asarray

    def _L0_attn_setup():
        import jax, jax.numpy as jnp
        import numpy as np
        N_HEADS = 16
        N_KV_HEADS = 4
        MAX_TIMESCALE = 10000.0

        def rms_norm(x):
            var = jnp.mean(jnp.square(x.astype(jnp.float32)), axis=-1, keepdims=True)
            return (x * jax.lax.rsqrt(var + 1e-06)).astype(x.dtype)

        def rotate_half(x):
            x1, x2 = jnp.split(x, 2, axis=-1)
            return jnp.concatenate([-x2, x1], axis=-1)

        def sine_table(features, length):
            fraction = jnp.arange(0, features, 2, dtype=jnp.float32) / features
            inv_freq = 1.0 / MAX_TIMESCALE ** fraction
            sinusoid = jnp.arange(length, dtype=jnp.float32)[:, None] * inv_freq[None, :]
            sinusoid = jnp.concatenate([sinusoid, sinusoid], axis=-1)
            return (jnp.sin(sinusoid), jnp.cos(sinusoid))
        key = jax.random.key(seed)
        ks = jax.random.split(key, 5)
        B, T, C = (2, 128, 256)
        N, K = (N_HEADS, N_KV_HEADS)
        H = C // N
        init_std = np.sqrt(2.0 / (5.0 * C))
        wang_std = 2.0 / 24 / np.sqrt(N * H)
        x = jax.random.normal(ks[0], (B, T, C), dtype=jnp.float32)
        q_kernel = jax.random.normal(ks[1], (C, N * H), dtype=jnp.float32) * init_std
        k_kernel = jax.random.normal(ks[2], (C, K * H), dtype=jnp.float32) * init_std
        v_kernel = jax.random.normal(ks[3], (C, K * H), dtype=jnp.float32) * init_std
        out_kernel = jax.random.normal(ks[4], (N * H, C), dtype=jnp.float32) * wang_std
        return {'x': x, 'q_kernel': q_kernel, 'k_kernel': k_kernel, 'v_kernel': v_kernel, 'out_kernel': out_kernel}
    _L0_attn_in = _L0_attn_setup()

    def _L0_ffn_setup():
        import jax, jax.numpy as jnp
        import numpy as np
        TOP_K = 4
        key = jax.random.key(seed)
        ks = jax.random.split(key, 8)
        B, S, H = (1, 128, 256)
        E, I = (60, 176)
        I_SH = 704
        s = 0.02
        return {'hidden_states': jax.random.normal(ks[0], (B, S, H), jnp.float32), 'gate_w': jax.random.normal(ks[1], (E, H), jnp.float32) * s, 'shared_gate_w': jax.random.normal(ks[2], (1, H), jnp.float32) * s, 'w13': jax.random.normal(ks[3], (E, 2 * I, H), jnp.float32) * s, 'w2': jax.random.normal(ks[4], (E, H, I), jnp.float32) * s, 'se_gate_up_w': jax.random.normal(ks[5], (2 * I_SH, H), jnp.float32) * s, 'se_down_w': jax.random.normal(ks[6], (H, I_SH), jnp.float32) * s}
    _L0_ffn_in = _L0_ffn_setup()
    _d = {'L0_attn_x': _L0_attn_in['x'], 'L0_attn_q_kernel': _L0_attn_in['q_kernel'], 'L0_attn_k_kernel': _L0_attn_in['k_kernel'], 'L0_attn_v_kernel': _L0_attn_in['v_kernel'], 'L0_attn_out_kernel': _L0_attn_in['out_kernel'], 'L0_ffn_gate_w': _L0_ffn_in['gate_w'], 'L0_ffn_shared_gate_w': _L0_ffn_in['shared_gate_w'], 'L0_ffn_w13': _L0_ffn_in['w13'], 'L0_ffn_w2': _L0_ffn_in['w2'], 'L0_ffn_se_gate_up_w': _L0_ffn_in['se_gate_up_w'], 'L0_ffn_se_down_w': _L0_ffn_in['se_down_w']}
    _x0 = _d['L0_attn_x']
    _d['L0_attn_x'] = jax.random.normal(jax.random.fold_in(jax.random.key(seed), 1), (2, 1024, 256), dtype=_x0.dtype)
    del _x0
    return _d

def reference(L0_attn_x, L0_attn_q_kernel, L0_attn_k_kernel, L0_attn_v_kernel, L0_attn_out_kernel, L0_ffn_gate_w, L0_ffn_shared_gate_w, L0_ffn_w13, L0_ffn_w2, L0_ffn_se_gate_up_w, L0_ffn_se_down_w):

    def _L0_attn_ref(x, q_kernel, k_kernel, v_kernel, out_kernel):
        import jax, jax.numpy as jnp
        import numpy as np
        N_HEADS = 16
        N_KV_HEADS = 4
        MAX_TIMESCALE = 10000.0

        def rms_norm(x):
            var = jnp.mean(jnp.square(x.astype(jnp.float32)), axis=-1, keepdims=True)
            return (x * jax.lax.rsqrt(var + 1e-06)).astype(x.dtype)

        def rotate_half(x):
            x1, x2 = jnp.split(x, 2, axis=-1)
            return jnp.concatenate([-x2, x1], axis=-1)

        def sine_table(features, length):
            fraction = jnp.arange(0, features, 2, dtype=jnp.float32) / features
            inv_freq = 1.0 / MAX_TIMESCALE ** fraction
            sinusoid = jnp.arange(length, dtype=jnp.float32)[:, None] * inv_freq[None, :]
            sinusoid = jnp.concatenate([sinusoid, sinusoid], axis=-1)
            return (jnp.sin(sinusoid), jnp.cos(sinusoid))
        B, T, C = x.shape
        N, K = (N_HEADS, N_KV_HEADS)
        G = N // K
        H = C // N
        q = rms_norm(jnp.dot(x, q_kernel))
        k = rms_norm(jnp.dot(x, k_kernel))
        v = jnp.dot(x, v_kernel)
        q = q.reshape(B, T, K, G, H)
        k = k.reshape(B, T, K, H)
        v = v.reshape(B, T, K, H)
        sin, cos = sine_table(H, T)
        qcos = cos[None, :, None, None, :]
        qsin = sin[None, :, None, None, :]
        kcos = cos[None, :, None, :]
        ksin = sin[None, :, None, :]
        q = (q * qcos + rotate_half(q) * qsin).astype(x.dtype)
        k = (k * kcos + rotate_half(k) * ksin).astype(x.dtype)
        scale = jax.lax.rsqrt(jnp.array(H, dtype=jnp.float32)).astype(q.dtype)
        logits = jnp.einsum('btkgh,bskh->bkgts', q * scale, k)
        probs = jax.nn.softmax(logits.astype(jnp.float32), axis=-1).astype(logits.dtype)
        encoded = jnp.einsum('bkgts,bskh->btkgh', probs, v)
        encoded = encoded.reshape(B, T, N * H)
        return jnp.dot(encoded, out_kernel)

    def _L0_ffn_ref(hidden_states, gate_w, shared_gate_w, w13, w2, se_gate_up_w, se_down_w):
        import jax, jax.numpy as jnp
        import numpy as np
        TOP_K = 4
        orig_shape = hidden_states.shape
        E, H = gate_w.shape
        I = w2.shape[2]
        x = hidden_states.reshape(-1, H)
        M = x.shape[0]
        gu = x @ se_gate_up_w.T
        I_sh = se_down_w.shape[1]
        shared = jax.nn.silu(gu[:, :I_sh]) * gu[:, I_sh:] @ se_down_w.T
        shared = shared * jax.nn.sigmoid(x @ shared_gate_w.T)
        logits = x @ gate_w.T
        probs = jax.nn.softmax(logits.astype(jnp.float32), axis=-1)
        weights, sel = jax.lax.top_k(probs, TOP_K)
        cw = jnp.zeros((M, E), jnp.float32).at[jnp.arange(M)[:, None], sel].add(weights)

        def step(acc, ews):
            w13_e, w2_e, cw_e = ews
            gu_e = x @ w13_e.T
            h = jax.nn.silu(gu_e[:, :I]) * gu_e[:, I:]
            return (acc + cw_e[:, None] * (h @ w2_e.T), None)
        sparse, _ = jax.lax.scan(step, jnp.zeros((M, H), jnp.float32), (w13, w2, cw.T))
        return (shared + sparse).reshape(orig_shape)
    x = L0_attn_x
    x = x + _L0_attn_ref(_layernorm(x, axis=-1), L0_attn_q_kernel, L0_attn_k_kernel, L0_attn_v_kernel, L0_attn_out_kernel)
    x = x + _L0_ffn_ref(_layernorm(x, axis=-1), L0_ffn_gate_w, L0_ffn_shared_gate_w, L0_ffn_w13, L0_ffn_w2, L0_ffn_se_gate_up_w, L0_ffn_se_down_w)
    return x

_drawn_inputs = setup_inputs


def setup_inputs(seed=0):
    import zlib

    import numpy as np

    out = dict(_drawn_inputs(seed))
    spreads = {}
    factors = {'L0_attn_q_kernel': 8.0,
     'L0_attn_k_kernel': 8.0,
     'L0_attn_v_kernel': 8.0,
     'L0_attn_out_kernel': 8.0,
     'L0_ffn_gate_w': 8.0,
     'L0_ffn_shared_gate_w': 8.0,
     'L0_ffn_w13': 8.0,
     'L0_ffn_w2': 8.0,
     'L0_ffn_se_gate_up_w': 3.997,
     'L0_ffn_se_down_w': 4.004}
    for name, (base, spread) in spreads.items():
        noise = np.random.default_rng([zlib.crc32(name.encode()), seed]).standard_normal(out[name].shape)
        drawn = base * np.exp(spread * noise) if base else spread * noise
        out[name] = jnp.asarray(drawn.astype(out[name].dtype))
    for name, factor in factors.items():
        out[name] = (out[name] * factor).astype(out[name].dtype)
    return out
```

```python
from contextlib import ExitStack

import numpy as np

import concourse.bass as bass
from concourse import mybir

ACT = mybir.ActivationFunctionType
ALU = mybir.AluOpType
AX = mybir.AxisListType
F32 = mybir.dt.float32
F32R = mybir.dt.float32r
BF16 = mybir.dt.bfloat16
I32 = mybir.dt.int32
U32 = mybir.dt.uint32

B, T, C = 2, 1024, 256
NH, NKV, HD = 16, 4, 16
NT = B * T // 128
E, I, TOPK = 60, 176, 4
ISH = 704
CAP = B * T
SLOTS = 256
AWAY = 1 << 20
ROW = 260
NPAIR = B * T * TOPK
WPK = 2 * 2 * I + 2 * C

NMORE = CAP // 128 - SLOTS // 128
C_ID, C_TRI, C_COS, C_SIN, C_IOTA, C_DID, C_MH = np.cumsum([0, 128, 128, 128, 128, 60, 64]).tolist()
NCST = C_MH + 4


def constants():
    c = np.zeros((128, NCST), np.float32)
    p = np.arange(128)
    c[:, C_ID:C_ID + 128] = np.eye(128)
    c[:, C_TRI:C_TRI + 128] = p[:, None] < p[None, :]
    frac = np.arange(0, HD, 2, dtype=np.float32) / np.float32(HD)
    inv = np.float32(1.0) / np.power(np.float32(10000.0), frac, dtype=np.float32)
    ang = np.arange(T, dtype=np.float32)[:, None] * inv[None, :]
    cos, sin = np.cos(ang.astype(np.float64)), np.sin(ang.astype(np.float64))
    cos = np.concatenate([cos, cos], 1).reshape(T // 128, 128, HD)
    sin = np.concatenate([-sin, sin], 1).reshape(T // 128, 128, HD)
    c[:, C_COS:C_COS + 128] = cos.transpose(1, 0, 2).reshape(128, -1)
    c[:, C_SIN:C_SIN + 128] = sin.transpose(1, 0, 2).reshape(128, -1)
    c[:, C_IOTA:C_IOTA + E] = np.arange(E)
    tok = np.arange(NT)[None, :, None] * 128 + p[:, None, None]
    c[:, C_DID:C_DID + NT * TOPK] = (tok * TOPK + np.arange(TOPK)).reshape(128, -1)
    c[:, C_MH:C_MH + 4] = -0.5
    return c


class Ctr:

    def __init__(self, sem):
        self.sem, self.n = sem, 0


class Eng:

    def __init__(self, sem):
        self.ctr, self.prog, self.met = Ctr(sem), [], {}

    def wait(self, *marks):
        for m in marks:
            if m is None:
                continue
            if isinstance(m, list):
                self.wait(*m)
                continue
            c, v = m
            if self.met.get(id(c), 0) < v:
                self.met[id(c)] = v
                self.prog.append(lambda e, c=c, v=v: e.wait_ge(c.sem, v))

    def __call__(self, fn, *marks):
        self.wait(*marks)
        c = self.ctr
        c.n += 1
        self.prog.append(lambda e: fn(e).then_inc(c.sem, 1))
        return (c, c.n)

    def dma(self, c, fn, *marks):
        self.wait(*marks)
        c.n += 16
        self.prog.append(lambda e: fn(e).then_inc(c.sem, 16))
        return (c, c.n)

    def last(self):
        return (self.ctr, self.ctr.n) if self.ctr.n else None

    def run(self, eng):
        for f in self.prog:
            f(eng)


class Bank:

    def __init__(self, ap):
        self.ap, self.free = ap, []


class Turns:

    def __init__(self, items):
        self.items, self.i = items, -1

    def __call__(self):
        self.i += 1
        return self.items[self.i % len(self.items)]


class Region:

    def __init__(self, nc, base, end):
        self.nc, self.at, self.end = nc, base, end

    def __call__(self, name, shape, dt):
        n = int(np.prod(shape[1:])) * (2 if dt == BF16 else 4)
        t = self.nc.alloc_sbuf_tensor_at(name, shape, dt, offset=self.at)
        self.at += -(-n // 32) * 32
        assert self.at <= self.end, (name, self.at, self.end)
        return t


def moe_block_kernel(nc, x, wqkv, wos, gw, wsh1, wsh2, wpk, cst, out, upto=99):
    ctx = ExitStack()
    sem = lambda name: ctx.enter_context(nc.semaphore(name))
    PE, V, S, G, Y = (Eng(sem(n)) for n in ("s_pe", "s_dve", "s_act", "s_pool", "s_sp"))
    dctr = {}

    def D(name):
        if name not in dctr:
            dctr[name] = Ctr(sem("d_" + name))
        return dctr[name]

    base, top = -(-nc.sbuf_base // 64) * 64, nc.sbuf_top
    P_ = Region(nc, base, top)
    X = P_("X", [128, NT, C], F32)
    xt0 = P_.at
    XTH = P_("XTH", [128, 4, 2, 512], F32R)
    XTL = P_("XTL", [128, 4, 2, 512], F32R)
    R0 = [Region(nc, xt0 + 8192, xt0 + 16384), Region(nc, xt0 + 24576, xt0 + 32768)]
    CST = P_("CST", [128, NCST], F32)
    IDB = P_("IDB", [128, 128], BF16)
    TRI = P_("TRI", [128, 128], BF16)
    ONE = P_("ONE", [128, 128], BF16)
    MAC = P_("MAC", [128, 4, E], BF16)
    ROWS = P_("ROWS", [128, 4, TOPK, ROW], F32)
    PF = P_("PF", [128, 2, ROW], F32)
    SIG = P_("SIG", [128, NT], F32)
    CNT = P_("CNT", [128, 64], I32)
    CNF = P_("CNF", [128, 64], F32)
    RKF = P_("RKF", [128, NT, TOPK], F32)
    EXF = P_("EXF", [128, NT, TOPK], F32)
    WKF = P_("WKF", [128, NT, TOPK], F32)
    ST = [P_(f"ST{i}", [128, 10], F32) for i in range(4)]
    SQ = [P_(f"SQ{i}", [128, 24], F32) for i in range(2)]
    a0 = P_.at
    R1 = Region(nc, a0, top)
    QT, KT, VS = [None, None], [None, None], [None, None]
    QT[0] = R1("QT0", [128, NH, 512], BF16)
    KT[0] = R1("KT0", [128, NKV, T], BF16)
    VS[0] = R1("VS0", [128, 8, NKV, 32], F32)
    WQH = R1("WQH", [128, 2, 384], F32R)
    WQL = R1("WQL", [128, 2, 384], F32R)
    XN = [R1(f"XN{i}", [128, C], F32) for i in range(2)]
    XNH = [R1(f"XNH{i}", [128, C], F32R) for i in range(2)]
    XNL = [R1(f"XNL{i}", [128, C], F32R) for i in range(2)]
    QS = [R1(f"QS{i}", [128, 320], F32) for i in range(2)]
    QD = R1("QD", [128, 4, 256], F32)
    RT = [R0[i](f"RT{i}", [128, 20, 16], F32) for i in range(2)]
    RU = [R0[i](f"RU{i}", [128, 20, 16], F32) for i in range(2)]
    EX = [R0[i](f"EX{i}", [128, 20, 8, 16], BF16) for i in range(2)]
    a1 = R1.at
    R2 = Region(nc, a1, top)
    QT[1] = R2("QT1", [128, NH, 512], BF16)
    KT[1] = R2("KT1", [128, NKV, T], BF16)
    VS[1] = R2("VS1", [128, 8, NKV, 32], F32)
    NP = 6
    PB = [R2(f"PB{i}", [128, 1024], F32) for i in range(NP)]
    ET = [R2(f"ET{i}", [128, 16, 32], F32) for i in range(2)]
    EM = R2("EM", [128, 16, 16], F32)
    ERC = R2("ERC", [128, 16, 1], F32)
    EHR = R2("EHR", [128, 16, 16], F32R)
    EHL = R2("EHL", [128, 16, 32], F32)
    ENC = R2("ENC", [128, NKV, 512], F32R)
    WOH = R2("WOH", [128, NKV, C], F32R)
    WOL = R2("WOL", [128, NKV, C], F32R)
    GWH = R2("GWH", [128, 2, 64], F32R)
    GWL = R2("GWL", [128, 2, 64], F32R)
    GL = R2("GL", [64, 512], F32)
    LG = R2("LG", [128, 4, 64], F32)
    GX = R2("GX", [128, 4, 65], F32)
    DEN = R2("DEN", [128, 2, 4], F32)
    MX = R2("MX", [128, 4, 8], F32)
    MI = R2("MI", [128, 4, 8], U32)
    OH = R2("OH", [128, 4, TOPK, E], BF16)
    PR = R2("PR", [128, 4, TOPK, E], F32)
    MB = R2("MB", [128, 4, E], BF16)
    MS = R2("MS", [128, E], F32)
    SLF = R2("SLF", [128, 4, TOPK], F32)
    SLI = [R2(f"SLI{i}", [128, 4 * TOPK], I32) for i in range(2)]

    PS = [ctx.enter_context(nc.psum_tensor(f"ps{i}", [128, 1024], F32)) for i in range(4)]
    half = lambda i: PS[i // 2][:, 512 * (i % 2):512 * (i % 2) + 512]
    bank = [Bank(half(i)) for i in range(8)]
    unit = [Bank(PS[i][:, :]) for i in range(2)]
    pvb = Turns(bank[4:6])
    misc = Turns(bank[6:8])

    XS = nc.dram_tensor("xs_scratch", [E * SLOTS, ROW], F32, kind="Internal").ap()
    YS = nc.dram_tensor("ys_scratch", [NPAIR, C], F32, kind="Internal").ap()

    def mm(o, l, r, st, sp, *w):
        return PE(lambda e: e.matmul(o, l, r, start=st, stop=sp), *w)

    def tr(o, i, ident, *w):
        return PE(lambda e: e.transpose(o, i, ident), *w)

    def cp(en, o, i, *w):
        if en is S:
            return S(lambda e: e.activation(o, i, ACT.Copy), *w)
        return en(lambda e: e.tensor_copy(o, i), *w)

    def act(o, i, f, *w, scale=1.0):
        return S(lambda e: e.activation(o, i, f, scale=scale), *w)

    def tt(en, o, a, b, op, *w):
        return en(lambda e: e.tensor_tensor(o, a, b, op), *w)

    def ts(en, o, a, s1, o1, *w):
        return en(lambda e: e.tensor_scalar(o, a, s1, None, o1), *w)

    def ts2(en, o, a, s1, s2, o1, o2, *w):
        return en(lambda e: e.tensor_scalar(o, a, s1, s2, o1, o2), *w)

    def stt(o, a, s, b, o1, o2, *w):
        return V(lambda e: e.scalar_tensor_tensor(o, a, s, b, o1, o2), *w)

    def red(o, a, *w):
        return V(lambda e: e.tensor_reduce(o, a, AX.X, ALU.add), *w)

    def count(o, a, *w):
        def do(e):
            with nc.allow_low_precision("a sum of four zeros and ones"):
                return e.tensor_reduce(o, a, AX.X, ALU.add)
        return V(do, *w)

    def bns(o, i, *w):
        return V(lambda e: e.bn_stats(o, i), *w)

    def bna(o, i, *w):
        return V(lambda e: e.bn_aggr(o, i), *w)

    def vtr(o, i, *w):
        return V(lambda e: e.transpose(o, i), *w)

    def rcp(o, i, *w):
        return V(lambda e: e.reciprocal(o, i), *w)

    def ms(en, o, v, *w):
        return en(lambda e: e.memset(o, v), *w)

    def f32(t):
        return t.bitcast(F32)

    def scaled(en, o, i, s, *w):
        if en is S:
            return act(o, i, ACT.Copy, *w, scale=s)
        return ts(en, o, i, s, ALU.mult, *w)

    d_c = Y.dma(D("cst"), lambda e: e.dma_start(CST[:, :], cst))
    xv = x.rearrange("(n p) c -> p n c", p=128)
    d_x = [None] * NT

    def load_x(en, q):
        m = en.dma(D(f"x{q}"), lambda e: e.dma_start(X[:, 4 * q:4 * q + 4, :], xv[:, 4 * q:4 * q + 4, :]))
        for i in range(4):
            d_x[4 * q + i] = m

    load_x(S, 0)
    WQR = PB[0][:, 0:768].rearrange("p (c n) -> p c n", c=2)
    WOR = PB[1][:, 0:1024].rearrange("p (g n) -> p g n", g=NKV)
    GWR = PB[2][:, 0:128].rearrange("p (c n) -> p c n", c=2)
    d_wq = Y.dma(D("wq"), lambda e: e.dma_start(WQR, wqkv.rearrange("(c p) n -> p c n", p=128)))
    load_x(S, 1)
    d_wo = Y.dma(D("wo"), lambda e: e.dma_start(WOR, wos.rearrange("(g p) n -> p g n", p=128)))
    d_gw = Y.dma(D("gw"), lambda e: e.dma_start(GWR, gw.rearrange("(c p) n -> p c n", p=128)))
    load_x(S, 2)
    load_x(Y, 3)

    IDF = CST[:, C_ID:C_ID + 128]
    MH = CST[:, C_MH:C_MH + 2]
    m_id = cp(V, IDB[:, :], CST[:, C_ID:C_ID + 128], d_c)
    m_tri = cp(V, TRI[:, :], CST[:, C_TRI:C_TRI + 128], d_c)
    m_one = ms(V, ONE[:, :], 1.0)
    m_mac = [ms(V, MAC[:, 0, :], 0.0)]
    m_vs1 = [ms(G, VS[b][:, :, :, 16:32], 1.0) for b in range(B)]
    m_rows = ms(G, ROWS[:, :, :, 258:260], 0.0)
    m_pf = ms(G, PF[:, :, :], 0.0)
    m_pf2 = ms(G, PF[:, :, 256:257], float(NPAIR), m_pf)

    xsv = XS.rearrange("(e p r) w -> p e (r w)", e=E, p=128)
    for q in range(4):
        G.dma(D("pf"), lambda e, q=q: e.dma_start(
            xsv[:, 15 * q:15 * q + 15, :], PF[:, :, :].rearrange("p j w -> p (j w)").unsqueeze(1).to_broadcast([128, 15, 2 * ROW])), m_pf2)
    d_pf = G.dma(D("pf"), lambda e: e.dma_start(
        YS.rearrange("(p r) c -> p r c", p=128),
        PF[:, 0, 0:C].unsqueeze(1).to_broadcast([128, NPAIR // 128, C])), m_pf2)

    def split(hi, lo, raw, w, e_hi=S, e_lo=V):
        h = cp(e_hi, hi, raw, w)
        return tt(e_lo, lo, raw, f32(hi), ALU.subtract, h)

    m_wq = split(WQH[:, :, :], WQL[:, :, :], WQR, d_wq)
    m_wo = m_gw = None

    cosT = CST[:, C_COS:C_COS + 128].rearrange("p (t d) -> p t d", d=16)
    sinT = CST[:, C_SIN:C_SIN + 128].rearrange("p (t d) -> p t d", d=16)
    fr = {}
    kt_ok = {}
    qt_ok = {}
    qt_free = {}

    def ln(src, st, key, *w):
        m = bns(st[:, 0:6], src, *w, fr.get(key))
        m = bna(st[:, 6:8], st[:, 0:6], m)
        m = ts(V, st[:, 9:10], st[:, 7:8], 1e-5, ALU.add, m)
        return tt(G, st[:, 8:9], st[:, 9:10], MH[:, 0:1], ALU.pow, m, d_c)

    def p1(i, full, e1, e2):
        p, (b, t) = i % 2, divmod(i, 8)
        st, sq = ST[p], SQ[p]
        m = ln(X[:, i, :], st, ("st", p), d_x[i])
        m = ts2(V, XN[p][:, :], X[:, i, :], st[:, 6:7], st[:, 8:9], ALU.subtract, ALU.mult, m, fr.get(("xn", p)))
        fr["st", p] = m
        yield
        k = misc()
        tr(k.ap[:, 0:128], XN[p][:, 0:128], IDF, m, k.free)
        m = tr(k.ap[:, 128:256], XN[p][:, 128:256], IDF)
        fr["xn", p] = m
        h = cp(e1, XNH[p][:, :], k.ap[:, 0:256], m, fr.get(("xnh", p)))
        m = tt(V, XNL[p][:, :], k.ap[:, 0:256], f32(XNH[p][:, :]), ALU.subtract, h)
        k.free = [m]
        yield
        k = misc()
        n = 0
        for l, r in ((XNH, WQH), (XNH, WQL), (XNL, WQH)):
            for c in range(2):
                mk = mm(k.ap[:, 0:384], l[p][:, 128 * c:128 * c + 128], r[:, c, :], n == 0, n == 5, m, m_wq, k.free)
                n += 1
        fr["xnh", p] = mk
        m1 = bns(sq[:, 0:6], k.ap[:, 0:256], mk, fr.get(("sq", p)))
        m2 = bns(sq[:, 6:12], k.ap[:, 256:320], mk)
        bna(sq[:, 12:14], sq[:, 0:6], m1)
        m = bna(sq[:, 14:16], sq[:, 6:12], m2)
        mv = sq[:, 12:16].rearrange("p (a b) -> p b a", b=2)
        m = tt(V, sq[:, 16:18], mv[:, 0, :], mv[:, 0, :], ALU.mult, m)
        m = stt(sq[:, 18:20], sq[:, 16:18], 1e-6, mv[:, 1, :], ALU.add, ALU.add, m)
        m = tt(G, sq[:, 20:22], sq[:, 18:20], MH, ALU.pow, m)
        yield
        q = QS[p][:, 0:256] if full else QD[:, i % 4, :]
        mv_ = cp(e1, VS[b][:, t, :, 0:16], k.ap[:, 320:384].rearrange("p (g d) -> p g d", d=16), m)
        mk_ = scaled(e1, QS[p][:, 256:320], k.ap[:, 256:320], sq[:, 21:22], m, fr.get(("qs", p)))
        mq = scaled(e1, q, k.ap[:, 0:256], sq[:, 20:21], m, fr.get(("qd", i % 4)) if not full else None)
        k.free = [mv_, mk_, mq, m]
        fr["sq", p] = [mk_, mq]
        vs_ok[i] = [mv_, m_vs1[b]]
        if full:
            yield from rope(i, QS[p][:, :].rearrange("p (h d) -> p h d", d=16), 0, 20, [mq, mk_], e1, e2, ("qs", p))
        else:
            fr["qd_ok", i % 4] = mq
            yield from rope(i, QS[p][:, 256:320].rearrange("p (h d) -> p h d", d=16), 16, 20, [mk_], e1, e2, ("qs", p))

    vs_ok = {}

    def later(i, e1, e2):
        yield from rope(i, QD[:, i % 4, :].rearrange("p (h d) -> p h d", d=16), 0, 16, [fr["qd_ok", i % 4]], e1, e2, ("qd", i % 4))

    def rope(i, src, h0, h1, w, e1, e2, skey):
        p, (b, t), nh = i % 2, divmod(i, 8), h1 - h0
        rt, ru, ex = RT[p][:, h0:h1, :], RU[p][:, h0:h1, :], EX[p]
        co = cosT[:, t:t + 1, :].to_broadcast([128, nh, 16])
        si = sinT[:, t:t + 1, :].to_broadcast([128, nh, 16])
        m1 = tt(e2, rt, src, co, ALU.mult, w, d_c, fr.get(("rt", p)))
        m2 = tt(V, ru[:, :, 0:8], src[:, :, 8:16], si[:, :, 0:8], ALU.mult, w, fr.get(("rt", p)))
        m3 = tt(V, ru[:, :, 8:16], src[:, :, 0:8], si[:, :, 8:16], ALU.mult, w)
        fr[skey] = [m1, m3]
        yield
        m = tt(V, rt, rt, ru, ALU.add, m1, m3)
        a1 = cp(V, ex[:, h0:h1, 0, :], rt, m, fr.get(("ex", p)))
        m = tt(V, ru, rt, ex[:, h0:h1, 0, :], ALU.subtract, a1)
        a2 = cp(V, ex[:, h0:h1, 1, :], ru, m)
        m = tt(V, rt, ru, ex[:, h0:h1, 1, :], ALU.subtract, a2)
        yield
        done = []
        if h0 == 0:
            a3 = cp(V, ex[:, 0:16, 6, :], rt[:, 0:16, :], m)
            done.append(cp(V, ex[:, 0:16, 2:4, :], ex[:, 0:16, 0:1, :].to_broadcast([128, 16, 2, 16]), a1))
            done.append(cp(V, ex[:, 0:16, 4:6, :], ex[:, 0:16, 1:2, :].to_broadcast([128, 16, 2, 16]), a2))
            done.append(cp(V, ex[:, 0:16, 7, :], ex[:, 0:16, 6, :], a3))
        if h1 == 20:
            a3 = cp(V, ex[:, 16:20, 3, :], rt[:, 16 - h0:20 - h0, :], m)
            done.append(cp(e2, ex[:, 16:20, 4:7:2, :], ex[:, 16:20, 0:1, :].to_broadcast([128, 4, 2, 16]), a1))
            done.append(cp(e2, ex[:, 16:20, 2:8:5, :], ex[:, 16:20, 1:2, :].to_broadcast([128, 4, 2, 16]), a2))
            done.append(cp(e2, ex[:, 16:20, 5, :], ex[:, 16:20, 3, :], a3))
        fr["rt", p] = [m, a3]
        yield
        ch, tc = divmod(i, 4)
        for g0, g1 in ((0, 8), (8, 16), (16, 20)):
            if g0 < h0 or g1 > h1:
                continue
            k = misc()
            kb = k.ap.bitcast(BF16).rearrange("p (h n) -> p h n", n=128)
            for h in range(g0, g1):
                m = tr(kb[:, h - g0, :], ex[:, h, :, :].rearrange("p s d -> p (s d)"), IDB[:, :], done, m_id, k.free)
            if g0 < 16:
                dst, w = QT[ch % 2][:, g0:g1, 128 * tc:128 * tc + 128], qt_free.get(ch - 2)
            else:
                dst, w = KT[b][:, :, 128 * t:128 * t + 128], None
            m2 = cp(e1 if g0 else V, dst, kb[:, 0:g1 - g0, :], m, w)
            k.free = [m2]
            if g0 < 16:
                qt_ok.setdefault(i, []).append(m2)
            else:
                kt_ok[i] = m2
            yield
        fr["ex", p] = m

    exp_m, pv_m, s_m = {}, {}, {}
    enc_ok = {}

    def geometry(n):
        ch, r = divmod(n, 64)
        g, r = divmod(r, 16)
        return ch, g, r // 2, r % 2

    def scores(n):
        ch, g, kt, hf = geometry(n)
        b = ch // 2
        u = unit[n % 2]
        w = [kt_ok[8 * b + kt]] + [m for i in range(4) for m in qt_ok[4 * ch + i]]
        for j in range(2):
            s_m[n] = mm(u.ap[:, 512 * j:512 * j + 512], KT[b][:, g, 128 * kt:128 * kt + 128],
                        QT[ch % 2][:, 4 * g + 2 * hf + j, :], True, True, w, exp_m.get(n - 2), *([bk.free for bk in bank[0:4]] if n < 2 else []))
        if n % 64 == 63:
            qt_free[ch] = s_m[n]

    def exponent(n):
        exp_m[n] = act(PB[n % NP][:, :], unit[n % 2].ap, ACT.Exp, s_m[n], pv_m.get(n - NP), pb_free, scale=0.25)

    pb_free = []

    def values(n):
        ch, g, kt, _ = geometry(n)
        b = ch // 2
        if kt == 0:
            pv_bank[ch, g] = pvb()
        k = pv_bank[ch, g]
        for j in range(4):
            m = mm(k.ap[32 * j:32 * j + 32, :], VS[b][:, kt, g, :], PB[(n - 1 + j // 2) % NP][:, 512 * (j % 2):512 * (j % 2) + 512],
                   kt == 0, kt == 7, exp_m[n - 1], exp_m[n], vs_ok[8 * b + kt], k.free)
        pv_m[n - 1] = pv_m[n] = m
        if kt == 7:
            normalise(ch, g, m)

    pv_bank, enc_used = {}, []

    def normalise(ch, g, m):
        k, p = pv_bank[ch, g], g % 2
        assert ch == 0 or ch - 1 in enc_used
        m = vtr(ET[p][:, :, :].rearrange("p a b -> p (a b)"), k.ap, m, fr.get(("et", p)))
        k.free = [m]
        m = rcp(ERC[:, :, :], ET[p][:, :, 16:17], m, fr.get("em"))
        m = tt(V, EM[:, :, :], ET[p][:, :, 0:16], ERC[:, :, :].to_broadcast([128, 16, 16]), ALU.mult, m)
        fr["et", p] = m
        h = cp(V, EHR[:, :, :], EM[:, :, :], m, fr.get("ehr"))
        m = tt(V, EHL[:, :, 16:32], EM[:, :, :], f32(EHR[:, :, :]), ALU.subtract, h, fr.get("ehl"))
        h = cp(V, EHL[:, :, 0:16], f32(EHR[:, :, :]), h, fr.get("ehl"))
        fr["em"], fr["ehr"] = m, [m, h]
        m = vtr(ET[p][:, :, :].rearrange("p a b -> p (a b)"), EHL[:, :, :].rearrange("p a b -> p (a b)"), m, h, fr["et", p])
        fr["ehl"] = m
        m = cp(V, ENC[:, g, :], ET[p][:, :, :].rearrange("p a b -> p (a b)"), m, fr.get("enc"))
        fr["et", p] = m
        enc_ok[ch, g] = m

    def drain(gens):
        for g in gens:
            for _ in g:
                pass

    def staggered(gens, lag):
        live, k = [], 0
        gens = list(gens)
        while gens or live:
            if gens and k % lag == 0:
                live.append(gens.pop(0))
            k += 1
            live = [g for g in live if next(g, "end") != "end"]

    startmisc = misc
    misc = Turns(bank[0:8])
    staggered([p1(i, i < 4, S, G) for i in range(8)], 3)
    misc = startmisc
    m_wo = split(WOH[:, :, :], WOL[:, :, :], WOR, d_wo)
    m_gw = split(GWH[:, :, :], GWL[:, :, :], GWR, d_gw)
    pb_free += [m_wq, m_wo, m_gw]

    def chain(gens):
        for g in gens:
            yield from g

    def attention(ch, bg):
        n0 = 64 * ch
        for n in range(n0, n0 + 64):
            exponent(n)
            if n + 2 < 256:
                if (n + 2) % 64 == 0:
                    for _ in bg:
                        pass
                scores(n + 2)
            if n % 2:
                values(n)
            next(bg, None)

    scores(0)
    scores(1)
    nch = 1 if upto == 1 else 4
    attention(0, chain([later(i, V, G) for i in range(4, 8)] + [p1(i, False, V, G) for i in range(12, 16)]))

    IOTA = CST[:, C_IOTA:C_IOTA + E]
    DID = CST[:, C_DID:C_DID + NT * TOPK].rearrange("p (t k) -> p t k", k=TOPK)
    x1_ok, sig_ok, xt_ok = {}, {}, {}
    rows_free = [m_rows]

    def post(ch, e1, xt_free=()):
        w, rows = [enc_ok[ch, g] for g in range(4)], {}
        for tc in range(4):
            i, n, k = 4 * ch + tc, 0, misc()
            for wt in (WOH, WOL):
                for g in range(4):
                    mk = mm(k.ap[:, 0:256], ENC[:, g, 128 * tc:128 * tc + 128], wt[:, g, :], n == 0, n == 7, w, m_wo, k.free)
                    n += 1
                yield
            m = tt(V, X[:, i, :], X[:, i, :], k.ap[:, 0:256], ALU.add, mk)
            k.free = [m]
            st, key = ST[2 + tc % 2], ("st", 2 + tc % 2)
            m = ln(X[:, i, :], st, key, m)
            m = ts2(V, ROWS[:, tc, :, 0:C], X[:, i:i + 1, :].to_broadcast([128, TOPK, C]), st[:, 6:7], st[:, 8:9],
                    ALU.subtract, ALU.mult, m, rows_free)
            fr[key] = rows[tc] = m
        fr["enc"] = mk
        enc_used.append(ch)
        yield
        for tc in range(4):
            k, m = misc(), rows[tc]
            tr(k.ap[:, 0:128], ROWS[:, tc, 0, 0:128], IDF, m, k.free)
            m = tr(k.ap[:, 128:256], ROWS[:, tc, 0, 128:256], IDF)
            kv = k.ap[:, 0:256].rearrange("p (c n) -> p c n", c=2)
            th, tl = XTH[:, ch, :, 128 * tc:128 * tc + 128], XTL[:, ch, :, 128 * tc:128 * tc + 128]
            h = cp(e1, th, kv, m, *xt_free)
            m = tt(V, tl, kv, f32(th), ALU.subtract, h, *xt_free)
            k.free = [m]
            yield
        xt_ok[ch] = m
        k, n = misc(), 0
        for l, r in ((GWH, XTH), (GWL, XTH), (GWH, XTL)):
            for c in range(2):
                mk = mm(k.ap[0:64, :], l[:, c, :], r[:, ch, c, :], n == 0, n == 5, m, m_gw, k.free)
                n += 1
            yield
        m = cp(V, GL[:, :], k.ap[0:64, :], mk, fr.get("gl"))
        k.free = [m]
        yield
        k = misc()
        for t in range(4):
            mk = tr(k.ap[:, 64 * t:64 * t + 64], GL[:, 128 * t:128 * t + 128], CST[0:64, C_ID:C_ID + 64], m, k.free)
        fr["gl"] = mk
        yield
        m = cp(V, LG[:, :, :].rearrange("p t e -> p (t e)"), k.ap[:, 0:256], mk, fr.get("lg"))
        k.free = [m]
        for t in range(4):
            m1 = V(lambda e, t=t: e.max(MX[:, t, :], LG[:, t, 0:E]), m, fr.get("mx"))
        for t in range(4):
            m2 = V(lambda e, t=t: e.max_index(MI[:, t, :], MX[:, t, :], LG[:, t, 0:E]), m1, fr.get("mi"))
        g1 = tt(V, GX[:, :, 0:E], LG[:, :, 0:E], MX[:, :, 0:1].to_broadcast([128, 4, E]), ALU.subtract, m1, fr.get("gx"))
        g2 = tt(V, GX[:, :, E:E + 4], MX[:, :, 0:4], MX[:, :, 0:1].to_broadcast([128, 4, 4]), ALU.subtract, m1, fr.get("gx"))
        g3 = ts(V, GX[:, :, E + 4:E + 5], LG[:, :, E:E + 1], -1.0, ALU.mult, m, fr.get("gx"))
        fr["lg"] = [m2, g1, g3]
        mfv = EXF[:, 4 * ch:4 * ch + 4, :]
        mf = cp(V, mfv, MI[:, :, 0:TOPK], m2)
        fr["mx"], fr["mi"] = [m2, g2], mf
        ex = act(GX[:, :, :], GX[:, :, :], ACT.Exp, g1, g2, g3)
        mo = tt(V, OH[:, :, :, :], IOTA.unsqueeze(1).unsqueeze(1).to_broadcast([128, 4, TOPK, E]),
                mfv.unsqueeze(3).to_broadcast([128, 4, TOPK, E]), ALU.is_equal, mf, fr.get("oh"))
        yield
        mb = count(MB[:, :, :], OH[:, :, :, :].rearrange("p t k e -> p t e k"), mo, fr.get("mb"))
        yield
        k = misc()
        for t in range(4):
            o = k.ap[:, 64 * t:64 * t + E]
            mk = mm(o, TRI[:, :], MB[:, t, :], True, False, mb, m_tri, k.free)
            for s_ in range(t):
                mk = mm(o, ONE[:, :], MB[:, s_, :], False, False, m_one)
            mk = mm(o, ONE[:, :], MAC[:, ch, :], False, True, m_mac[ch], m_one)
        m = red(MS[:, :], MB[:, :, :].rearrange("p t e -> p e t"), mb, fr.get("ms"))
        m_mac.append(tt(V, MAC[:, (ch + 1) % 4, :], MAC[:, ch, :], MS[:, :], ALU.add, m, mk if ch == 3 else None))
        fr["ms"], fr["mb"] = m_mac[-1], [m, mk]
        if ch == 3:
            mc = mm(k.ap[:, 256:256 + E], ONE[:, :], MAC[:, 0, :], True, True, m_mac[-1], m_one)
            m = cp(V, CNF[:, 0:E], k.ap[:, 256:256 + E], mc)
            m = V(lambda e: e.tensor_reduce(CNF[:, E:E + 1], CNF[:, 0:E], AX.X, ALU.max), m)
            cp(V, CNT[:, 0:E + 1], CNF[:, 0:E + 1], m)
        yield
        kr = k.ap[:, 0:256].rearrange("p (t e) -> p t e", t=4)[:, :, 0:E]
        m = tt(V, PR[:, :, :, :], OH[:, :, :, :], kr.unsqueeze(2).to_broadcast([128, 4, TOPK, E]), ALU.mult, mk, fr.get("pr"))
        fr["oh"], k.free = m, [m]
        rk = RKF[:, 4 * ch:4 * ch + 4, :]
        m = red(rk, PR[:, :, :, :], m)
        fr["pr"] = m
        m1 = ts2(V, SLF[:, :, :], rk, float(SLOTS), float(AWAY), ALU.is_ge, ALU.mult, m, fr.get("slf"))
        m1 = tt(V, SLF[:, :, :], SLF[:, :, :], rk, ALU.add, m1)
        m1 = stt(SLF[:, :, :], mfv, float(SLOTS), SLF[:, :, :], ALU.mult, ALU.add, m1)
        sl = SLI[ch % 2]
        ms_ = cp(V, sl[:, :], SLF[:, :, :].rearrange("p t k -> p (t k)"), m1, fr.get(("sli", ch % 2)))
        fr["slf"] = ms_
        m = red(DEN[:, 0, :], GX[:, :, 0:E], ex, fr.get("den"))
        m2 = ts(V, DEN[:, 1, :], GX[:, :, E + 4], 1.0, ALU.add, ex, fr.get("den"))
        m = rcp(DEN[:, :, :], DEN[:, :, :], m, m2)
        m3 = cp(V, SIG[:, 4 * ch:4 * ch + 4], DEN[:, 1, :], m)
        sig_ok[ch] = m3
        wk = WKF[:, 4 * ch:4 * ch + 4, :]
        m1 = tt(V, wk, GX[:, :, E:E + 4], DEN[:, 0, :].unsqueeze(2).to_broadcast([128, 4, TOPK]), ALU.mult, m)
        fr["gx"], fr["den"] = m1, [m1, m3]
        m1 = cp(V, ROWS[:, :, :, C + 1], wk, m1, rows_free)
        m2 = cp(V, ROWS[:, :, :, C], DID[:, 4 * ch:4 * ch + 4, :], d_c, rows_free)
        yield
        for t in range(4):
            for q in range(TOPK):
                o = SLI[ch % 2][:, TOPK * t + q:TOPK * t + q + 1]
                src = ROWS[:, t, q, :]
                ms2 = G.dma(D("sc"), lambda e, o=o, src=src: e.indirect_dma_start(
                    XS[:, :], bass.IndirectOffsetOnAxis(ap=o, axis=0), src, None,
                    bounds_check=E * SLOTS - 1, oob_is_err=False), ms_, m1, m2, d_pf)
            yield
        fr["sli", ch % 2] = ms2
        rows_free[:] = [ms2]
        sc_ok[ch] = ms2

    sc_ok = {}

    if upto >= 2:
        attention(1, chain([post(0, V)] + [p1(i, True, V, G) for i in range(8, 12)]))
        attention(2, chain([post(1, V)] + [later(i, V, G) for i in range(12, 16)]))
        p1_done = [q.last() for q in (PE, V, S, G)]
        attention(3, chain([post(2, V, p1_done)]))

    ov = out.rearrange("(n p) c -> p n c", p=128)
    fence = lambda: [q.last() for q in (PE, V, S, G)] + [(c, c.n) for c in dctr.values()]
    if upto >= 2:
        drain([post(3, S, p1_done)])
    if upto == 2:
        Y.dma(D("out"), lambda e: e.dma_start(ov, X[:, :, :]), fence())

    if upto >= 3:
        att_done = fence()
        W1 = Region(nc, a0, a1)
        S1H, S1L = W1("S1H", [128, 2, 2 * ISH], F32R), W1("S1L", [128, 2, 2 * ISH], F32R)
        S2H, S2L = W1("S2H", [128, 6, C], F32R), W1("S2L", [128, 6, C], F32R)
        SRW = W1("SRW", [128, 2 * 2 * ISH], F32)
        W2 = Region(nc, a1, top)
        SSG = [W2(f"SSG{i}", [128, 256], F32) for i in range(2)]
        SHF = [W2(f"SHF{i}", [128, 256], F32) for i in range(2)]
        SHH = [W2(f"SHH{i}", [128, 256], F32R) for i in range(2)]
        SHL = [W2(f"SHL{i}", [128, 256], F32R) for i in range(2)]
        STT = W2("STT", [128, 256], F32R)
        r1 = SRW[:, :].rearrange("p (c n) -> p c n", c=2)
        m = Y.dma(D("s1"), lambda e: e.dma_start(r1, wsh1.rearrange("(c p) n -> p c n", p=128)), att_done)
        m_s1 = split(S1H[:, :, :], S1L[:, :, :], r1, [m] + att_done)
        r2 = SRW[:, 0:6 * C].rearrange("p (f n) -> p f n", f=6)
        m = Y.dma(D("s1"), lambda e: e.dma_start(r2, wsh2.rearrange("(f p) n -> p f n", p=128)), m_s1)
        m_s2 = split(S2H[:, :, :], S2L[:, :, :], r2, m)
        shb = Turns(bank[0:4])
        sha = bank[4:6]
        shared_free = {}

        def shared(uu):
            ch, hf = divmod(uu, 2)
            w = [xt_ok[ch], m_s1]
            pend = None

            def down(f, h, l):
                wd = [m_s2]
                for t in range(2):
                    o, cs = sha[t].ap[:, 0:C], slice(128 * t, 128 * t + 128)
                    if f < 5:
                        mm(o, SHH[f % 2][:, cs], S2H[:, f, :], f == 0, False, h, wd, sha[t].free)
                        mm(o, SHH[f % 2][:, cs], S2L[:, f, :], False, False)
                        m = mm(o, SHL[f % 2][:, cs], S2H[:, f, :], False, False, l)
                    else:
                        mm(o, STT[:, cs], S2H[:, f, :], False, False, h, l)
                        m = mm(o, STT[:, cs], S2L[:, f, :], False, True)
                return m

            for f in range(6):
                k, p = shb(), f % 2
                for part in range(2 if f < 5 else 1):
                    n, c0 = 0, 256 * f + 128 * part
                    for l, r in ((S1H, XTH), (S1L, XTH), (S1H, XTL)):
                        for c in range(2):
                            mk = mm(k.ap[:, 256 * part:256 * part + 256], l[:, c, c0:c0 + 128],
                                    r[:, ch, c, 256 * hf:256 * hf + 256], n == 0, n == 5, w, k.free)
                            n += 1
                    yield
                if f < 5:
                    s_ = act(SSG[p][:, :], k.ap[:, 0:256], ACT.Silu, mk, shared_free.get(("sg", p)), att_done)
                    m = tt(V, SHF[p][:, :], SSG[p][:, :], k.ap[:, 256:512], ALU.mult, s_, shared_free.get(("hf", p)), att_done)
                    k.free, shared_free["sg", p] = [m], m
                    h = cp(S, SHH[p][:, :], SHF[p][:, :], m, shared_free.get(("hh", p)), att_done)
                    l = tt(V, SHL[p][:, :], SHF[p][:, :], f32(SHH[p][:, :]), ALU.subtract, h, shared_free.get(("hh", p)), att_done)
                else:
                    s_ = act(SSG[p][0:64, :], k.ap[0:64, 0:256], ACT.Silu, mk, shared_free.get(("sg", p)))
                    m = tt(V, SHF[p][0:64, :], SSG[p][0:64, :], k.ap[64:128, 0:256], ALU.mult, s_, shared_free.get(("hf", p)))
                    k.free, shared_free["sg", p] = [m], m
                    h = cp(S, STT[0:64, :], SHF[p][0:64, :], m, shared_free.get("tt"), att_done)
                    l = tt(V, STT[64:128, :], SHF[p][0:64, :], f32(STT[0:64, :]), ALU.subtract, h, shared_free.get("tt"), att_done)
                shared_free["hf", p] = l
                if pend:
                    m = down(*pend)
                    shared_free["hh", pend[0] % 2] = m
                    yield
                pend = (f, h, l)
            m = down(*pend)
            shared_free["tt"] = m
            for t in range(2):
                i = 4 * ch + 2 * hf + t
                x1_ok[i] = stt(X[:, i, :], sha[t].ap[:, 0:C], SIG[:, i:i + 1], X[:, i, :], ALU.mult, ALU.add, m, sig_ok[ch])
                sha[t].free = [x1_ok[i]]
            yield

        drain([shared(uu) for uu in range(8)])
        if upto == 3:
            Y.dma(D("out"), lambda e: e.dma_start(ov, X[:, :, :]), fence())

    if upto >= 4:
        post_done = fence()
        W3 = Region(nc, W2.at, top)
        WR = [W3(f"WR{i}", [128, WPK], F32) for i in range(3)]
        W13H = [W3(f"W13H{i}", [128, 2, 2 * I], F32R) for i in range(2)]
        W13L = [W3(f"W13L{i}", [128, 2, 2 * I], F32R) for i in range(2)]
        W2H = [W3(f"W2H{i}", [128, 2, C], F32R) for i in range(2)]
        W2L = [W3(f"W2L{i}", [128, 2, C], F32R) for i in range(2)]
        XB = [W3(f"XB{i}", [128, 2, ROW], F32) for i in range(3)]
        XBH = [W3(f"XBH{i}", [128, 2, 2, 128], F32R) for i in range(2)]
        XBL = [W3(f"XBL{i}", [128, 2, 2, 128], F32R) for i in range(2)]
        SGE = W3("SGE", [128, 2, I], F32)
        HE = [W3(f"HE{i}", [128, 2, I], F32) for i in range(2)]
        HMH = [W3(f"HMH{i}", [128, 2, 128], F32R) for i in range(2)]
        HML = [W3(f"HML{i}", [128, 2, 128], F32R) for i in range(2)]
        HTT = [W3(f"HTT{i}", [128, 2, 128], F32R) for i in range(2)]
        YB = [W3(f"YB{i}", [128, 2, C], F32) for i in range(2)]
        YI = [W3(f"YI{i}", [128, 2], I32) for i in range(3)]
        gu, xtb, htb, yb_ = Bank(PS[0]), bank[2], bank[3], bank[6]
        for k in (gu, xtb, htb, yb_):
            k.free = post_done
        ef = {}
        free = lambda *key: ef.get(key, post_done)
        m_tt = [ms(V, f32(HTT[i][32:64, :, :]), 0.0, post_done) for i in range(2)]
        wl, xl, mk_ = {}, {}, {}

        def load(e):
            wl[e] = Y.dma(D(f"w{e % 3}"), lambda q: q.dma_start(WR[e % 3][:, :], wpk[e]), free("wr", e % 3))
            xl[e] = Y.dma(D(f"xe{e % 3}"), lambda q: q.dma_start(
                XB[e % 3][:, :, :], XS[SLOTS * e:SLOTS * e + SLOTS, :].rearrange("(j p) w -> p j w", p=128)),
                list(sc_ok.values()), free("xb", e % 3))

        def split13(e):
            p, r = e % 2, WR[e % 3][:, 0:4 * I].rearrange("p (c n) -> p c n", c=2)
            h = cp(S, W13H[p][:, :, :], r, wl[e], free("w13", p))
            mk_["w13", e] = tt(V, W13L[p][:, :, :], r, f32(W13H[p][:, :, :]), ALU.subtract, h, free("w13", p))

        def split2(e):
            p, r = e % 2, WR[e % 3][:, 4 * I:].rearrange("p (c n) -> p c n", c=2)
            h = cp(S, W2H[p][:, :, :], r, wl[e], free("w2", p))
            mk_["w2", e] = tt(G, W2L[p][:, :, :], r, f32(W2H[p][:, :, :]), ALU.subtract, h, free("w2", p))
            ef["wr", e % 3] = [mk_["w13", e], mk_["w2", e]]

        def xt_pe(e):
            for j in range(2):
                for c in range(2):
                    q = 256 * j + 128 * c
                    mk_["xt", e] = tr(xtb.ap[:, q:q + 128], XB[e % 3][:, j, 128 * c:128 * c + 128], IDF, xl[e], xtb.free)

        def xt_split(e):
            p, v = e % 2, xtb.ap.rearrange("p (j c n) -> p j c n", j=2, c=2)
            h = cp(S, XBH[p][:, :, :, :], v, mk_["xt", e], free("xbh", p))
            m = tt(V, XBL[p][:, :, :, :], v, f32(XBH[p][:, :, :, :]), ALU.subtract, h, free("xbh", p))
            xtb.free = [m]
            mk_["xbl", e] = m
            mk_["yi", e] = cp(V, YI[e % 3][:, :], XB[e % 3][:, :, C], xl[e], free("yi", e % 3))

        def up(e, j):
            p, n = e % 2, 0
            for l, r in ((XBH, W13H), (XBH, W13L), (XBL, W13H)):
                for c in range(2):
                    m = mm(gu.ap[:, 512 * j:512 * j + 2 * I], l[p][:, j, c, :], r[p][:, c, :], n == 0, n == 5,
                           mk_["xbl", e], mk_["w13", e], gu.free)
                    n += 1
            mk_["up", e] = m
            ef["w13", p] = ef["xbh", p] = [m]

        def gated(e):
            p, v = e % 2, gu.ap.rearrange("p (j n) -> p j n", j=2)
            s_ = act(SGE[:, :, :], v[:, :, 0:I], ACT.Silu, mk_["up", e], free("sge"))
            m = tt(V, HE[p][:, :, :], SGE[:, :, :], v[:, :, I:2 * I], ALU.mult, s_, free("he", p))
            ef["sge",] = gu.free = [m]
            mk_["he", e] = m

        def ht_pe(e):
            p = e % 2
            for j in range(2):
                tr(htb.ap[:, 128 * j:128 * j + 128], HE[p][:, j, 0:128], IDF, mk_["he", e], htb.free)
                m = tr(htb.ap[0:48, 256 + 128 * j:384 + 128 * j], HE[p][:, j, 128:I], IDF)
            mk_["ht", e] = m
            ef["he", p] = [m]

        def ht_split(e):
            p = e % 2
            v, vt = htb.ap[:, 0:256].rearrange("p (j n) -> p j n", j=2), htb.ap[0:48, 256:512].rearrange("p (j n) -> p j n", j=2)
            h1 = cp(S, HMH[p][:, :, :], v, mk_["ht", e], free("hm", p))
            h2 = cp(S, HTT[p][0:48, :, :], vt, mk_["ht", e], free("hm", p), m_tt[p])
            m1 = tt(V, HML[p][:, :, :], v, f32(HMH[p][:, :, :]), ALU.subtract, h1, h2, free("hm", p))
            m2 = tt(V, HTT[p][64:112, :, :], vt, f32(HTT[p][0:48, :, :]), ALU.subtract, h2, free("hm", p))
            htb.free = [m1, m2]
            mk_["hl", e] = [m1, m2]

        def down(e):
            p = e % 2
            for j in range(2):
                o = yb_.ap[:, C * j:C * j + C]
                mm(o, HMH[p][:, j, :], W2H[p][:, 0, :], True, False, mk_["hl", e], mk_["w2", e], yb_.free)
                mm(o, HMH[p][:, j, :], W2L[p][:, 0, :], False, False)
                mm(o, HML[p][:, j, :], W2H[p][:, 0, :], False, False)
                mm(o, HTT[p][0:112, j, :], W2H[p][0:112, 1, :], False, False)
                m = mm(o, HTT[p][0:112, j, :], W2L[p][0:112, 1, :], False, True)
            mk_["y", e] = m
            ef["hm", p] = ef["w2", p] = [m]

        def give(e):
            p, b = e % 2, e % 3
            m1 = scaled(S, YB[p][:, 0, :], yb_.ap[:, 0:C], XB[b][:, 0, C + 1:C + 2], mk_["y", e], free("yb", p))
            m2 = scaled(V, YB[p][:, 1, :], yb_.ap[:, C:2 * C], XB[b][:, 1, C + 1:C + 2], m1, free("yb", p))
            yb_.free = [m2]
            for j in range(2):
                m = G.dma(D(f"so{p}"), lambda q, j=j: q.indirect_dma_start(
                    YS[:, :], bass.IndirectOffsetOnAxis(ap=YI[b][:, j:j + 1], axis=0), YB[p][:, j, :], None,
                    bounds_check=NPAIR - 1, oob_is_err=False), m1, m2, mk_["yi", e], d_pf)
            ef["yb", p] = ef["yi", b] = ef["xb", b] = [m]

        for e in range(3):
            load(e)
        split13(0)
        xt_pe(0)
        xt_split(0)
        for e in range(E + 1):
            if e:
                ht_pe(e - 1)
                ht_split(e - 1)
            if e < E:
                up(e, 0)
                if e + 1 < E:
                    xt_pe(e + 1)
                    xt_split(e + 1)
                up(e, 1)
                split2(e)
                gated(e)
            if e:
                down(e - 1)
                give(e - 1)
                if e + 2 < E:
                    load(e + 2)
            if e + 1 < E:
                split13(e + 1)

    if upto >= 5:
        moe_done = fence()
        W4 = Region(nc, W2.at, top)
        FB = [Bank(W4(f"FB{i}", [128, TOPK, C], F32)) for i in range(8)]
        FO = [Bank(W4(f"FO{i}", [128, C], F32)) for i in range(4)]
        yv = YS.rearrange("(n p k) c -> n p k c", p=128, k=TOPK)
        ok = {}

        def fetch(i):
            k = FB[i % 8]
            ok[i] = Y.dma(D(f"fb{i % 8}"), lambda q: q.dma_start(k.ap[:, :, :], yv[i]), moe_done if i < 8 else k.free)

        for i in range(8):
            fetch(i)
        for i in range(NT):
            k, o = FB[i % 8], FO[i % 4]
            m = red(o.ap[:, :], k.ap[:, :, :].rearrange("p k c -> p c k"), ok[i], moe_done, o.free)
            k.free = [m]
            m = tt(V, o.ap[:, :], o.ap[:, :], X[:, i, :], ALU.add, m, x1_ok[i])
            o.free = [S.dma(D(f"fo{i % 4}"), lambda q, i=i, o=o: q.dma_start(ov[:, i, :], o.ap[:, :]), m)]
            if i + 8 < NT:
                fetch(i + 8)

    for c in dctr.values():
        Y.wait((c, c.n))

    with nc.Block() as block:

        @block.sync
        def _(e):
            Y.run(e)

        @block.tensor
        def _(e):
            PE.run(e)

        @block.vector
        def _(e):
            V.run(e)

        @block.scalar
        def _(e):
            S.run(e)

        @block.gpsimd
        def _(e):
            G.run(e)

    if upto >= 5:
        overflow(nc, wpk, YS, ov, X, XTH, XTL, CST, CNT, RKF, EXF, WKF, a0, top, PS)
    ctx.close()


def overflow(nc, wpk, YS, ov, X, XTH, XTL, CST, CNT, RKF, EXF, WKF, a0, top, PS):
    ctx = ExitStack()
    sems = [ctx.enter_context(nc.semaphore(f"o{i}")) for i in range(7)]
    every = range(sems[0].num, sems[0].num + 7)
    s_w, s_g, s_v, s_t, s_c, s_q, s_p = sems
    assert [q.num for q in sems] == list(every)
    TOK = nc.dram_tensor("tok_scratch", [B * T, C], F32, kind="Internal").ap()
    WTS = nc.dram_tensor("wts_scratch", [NPAIR, 1], F32, kind="Internal").ap()
    IDS = nc.dram_tensor("ids_scratch", [E * CAP, 1], I32, kind="Internal").ap()
    M = Region(nc, a0, top)
    NONE = M("NONE", [128, E * CAP // 128], I32)
    OSF, OSL = M("OSF", [128, NT, TOPK], F32), M("OSL", [128, NT * TOPK], I32)
    ODI = M("ODI", [128, NT * TOPK], I32)
    OTH, OTL = M("OTH", [128, C], F32), M("OTL", [128, C], F32)
    OID, OTK = M("OID", [128, 1], I32), M("OTK", [128, 1], I32)
    OWT = M("OWT", [128, 1], F32)
    OW = M("OW", [128, WPK], F32)
    OX = M("OX", [128, C], F32)
    OXT = M("OXT", [128, C], F32)
    OSG, OH_ = M("OSG", [128, I], F32), M("OH_", [128, I], F32)
    OHT = M("OHT", [128, 2, 128], F32)
    OY = M("OY", [128, C], F32)
    OF, OO = M("OF", [128, TOPK, C], F32), M("OO", [128, C], F32)
    IDF = CST[:, C_ID:C_ID + 128]
    p0, p1, p2, p3 = (PS[i][:, 0:512] for i in range(4))

    most = nc.values_load(CNT[0:1, E:E + 1], min_val=0, max_val=CAP)
    everyone = (nc.sync, nc.tensor, nc.vector, nc.scalar, nc.gpsimd)
    with nc.If(most > SLOTS):
        for e in everyone:
            e.nop()
        with nc.Block() as block:

            @block.vector
            def _(v):
                v.memset(NONE[:, :], NPAIR).then_inc(s_v, 1)
                v.scalar_tensor_tensor(OSF[:, :, :], EXF[:, :, :], float(CAP), RKF[:, :, :], ALU.mult, ALU.add).then_inc(s_v, 1)
                v.wait_ge(s_v, 2)
                v.tensor_copy(OSL[:, :], OSF[:, :, :].rearrange("p t k -> p (t k)")).then_inc(s_v, 1)
                v.tensor_copy(ODI[:, :], CST[:, C_DID:C_DID + NT * TOPK]).then_inc(s_v, 1)
                for i in range(NT):
                    v.wait_ge(s_t, 2 * i + 1)
                    if i:
                        v.wait_ge(s_w, 16 * i)
                    v.tensor_copy(OTH[:, :], p0[:, 0:C]).then_inc(s_v, 1)
                    v.wait_ge(s_t, 2 * i + 2)
                    v.wait_ge(s_v, 2 * i + 5)
                    v.tensor_tensor(OTH[:, :], OTH[:, :], p1[:, 0:C], ALU.add).then_inc(s_v, 1)

            @block.tensor
            def _(t):
                for i in range(NT):
                    if i:
                        t.wait_ge(s_v, 4 + 2 * i)
                    for o, src in ((p0, XTH), (p1, XTL)):
                        for c in range(2):
                            q = t.transpose(o[:, 128 * c:128 * c + 128],
                                            src[:, i // 4, c, 128 * (i % 4):128 * (i % 4) + 128].bitcast(F32), IDF)
                        q.then_inc(s_t, 1)

            @block.sync
            def _(y):
                for i in range(NT):
                    y.wait_ge(s_v, 6 + 2 * i)
                    y.dma_start(TOK[128 * i:128 * i + 128, :], OTH[:, :]).then_inc(s_w, 16)
                y.wait_ge(s_w, 16 * NT)

            @block.gpsimd
            def _(g):
                g.dma_start(WTS.rearrange("(t p k) w -> p t (k w)", p=128, k=TOPK), WKF[:, :, :]).then_inc(s_q, 16)
                g.wait_ge(s_v, 4)
                g.dma_start(IDS.rearrange("(p n) w -> p (n w)", p=128), NONE[:, :]).then_inc(s_q, 16)
                g.wait_ge(s_q, 32)
                for i in range(NT * TOPK):
                    g.indirect_dma_start(IDS[:, :], bass.IndirectOffsetOnAxis(ap=OSL[:, i:i + 1], axis=0), ODI[:, i:i + 1], None,
                                         bounds_check=E * CAP - 1, oob_is_err=False).then_inc(s_q, 16)
                g.wait_ge(s_q, 16 * (2 + NT * TOPK))
                g.dma_reset(every)

        nc.all_engine_barrier(sems_to_clear=every)
        with nc.Fori(0, E) as ex:
            have = nc.values_load(CNT[0:1, bass.ds(ex, 1)], min_val=0, max_val=CAP)
            with nc.Fori(0, NMORE) as j:
                with nc.If(have > j * 128 + SLOTS):
                    for e in everyone:
                        e.nop()
                    with nc.Block() as block:

                        @block.sync
                        def _(y):
                            y.dma_start(OID[:, :], IDS[bass.ds(ex * CAP + j * 128 + SLOTS, 128), :]).then_inc(s_p, 16)
                            y.dma_start(OW[:, :], wpk[bass.ds(ex, 1), :, :].rearrange("a p n -> (a p) n")).then_inc(s_w, 16)
                            y.wait_ge(s_w, 16)

                        @block.gpsimd
                        def _(g):
                            g.wait_ge(s_v, 3)
                            g.indirect_dma_start(OX[:, :], None, TOK[:, :], bass.IndirectOffsetOnAxis(ap=OTK[:, :], axis=0),
                                                 bounds_check=B * T - 1, oob_is_err=False).then_inc(s_g, 16)
                            g.indirect_dma_start(OWT[:, :], None, WTS[:, :], bass.IndirectOffsetOnAxis(ap=OID[:, :], axis=0),
                                                 bounds_check=NPAIR - 1, oob_is_err=False).then_inc(s_g, 16)
                            g.wait_ge(s_v, 8)
                            g.indirect_dma_start(YS[:, :], bass.IndirectOffsetOnAxis(ap=OID[:, :], axis=0), OY[:, :], None,
                                                 bounds_check=NPAIR - 1, oob_is_err=False).then_inc(s_q, 16)
                            g.wait_ge(s_q, 16)
                            g.dma_reset(every)

                        @block.vector
                        def _(v):
                            v.memset(OX[:, :], 0.0).then_inc(s_v, 1)
                            v.memset(OWT[:, :], 0.0).then_inc(s_v, 1)
                            v.wait_ge(s_p, 16)
                            v.tensor_scalar(OTK[:, :], OID[:, :], 2, None, ALU.logical_shift_right).then_inc(s_v, 1)
                            v.wait_ge(s_t, 1)
                            v.tensor_copy(OXT[:, :], p0[:, 0:C]).then_inc(s_v, 1)
                            v.wait_ge(s_c, 1)
                            v.tensor_tensor(OH_[:, :], OSG[:, :], p1[:, I:2 * I], ALU.mult).then_inc(s_v, 1)
                            v.wait_ge(s_t, 3)
                            v.tensor_copy(OHT[:, 0, :], p2[:, 0:128]).then_inc(s_v, 1)
                            v.tensor_copy(OHT[0:48, 1, :], p2[0:48, 128:256]).then_inc(s_v, 1)
                            v.wait_ge(s_t, 4)
                            v.tensor_scalar(OY[:, :], p3[:, 0:C], OWT[:, 0:1], None, ALU.mult).then_inc(s_v, 1)

                        @block.scalar
                        def _(a):
                            a.wait_ge(s_t, 2)
                            a.activation(OSG[:, :], p1[:, 0:I], ACT.Silu).then_inc(s_c, 1)

                        @block.tensor
                        def _(t):
                            t.wait_ge(s_g, 32)
                            t.transpose(p0[:, 0:128], OX[:, 0:128], IDF)
                            t.transpose(p0[:, 128:256], OX[:, 128:256], IDF).then_inc(s_t, 1)
                            t.wait_ge(s_w, 16)
                            t.wait_ge(s_v, 4)
                            t.matmul(p1[:, 0:2 * I], OXT[:, 0:128], OW[:, 0:2 * I], start=True, stop=False)
                            t.matmul(p1[:, 0:2 * I], OXT[:, 128:256], OW[:, 2 * I:4 * I], start=False, stop=True).then_inc(s_t, 1)
                            t.wait_ge(s_v, 5)
                            t.transpose(p2[:, 0:128], OH_[:, 0:128], IDF)
                            t.transpose(p2[0:48, 128:256], OH_[:, 128:I], IDF).then_inc(s_t, 1)
                            t.wait_ge(s_v, 7)
                            t.matmul(p3[:, 0:C], OHT[:, 0, :], OW[:, 4 * I:4 * I + C], start=True, stop=False)
                            t.matmul(p3[:, 0:C], OHT[0:48, 1, :], OW[0:48, 4 * I + C:], start=False, stop=True).then_inc(s_t, 1)

                    nc.all_engine_barrier(sems_to_clear=every)

        with nc.Block() as block:
            yv = YS.rearrange("(n p k) c -> n p k c", p=128, k=TOPK)

            @block.sync
            def _(y):
                for i in range(NT):
                    if i:
                        y.wait_ge(s_v, 2 * i - 1)
                    y.dma_start(OF[:, :, :], yv[i]).then_inc(s_w, 16)
                    y.wait_ge(s_v, 2 * i + 2)
                    y.dma_start(ov[:, i, :], OO[:, :]).then_inc(s_p, 16)
                    y.wait_ge(s_p, 16 * i + 16)

            @block.vector
            def _(v):
                for i in range(NT):
                    v.wait_ge(s_w, 16 * i + 16)
                    if i:
                        v.wait_ge(s_p, 16 * i)
                    v.tensor_reduce(OO[:, :], OF[:, :, :].rearrange("p k c -> p c k"), AX.X, ALU.add).then_inc(s_v, 1)
                    v.wait_ge(s_v, 2 * i + 1)
                    v.tensor_tensor(OO[:, :], OO[:, :], X[:, i, :], ALU.add).then_inc(s_v, 1)
    ctx.close()


def layout(x, wq, wk, wv, wo, gate, sgate, w13, w2, sgu, sdn):
    wqkv = np.concatenate([wq, wk, wv], 1)
    wo5 = wo.reshape(NKV, 4, 1, HD, C)
    wos = np.concatenate([wo5, wo5], 2).reshape(NKV * 128, C)
    gw = np.concatenate([gate, sgate, np.zeros((3, C), gate.dtype)], 0).T
    g, u = sgu[:ISH], sgu[ISH:]
    order = [w[f:min(f + 128, ISH)] for f in range(0, ISH, 128) for w in (g, u)]
    wsh1 = np.concatenate(order, 0).T
    sdt = sdn.T
    wsh2 = np.concatenate([sdt, sdt[640:]], 0)
    a = w13.transpose(0, 2, 1).reshape(E, 2, 128, 2 * I).transpose(0, 2, 1, 3).reshape(E, 128, 4 * I)
    w2t = w2.transpose(0, 2, 1)
    z = np.zeros((E, 16, C), w2.dtype)
    tail = np.concatenate([w2t[:, 128:], z, w2t[:, 128:], z], 1)
    wpk = np.concatenate([a, w2t[:, :128], tail], 2)
    flat = dict(x=x.reshape(B * T, C), wqkv=wqkv, wos=wos, gw=gw, wsh1=wsh1, wsh2=wsh2, wpk=wpk, cst=constants())
    return {k: np.ascontiguousarray(v) for k, v in flat.items()}


def kernel(L0_attn_x, L0_attn_q_kernel, L0_attn_k_kernel, L0_attn_v_kernel, L0_attn_out_kernel, L0_ffn_gate_w,
           L0_ffn_shared_gate_w, L0_ffn_w13, L0_ffn_w2, L0_ffn_se_gate_up_w, L0_ffn_se_down_w):
    import concourse.bacc as _bacc
    from concourse.bass_utils import run_bass_kernel_spmd as _run

    given = [np.asarray(a) for a in (
        L0_attn_x, L0_attn_q_kernel, L0_attn_k_kernel, L0_attn_v_kernel, L0_attn_out_kernel, L0_ffn_gate_w,
        L0_ffn_shared_gate_w, L0_ffn_w13, L0_ffn_w2, L0_ffn_se_gate_up_w, L0_ffn_se_down_w)]
    nc = _bacc.Bacc("TRN2", target_bir_lowering=False, num_devices=1)
    arrays, args = {}, []
    for name, a in layout(*given).items():
        arrays[f"in_{name}"] = a
        args.append(nc.dram_tensor(f"in_{name}", a.shape, mybir.dt.from_np(a.dtype), kind="ExternalInput").ap())
    args.append(nc.dram_tensor("out_0_dram", (B * T, C), F32, kind="ExternalOutput").ap())
    moe_block_kernel(nc, *args)
    r = _run(nc, [arrays], core_ids=[0])
    return r.results[0]["out_0_dram"].reshape(B, T, C)
```

```python
from contextlib import ExitStack

import numpy as np

import concourse.bass as bass
from concourse import mybir

ACT = mybir.ActivationFunctionType
ALU = mybir.AluOpType
AX = mybir.AxisListType
F32 = mybir.dt.float32
F32R = mybir.dt.float32r
BF16 = mybir.dt.bfloat16
I32 = mybir.dt.int32
U32 = mybir.dt.uint32

B, T, C = 2, 1024, 256
NH, NKV, HD = 16, 4, 16
NT = B * T // 128
E, I, TOPK = 60, 176, 4
ISH = 704
CAP = B * T
SLOTS = 256
FULL, PART = 4, 44
AWAY = 1 << 20
ROW = 260
NPAIR = B * T * TOPK
WPK = 2 * 2 * I + 2 * C
TAIL = I - 128

NMORE = CAP // 128 - 1
C_ID, C_TRI, C_COS, C_SIN, C_IOTA, C_DID, C_MH, C_ROW, C_ONE = np.cumsum([0, 128, 128, 128, 128, 60, 64, 4, 1]).tolist()
NCST = C_ONE + 1


def constants():
    c = np.zeros((128, NCST), np.float32)
    p = np.arange(128)
    c[:, C_ID:C_ID + 128] = np.eye(128)
    c[:, C_TRI:C_TRI + 128] = p[:, None] < p[None, :]
    frac = np.arange(0, HD, 2, dtype=np.float32) / np.float32(HD)
    inv = np.float32(1.0) / np.power(np.float32(10000.0), frac, dtype=np.float32)
    ang = np.arange(T, dtype=np.float32)[:, None] * inv[None, :]
    cos, sin = np.cos(ang.astype(np.float64)), np.sin(ang.astype(np.float64))
    cos = np.concatenate([cos, cos], 1).reshape(T // 128, 128, HD)
    sin = np.concatenate([-sin, sin], 1).reshape(T // 128, 128, HD)
    c[:, C_COS:C_COS + 128] = cos.transpose(1, 0, 2).reshape(128, -1)
    c[:, C_SIN:C_SIN + 128] = sin.transpose(1, 0, 2).reshape(128, -1)
    c[:, C_IOTA:C_IOTA + E] = np.arange(E)
    tok = np.arange(NT)[None, :, None] * 128 + p[:, None, None]
    c[:, C_DID:C_DID + NT * TOPK] = (tok * TOPK + np.arange(TOPK)).reshape(128, -1)
    c[:, C_MH:C_MH + 4] = -0.5
    c[:, C_ROW] = p
    c[:, C_ONE] = 1.0
    return c


class Ctr:

    def __init__(self, sem):
        self.sem, self.n = sem, 0


class Eng:

    def __init__(self, sem):
        self.ctr, self.prog, self.met = Ctr(sem), [], {}

    def wait(self, *marks):
        for m in marks:
            if m is None:
                continue
            if isinstance(m, list):
                self.wait(*m)
                continue
            c, v = m
            if self.met.get(id(c), 0) < v:
                self.met[id(c)] = v
                self.prog.append(lambda e, c=c, v=v: e.wait_ge(c.sem, v))

    def __call__(self, fn, *marks):
        self.wait(*marks)
        c = self.ctr
        c.n += 1
        self.prog.append(lambda e: fn(e).then_inc(c.sem, 1))
        return (c, c.n)

    def dma(self, c, fn, *marks):
        self.wait(*marks)
        c.n += 16
        self.prog.append(lambda e: fn(e).then_inc(c.sem, 16))
        return (c, c.n)

    def last(self):
        return (self.ctr, self.ctr.n) if self.ctr.n else None

    def run(self, eng):
        for f in self.prog:
            f(eng)


class Bank:

    def __init__(self, ap):
        self.ap, self.free = ap, []


class Turns:

    def __init__(self, items):
        self.items, self.i = items, -1

    def __call__(self):
        self.i += 1
        return self.items[self.i % len(self.items)]


class Region:

    def __init__(self, nc, base, end):
        self.nc, self.at, self.end = nc, base, end

    def __call__(self, name, shape, dt):
        n = int(np.prod(shape[1:])) * (2 if dt == BF16 else 4)
        t = self.nc.alloc_sbuf_tensor_at(name, shape, dt, offset=self.at)
        self.at += -(-n // 32) * 32
        assert self.at <= self.end, (name, self.at, self.end)
        return t


def moe_block_kernel(nc, x, wqkv, wos, gw, wsh1, wsh2, wpk, cst, out, upto=99):
    ctx = ExitStack()
    sem = lambda name: ctx.enter_context(nc.semaphore(name))
    PE, V, S, G, Y = (Eng(sem(n)) for n in ("s_pe", "s_dve", "s_act", "s_pool", "s_sp"))
    dctr = {}

    def D(name):
        if name not in dctr:
            dctr[name] = Ctr(sem("d_" + name))
        return dctr[name]

    base, top = -(-nc.sbuf_base // 64) * 64, nc.sbuf_top
    P_ = Region(nc, base, top)
    X = P_("X", [128, NT, C], F32)
    xt0 = P_.at
    XTH = P_("XTH", [128, 4, 2, 512], F32R)
    XTL = P_("XTL", [128, 4, 2, 512], F32R)
    R0 = [Region(nc, xt0 + 8192, xt0 + 16384), Region(nc, xt0 + 24576, xt0 + 32768)]
    CST = P_("CST", [128, NCST], F32)
    IDB = P_("IDB", [128, 128], BF16)
    TRI = P_("TRI", [128, 128], BF16)
    ONE = P_("ONE", [128, 128], BF16)
    MAC = P_("MAC", [128, 4, E], BF16)
    r0 = P_.at
    ROWS = P_("ROWS", [128, 4, TOPK, ROW], F32)
    PF = P_("PF", [128, 2, ROW], F32)
    r1_ = P_.at
    SIG = P_("SIG", [128, NT], F32)
    CNT = P_("CNT", [128, 64], I32)
    CNF = P_("CNF", [128, 64], F32)
    ORD = P_("ORD", [1, 64], I32)
    KEY = P_("KEY", [128, 64], F32)
    KEG = P_("KEG", [128, 64], F32)
    KES = P_("KES", [128, 4], F32)
    RKF = P_("RKF", [128, NT, TOPK], F32)
    EXF = P_("EXF", [128, NT, TOPK], F32)
    WKF = P_("WKF", [128, NT, TOPK], F32)
    ST = [P_(f"ST{i}", [128, 10], F32) for i in range(4)]
    SQ = [P_(f"SQ{i}", [128, 24], F32) for i in range(2)]
    a0 = P_.at
    R1 = Region(nc, a0, top)
    QT, KT, VS = [None, None], [None, None], [None, None]
    QT[0] = R1("QT0", [128, NH, 512], BF16)
    KT[0] = R1("KT0", [128, NKV, T], BF16)
    VS[0] = R1("VS0", [128, 8, NKV, 32], F32)
    WQH = R1("WQH", [128, 2, 384], F32R)
    WQL = R1("WQL", [128, 2, 384], F32R)
    XN = [R1(f"XN{i}", [128, C], F32) for i in range(2)]
    XNH = [R1(f"XNH{i}", [128, C], F32R) for i in range(2)]
    XNL = [R1(f"XNL{i}", [128, C], F32R) for i in range(2)]
    QS = [R1(f"QS{i}", [128, 320], F32) for i in range(2)]
    QD = R1("QD", [128, 4, 256], F32)
    RT = [R0[i](f"RT{i}", [128, 20, 16], F32) for i in range(2)]
    RU = [R0[i](f"RU{i}", [128, 20, 16], F32) for i in range(2)]
    EX = [R0[i](f"EX{i}", [128, 20, 8, 16], BF16) for i in range(2)]
    a1 = R1.at
    R2 = Region(nc, a1, top)
    QT[1] = R2("QT1", [128, NH, 512], BF16)
    KT[1] = R2("KT1", [128, NKV, T], BF16)
    VS[1] = R2("VS1", [128, 8, NKV, 32], F32)
    NP = 6
    PB = [R2(f"PB{i}", [128, 1024], F32) for i in range(NP)]
    ET = [R2(f"ET{i}", [128, 16, 32], F32) for i in range(2)]
    EM = R2("EM", [128, 16, 16], F32)
    ERC = R2("ERC", [128, 16, 1], F32)
    EHR = R2("EHR", [128, 16, 16], F32R)
    EHL = R2("EHL", [128, 16, 32], F32)
    ENC = R2("ENC", [128, NKV, 512], F32R)
    WOH = R2("WOH", [128, NKV, C], F32R)
    WOL = R2("WOL", [128, NKV, C], F32R)
    GWH = R2("GWH", [128, 2, 64], F32R)
    GWL = R2("GWL", [128, 2, 64], F32R)
    GL = R2("GL", [64, 512], F32)
    LG = R2("LG", [128, 4, 64], F32)
    GX = R2("GX", [128, 4, 65], F32)
    DEN = R2("DEN", [128, 2, 4], F32)
    MX = R2("MX", [128, 4, 8], F32)
    MI = R2("MI", [128, 4, 8], U32)
    OH = R2("OH", [128, 4, TOPK, E], BF16)
    PR = R2("PR", [128, 4, TOPK, E], F32)
    MB = R2("MB", [128, 4, E], BF16)
    MS = R2("MS", [128, E], F32)
    SLF = R2("SLF", [128, 4, TOPK], F32)
    SLI = [R2(f"SLI{i}", [128, 4 * TOPK], I32) for i in range(2)]

    PS = [ctx.enter_context(nc.psum_tensor(f"ps{i}", [128, 1024], F32)) for i in range(4)]
    half = lambda i: PS[i // 2][:, 512 * (i % 2):512 * (i % 2) + 512]
    bank = [Bank(half(i)) for i in range(8)]
    unit = [Bank(PS[i][:, :]) for i in range(2)]
    pvb = Turns(bank[4:6])
    misc = Turns(bank[6:8])

    XS = nc.dram_tensor("xs_scratch", [E * SLOTS, ROW], F32, kind="Internal").ap()
    TOK = nc.dram_tensor("tok_scratch", [B * T, C], F32, kind="Internal").ap()
    YS = nc.dram_tensor("ys_scratch", [NPAIR, C], F32, kind="Internal").ap()

    def mm(o, l, r, st, sp, *w):
        return PE(lambda e: e.matmul(o, l, r, start=st, stop=sp), *w)

    def tr(o, i, ident, *w):
        return PE(lambda e: e.transpose(o, i, ident), *w)

    def cp(en, o, i, *w):
        if en is S:
            return S(lambda e: e.activation(o, i, ACT.Copy), *w)
        return en(lambda e: e.tensor_copy(o, i), *w)

    def act(o, i, f, *w, scale=1.0):
        return S(lambda e: e.activation(o, i, f, scale=scale), *w)

    def tt(en, o, a, b, op, *w):
        return en(lambda e: e.tensor_tensor(o, a, b, op), *w)

    def ts(en, o, a, s1, o1, *w):
        return en(lambda e: e.tensor_scalar(o, a, s1, None, o1), *w)

    def ts2(en, o, a, s1, s2, o1, o2, *w):
        return en(lambda e: e.tensor_scalar(o, a, s1, s2, o1, o2), *w)

    def stt(o, a, s, b, o1, o2, *w):
        return V(lambda e: e.scalar_tensor_tensor(o, a, s, b, o1, o2), *w)

    def red(o, a, *w):
        return V(lambda e: e.tensor_reduce(o, a, AX.X, ALU.add), *w)

    def count(o, a, *w):
        def do(e):
            with nc.allow_low_precision("a sum of four zeros and ones"):
                return e.tensor_reduce(o, a, AX.X, ALU.add)
        return V(do, *w)

    def bns(o, i, *w):
        return V(lambda e: e.bn_stats(o, i), *w)

    def bna(o, i, *w):
        return V(lambda e: e.bn_aggr(o, i), *w)

    def vtr(o, i, *w):
        return V(lambda e: e.transpose(o, i), *w)

    def rcp(o, i, *w):
        return V(lambda e: e.reciprocal(o, i), *w)

    def ms(en, o, v, *w):
        return en(lambda e: e.memset(o, v), *w)

    def f32(t):
        return t.bitcast(F32)

    def scaled(en, o, i, s, *w):
        if en is S:
            return act(o, i, ACT.Copy, *w, scale=s)
        return ts(en, o, i, s, ALU.mult, *w)

    d_c = Y.dma(D("cst"), lambda e: e.dma_start(CST[:, :], cst))
    xv = x.rearrange("(n p) c -> p n c", p=128)
    d_x = [None] * NT

    def load_x(en, q):
        m = en.dma(D(f"x{q}"), lambda e: e.dma_start(X[:, 4 * q:4 * q + 4, :], xv[:, 4 * q:4 * q + 4, :]))
        for i in range(4):
            d_x[4 * q + i] = m

    load_x(S, 0)
    WQR = PB[0][:, 0:768].rearrange("p (c n) -> p c n", c=2)
    WOR = PB[1][:, 0:1024].rearrange("p (g n) -> p g n", g=NKV)
    GWR = PB[2][:, 0:128].rearrange("p (c n) -> p c n", c=2)
    d_wq = Y.dma(D("wq"), lambda e: e.dma_start(WQR, wqkv.rearrange("(c p) n -> p c n", p=128)))
    load_x(S, 1)
    d_wo = Y.dma(D("wo"), lambda e: e.dma_start(WOR, wos.rearrange("(g p) n -> p g n", p=128)))
    d_gw = Y.dma(D("gw"), lambda e: e.dma_start(GWR, gw.rearrange("(c p) n -> p c n", p=128)))
    load_x(S, 2)
    load_x(Y, 3)

    IDF = CST[:, C_ID:C_ID + 128]
    MH = CST[:, C_MH:C_MH + 2]
    m_id = cp(V, IDB[:, :], CST[:, C_ID:C_ID + 128], d_c)
    m_tri = cp(V, TRI[:, :], CST[:, C_TRI:C_TRI + 128], d_c)
    m_one = ms(V, ONE[:, :], 1.0)
    m_mac = [ms(V, MAC[:, 0, :], 0.0)]
    m_vs1 = [ms(G, VS[b][:, :, :, 16:32], 1.0) for b in range(B)]
    m_rows = ms(G, ROWS[:, :, :, 258:260], 0.0)
    m_pf = ms(G, PF[:, :, :], 0.0)
    m_pf2 = ms(G, PF[:, :, 256:257], float(NPAIR), m_pf)

    xsv = XS.rearrange("(e p r) w -> p e (r w)", e=E, p=128)
    for q in range(4):
        G.dma(D("pf"), lambda e, q=q: e.dma_start(
            xsv[:, 15 * q:15 * q + 15, :], PF[:, :, :].rearrange("p j w -> p (j w)").unsqueeze(1).to_broadcast([128, 15, 2 * ROW])), m_pf2)
    d_pf = G.dma(D("pf"), lambda e: e.dma_start(
        YS.rearrange("(p r) c -> p r c", p=128),
        PF[:, 0, 0:C].unsqueeze(1).to_broadcast([128, NPAIR // 128, C])), m_pf2)

    def split(hi, lo, raw, w, e_hi=S, e_lo=V):
        h = cp(e_hi, hi, raw, w)
        return tt(e_lo, lo, raw, f32(hi), ALU.subtract, h)

    m_wq = split(WQH[:, :, :], WQL[:, :, :], WQR, d_wq)
    m_wo = m_gw = None

    cosT = CST[:, C_COS:C_COS + 128].rearrange("p (t d) -> p t d", d=16)
    sinT = CST[:, C_SIN:C_SIN + 128].rearrange("p (t d) -> p t d", d=16)
    fr = {}
    kt_ok = {}
    qt_ok = {}
    qt_free = {}

    def ln(src, st, key, *w):
        m = bns(st[:, 0:6], src, *w, fr.get(key))
        m = bna(st[:, 6:8], st[:, 0:6], m)
        m = ts(V, st[:, 9:10], st[:, 7:8], 1e-5, ALU.add, m)
        return tt(G, st[:, 8:9], st[:, 9:10], MH[:, 0:1], ALU.pow, m, d_c)

    def p1(i, full, e1, e2):
        p, (b, t) = i % 2, divmod(i, 8)
        st, sq = ST[p], SQ[p]
        m = ln(X[:, i, :], st, ("st", p), d_x[i])
        m = ts2(V, XN[p][:, :], X[:, i, :], st[:, 6:7], st[:, 8:9], ALU.subtract, ALU.mult, m, fr.get(("xn", p)))
        fr["st", p] = m
        yield
        k = misc()
        tr(k.ap[:, 0:128], XN[p][:, 0:128], IDF, m, k.free)
        m = tr(k.ap[:, 128:256], XN[p][:, 128:256], IDF)
        fr["xn", p] = m
        h = cp(e1, XNH[p][:, :], k.ap[:, 0:256], m, fr.get(("xnh", p)))
        m = tt(V, XNL[p][:, :], k.ap[:, 0:256], f32(XNH[p][:, :]), ALU.subtract, h)
        k.free = [m]
        yield
        k = misc()
        n = 0
        for l, r in ((XNH, WQH), (XNH, WQL), (XNL, WQH)):
            for c in range(2):
                mk = mm(k.ap[:, 0:384], l[p][:, 128 * c:128 * c + 128], r[:, c, :], n == 0, n == 5, m, m_wq, k.free)
                n += 1
        fr["xnh", p] = mk
        m1 = bns(sq[:, 0:6], k.ap[:, 0:256], mk, fr.get(("sq", p)))
        m2 = bns(sq[:, 6:12], k.ap[:, 256:320], mk)
        bna(sq[:, 12:14], sq[:, 0:6], m1)
        m = bna(sq[:, 14:16], sq[:, 6:12], m2)
        mv = sq[:, 12:16].rearrange("p (a b) -> p b a", b=2)
        m = tt(V, sq[:, 16:18], mv[:, 0, :], mv[:, 0, :], ALU.mult, m)
        m = stt(sq[:, 18:20], sq[:, 16:18], 1e-6, mv[:, 1, :], ALU.add, ALU.add, m)
        m = tt(G, sq[:, 20:22], sq[:, 18:20], MH, ALU.pow, m)
        yield
        q = QS[p][:, 0:256] if full else QD[:, i % 4, :]
        mv_ = cp(e1, VS[b][:, t, :, 0:16], k.ap[:, 320:384].rearrange("p (g d) -> p g d", d=16), m)
        mk_ = scaled(e1, QS[p][:, 256:320], k.ap[:, 256:320], sq[:, 21:22], m, fr.get(("qs", p)))
        mq = scaled(e1, q, k.ap[:, 0:256], sq[:, 20:21], m, fr.get(("qd", i % 4)) if not full else None)
        k.free = [mv_, mk_, mq, m]
        fr["sq", p] = [mk_, mq]
        vs_ok[i] = [mv_, m_vs1[b]]
        if full:
            yield from rope(i, QS[p][:, :].rearrange("p (h d) -> p h d", d=16), 0, 20, [mq, mk_], e1, e2, ("qs", p))
        else:
            fr["qd_ok", i % 4] = mq
            yield from rope(i, QS[p][:, 256:320].rearrange("p (h d) -> p h d", d=16), 16, 20, [mk_], e1, e2, ("qs", p))

    vs_ok = {}

    def later(i, e1, e2):
        yield from rope(i, QD[:, i % 4, :].rearrange("p (h d) -> p h d", d=16), 0, 16, [fr["qd_ok", i % 4]], e1, e2, ("qd", i % 4))

    def rope(i, src, h0, h1, w, e1, e2, skey):
        p, (b, t), nh = i % 2, divmod(i, 8), h1 - h0
        rt, ru, ex = RT[p][:, h0:h1, :], RU[p][:, h0:h1, :], EX[p]
        co = cosT[:, t:t + 1, :].to_broadcast([128, nh, 16])
        si = sinT[:, t:t + 1, :].to_broadcast([128, nh, 16])
        m1 = tt(e2, rt, src, co, ALU.mult, w, d_c, fr.get(("rt", p)))
        m2 = tt(V, ru[:, :, 0:8], src[:, :, 8:16], si[:, :, 0:8], ALU.mult, w, fr.get(("rt", p)))
        m3 = tt(V, ru[:, :, 8:16], src[:, :, 0:8], si[:, :, 8:16], ALU.mult, w)
        fr[skey] = [m1, m3]
        yield
        m = tt(V, rt, rt, ru, ALU.add, m1, m3)
        a1 = cp(V, ex[:, h0:h1, 0, :], rt, m, fr.get(("ex", p)))
        m = tt(V, ru, rt, ex[:, h0:h1, 0, :], ALU.subtract, a1)
        a2 = cp(V, ex[:, h0:h1, 1, :], ru, m)
        m = tt(V, rt, ru, ex[:, h0:h1, 1, :], ALU.subtract, a2)
        yield
        done = []
        if h0 == 0:
            a3 = cp(V, ex[:, 0:16, 6, :], rt[:, 0:16, :], m)
            done.append(cp(V, ex[:, 0:16, 2:4, :], ex[:, 0:16, 0:1, :].to_broadcast([128, 16, 2, 16]), a1))
            done.append(cp(V, ex[:, 0:16, 4:6, :], ex[:, 0:16, 1:2, :].to_broadcast([128, 16, 2, 16]), a2))
            done.append(cp(V, ex[:, 0:16, 7, :], ex[:, 0:16, 6, :], a3))
        if h1 == 20:
            a3 = cp(V, ex[:, 16:20, 3, :], rt[:, 16 - h0:20 - h0, :], m)
            done.append(cp(e2, ex[:, 16:20, 4:7:2, :], ex[:, 16:20, 0:1, :].to_broadcast([128, 4, 2, 16]), a1))
            done.append(cp(e2, ex[:, 16:20, 2:8:5, :], ex[:, 16:20, 1:2, :].to_broadcast([128, 4, 2, 16]), a2))
            done.append(cp(e2, ex[:, 16:20, 5, :], ex[:, 16:20, 3, :], a3))
        fr["rt", p] = [m, a3]
        yield
        ch, tc = divmod(i, 4)
        for g0, g1 in ((0, 8), (8, 16), (16, 20)):
            if g0 < h0 or g1 > h1:
                continue
            k = misc()
            kb = k.ap.bitcast(BF16).rearrange("p (h n) -> p h n", n=128)
            for h in range(g0, g1):
                m = tr(kb[:, h - g0, :], ex[:, h, :, :].rearrange("p s d -> p (s d)"), IDB[:, :], done, m_id, k.free)
            if g0 < 16:
                dst, w = QT[ch % 2][:, g0:g1, 128 * tc:128 * tc + 128], qt_free.get(ch - 2)
            else:
                dst, w = KT[b][:, :, 128 * t:128 * t + 128], None
            m2 = cp(e1 if g0 else V, dst, kb[:, 0:g1 - g0, :], m, w)
            k.free = [m2]
            if g0 < 16:
                qt_ok.setdefault(i, []).append(m2)
            else:
                kt_ok[i] = m2
            yield
        fr["ex", p] = m

    exp_m, pv_m, s_m = {}, {}, {}
    enc_ok = {}

    def geometry(n):
        ch, r = divmod(n, 64)
        g, r = divmod(r, 16)
        return ch, g, r // 2, r % 2

    def scores(n):
        ch, g, kt, hf = geometry(n)
        b = ch // 2
        u = unit[n % 2]
        w = [kt_ok[8 * b + kt]] + [m for i in range(4) for m in qt_ok[4 * ch + i]]
        for j in range(2):
            s_m[n] = mm(u.ap[:, 512 * j:512 * j + 512], KT[b][:, g, 128 * kt:128 * kt + 128],
                        QT[ch % 2][:, 4 * g + 2 * hf + j, :], True, True, w, exp_m.get(n - 2), *([bk.free for bk in bank[0:4]] if n < 2 else []))
        if n % 64 == 63:
            qt_free[ch] = s_m[n]

    def exponent(n):
        exp_m[n] = act(PB[n % NP][:, :], unit[n % 2].ap, ACT.Exp, s_m[n], pv_m.get(n - NP), pb_free, scale=0.25)

    pb_free = []

    def values(n):
        ch, g, kt, _ = geometry(n)
        b = ch // 2
        if kt == 0:
            pv_bank[ch, g] = pvb()
        k = pv_bank[ch, g]
        for j in range(4):
            m = mm(k.ap[32 * j:32 * j + 32, :], VS[b][:, kt, g, :], PB[(n - 1 + j // 2) % NP][:, 512 * (j % 2):512 * (j % 2) + 512],
                   kt == 0, kt == 7, exp_m[n - 1], exp_m[n], vs_ok[8 * b + kt], k.free)
        pv_m[n - 1] = pv_m[n] = m
        if kt == 7:
            normalise(ch, g, m)

    pv_bank, enc_used = {}, []

    def normalise(ch, g, m):
        k, p = pv_bank[ch, g], g % 2
        assert ch == 0 or ch - 1 in enc_used
        m = vtr(ET[p][:, :, :].rearrange("p a b -> p (a b)"), k.ap, m, fr.get(("et", p)))
        k.free = [m]
        m = rcp(ERC[:, :, :], ET[p][:, :, 16:17], m, fr.get("em"))
        m = tt(V, EM[:, :, :], ET[p][:, :, 0:16], ERC[:, :, :].to_broadcast([128, 16, 16]), ALU.mult, m)
        fr["et", p] = m
        h = cp(V, EHR[:, :, :], EM[:, :, :], m, fr.get("ehr"))
        m = tt(V, EHL[:, :, 16:32], EM[:, :, :], f32(EHR[:, :, :]), ALU.subtract, h, fr.get("ehl"))
        h = cp(V, EHL[:, :, 0:16], f32(EHR[:, :, :]), h, fr.get("ehl"))
        fr["em"], fr["ehr"] = m, [m, h]
        m = vtr(ET[p][:, :, :].rearrange("p a b -> p (a b)"), EHL[:, :, :].rearrange("p a b -> p (a b)"), m, h, fr["et", p])
        fr["ehl"] = m
        m = cp(V, ENC[:, g, :], ET[p][:, :, :].rearrange("p a b -> p (a b)"), m, fr.get("enc"))
        fr["et", p] = m
        enc_ok[ch, g] = m

    def drain(gens):
        for g in gens:
            for _ in g:
                pass

    def staggered(gens, lag):
        live, k = [], 0
        gens = list(gens)
        while gens or live:
            if gens and k % lag == 0:
                live.append(gens.pop(0))
            k += 1
            live = [g for g in live if next(g, "end") != "end"]

    startmisc = misc
    misc = Turns(bank[0:8])
    staggered([p1(i, i < 4, S, G) for i in range(8)], 3)
    misc = startmisc
    m_wo = split(WOH[:, :, :], WOL[:, :, :], WOR, d_wo)
    m_gw = split(GWH[:, :, :], GWL[:, :, :], GWR, d_gw)
    pb_free += [m_wq, m_wo, m_gw]

    def chain(gens):
        for g in gens:
            yield from g

    def attention(ch, bg):
        n0 = 64 * ch
        for n in range(n0, n0 + 64):
            exponent(n)
            if n + 2 < 256:
                if (n + 2) % 64 == 0:
                    for _ in bg:
                        pass
                scores(n + 2)
            if n % 2:
                values(n)
            next(bg, None)

    scores(0)
    scores(1)
    nch = 1 if upto == 1 else 4
    attention(0, chain([later(i, V, G) for i in range(4, 8)] + [p1(i, False, V, G) for i in range(12, 16)]))

    IOTA = CST[:, C_IOTA:C_IOTA + E]
    DID = CST[:, C_DID:C_DID + NT * TOPK].rearrange("p (t k) -> p t k", k=TOPK)
    x1_ok, sig_ok, xt_ok = {}, {}, {}
    rows_free = [m_rows]

    def post(ch, e1, xt_free=()):
        w, rows = [enc_ok[ch, g] for g in range(4)], {}
        for tc in range(4):
            i, n, k = 4 * ch + tc, 0, misc()
            for wt in (WOH, WOL):
                for g in range(4):
                    mk = mm(k.ap[:, 0:256], ENC[:, g, 128 * tc:128 * tc + 128], wt[:, g, :], n == 0, n == 7, w, m_wo, k.free)
                    n += 1
                yield
            m = tt(V, X[:, i, :], X[:, i, :], k.ap[:, 0:256], ALU.add, mk)
            k.free = [m]
            st, key = ST[2 + tc % 2], ("st", 2 + tc % 2)
            m = ln(X[:, i, :], st, key, m)
            m = ts2(V, ROWS[:, tc, :, 0:C], X[:, i:i + 1, :].to_broadcast([128, TOPK, C]), st[:, 6:7], st[:, 8:9],
                    ALU.subtract, ALU.mult, m, rows_free)
            fr[key] = rows[tc] = m
        fr["enc"] = mk
        enc_used.append(ch)
        yield
        for tc in range(4):
            k, m = misc(), rows[tc]
            tr(k.ap[:, 0:128], ROWS[:, tc, 0, 0:128], IDF, m, k.free)
            m = tr(k.ap[:, 128:256], ROWS[:, tc, 0, 128:256], IDF)
            kv = k.ap[:, 0:256].rearrange("p (c n) -> p c n", c=2)
            th, tl = XTH[:, ch, :, 128 * tc:128 * tc + 128], XTL[:, ch, :, 128 * tc:128 * tc + 128]
            h = cp(e1, th, kv, m, *xt_free)
            m = tt(V, tl, kv, f32(th), ALU.subtract, h, *xt_free)
            k.free = [m]
            yield
        xt_ok[ch] = m
        k, n = misc(), 0
        for l, r in ((GWH, XTH), (GWL, XTH), (GWH, XTL)):
            for c in range(2):
                mk = mm(k.ap[0:64, :], l[:, c, :], r[:, ch, c, :], n == 0, n == 5, m, m_gw, k.free)
                n += 1
            yield
        m = cp(V, GL[:, :], k.ap[0:64, :], mk, fr.get("gl"))
        k.free = [m]
        yield
        k = misc()
        for t in range(4):
            mk = tr(k.ap[:, 64 * t:64 * t + 64], GL[:, 128 * t:128 * t + 128], CST[0:64, C_ID:C_ID + 64], m, k.free)
        fr["gl"] = mk
        yield
        m = cp(V, LG[:, :, :].rearrange("p t e -> p (t e)"), k.ap[:, 0:256], mk, fr.get("lg"))
        k.free = [m]
        for t in range(4):
            m1 = V(lambda e, t=t: e.max(MX[:, t, :], LG[:, t, 0:E]), m, fr.get("mx"))
        for t in range(4):
            m2 = V(lambda e, t=t: e.max_index(MI[:, t, :], MX[:, t, :], LG[:, t, 0:E]), m1, fr.get("mi"))
        g1 = tt(V, GX[:, :, 0:E], LG[:, :, 0:E], MX[:, :, 0:1].to_broadcast([128, 4, E]), ALU.subtract, m1, fr.get("gx"))
        g2 = tt(V, GX[:, :, E:E + 4], MX[:, :, 0:4], MX[:, :, 0:1].to_broadcast([128, 4, 4]), ALU.subtract, m1, fr.get("gx"))
        g3 = ts(V, GX[:, :, E + 4:E + 5], LG[:, :, E:E + 1], -1.0, ALU.mult, m, fr.get("gx"))
        fr["lg"] = [m2, g1, g3]
        mfv = EXF[:, 4 * ch:4 * ch + 4, :]
        mf = cp(V, mfv, MI[:, :, 0:TOPK], m2)
        fr["mx"], fr["mi"] = [m2, g2], mf
        ex = act(GX[:, :, :], GX[:, :, :], ACT.Exp, g1, g2, g3)
        mo = tt(V, OH[:, :, :, :], IOTA.unsqueeze(1).unsqueeze(1).to_broadcast([128, 4, TOPK, E]),
                mfv.unsqueeze(3).to_broadcast([128, 4, TOPK, E]), ALU.is_equal, mf, fr.get("oh"))
        yield
        mb = count(MB[:, :, :], OH[:, :, :, :].rearrange("p t k e -> p t e k"), mo, fr.get("mb"))
        yield
        k = misc()
        for t in range(4):
            o = k.ap[:, 64 * t:64 * t + E]
            mk = mm(o, TRI[:, :], MB[:, t, :], True, False, mb, m_tri, k.free)
            for s_ in range(t):
                mk = mm(o, ONE[:, :], MB[:, s_, :], False, False, m_one)
            mk = mm(o, ONE[:, :], MAC[:, ch, :], False, True, m_mac[ch], m_one)
        m = red(MS[:, :], MB[:, :, :].rearrange("p t e -> p e t"), mb, fr.get("ms"))
        m_mac.append(tt(V, MAC[:, (ch + 1) % 4, :], MAC[:, ch, :], MS[:, :], ALU.add, m, mk if ch == 3 else None))
        fr["ms"], fr["mb"] = m_mac[-1], [m, mk]
        if ch == 3:
            mc = mm(k.ap[:, 256:256 + E], ONE[:, :], MAC[:, 0, :], True, True, m_mac[-1], m_one)
            m = cp(V, CNF[:, 0:E], k.ap[:, 256:256 + E], mc)
            mc = cp(V, CNT[:, 0:E], CNF[:, 0:E], m)
            m = stt(KEY[:, 0:E], CNF[:, 0:E], 64.0, IOTA, ALU.mult, ALU.subtract, m)
            m1 = tt(V, KEG[0:E, 0:E], KEY[0:E, 0:E], CST[0:E, C_ID:C_ID + E], ALU.mult, m)
            m1 = red(KES[0:E, 0:1], KEG[0:E, 0:E], m1)
            m = ts(V, KEG[0:E, 0:E], KEY[0:E, 0:E], KES[0:E, 0:1], ALU.is_gt, m1)
            m = red(KES[0:E, 1:2], KEG[0:E, 0:E], m)
            m1 = ts(V, KEG[0:E, 0:E], CST[0:E, C_IOTA:C_IOTA + E], KES[0:E, 1:2], ALU.is_equal, m)
            m2 = ts2(V, KES[0:E, 2:3], KES[0:E, 1:2], float(PART), 64.0 * 64.0, ALU.is_lt, ALU.mult, m)
            m3 = ts2(V, KES[0:E, 3:4], KES[0:E, 1:2], float(FULL), 64.0 * 64.0, ALU.is_lt, ALU.mult, m)
            m2 = stt(KES[0:E, 2:3], KES[0:E, 2:3], 64.0 * 128.0, KES[0:E, 3:4], ALU.add, ALU.add, m2, m3)
            m2 = tt(V, KES[0:E, 3:4], KES[0:E, 0:1], KES[0:E, 2:3], ALU.is_gt, m2)
            mm(k.ap[0:1, 320:320 + E], CST[0:E, C_ROW:C_ROW + 1], KEG[0:E, 0:E], True, True, m1)
            m = mm(k.ap[0:1, 320 + E:321 + E], KES[0:E, 3:4], CST[0:E, C_ONE:C_ONE + 1], True, True, m2)
            sp_ok.append(cp(V, ORD[0:1, 0:E + 1], k.ap[0:1, 320:321 + E], m))
        yield
        kr = k.ap[:, 0:256].rearrange("p (t e) -> p t e", t=4)[:, :, 0:E]
        m = tt(V, PR[:, :, :, :], OH[:, :, :, :], kr.unsqueeze(2).to_broadcast([128, 4, TOPK, E]), ALU.mult, mk, fr.get("pr"))
        fr["oh"], k.free = m, [m]
        rk = RKF[:, 4 * ch:4 * ch + 4, :]
        m = red(rk, PR[:, :, :, :], m)
        fr["pr"] = m
        m1 = ts2(V, SLF[:, :, :], rk, float(SLOTS), float(AWAY), ALU.is_ge, ALU.mult, m, fr.get("slf"))
        m1 = tt(V, SLF[:, :, :], SLF[:, :, :], rk, ALU.add, m1)
        m1 = stt(SLF[:, :, :], mfv, float(SLOTS), SLF[:, :, :], ALU.mult, ALU.add, m1)
        sl = SLI[ch % 2]
        ms_ = cp(V, sl[:, :], SLF[:, :, :].rearrange("p t k -> p (t k)"), m1, fr.get(("sli", ch % 2)))
        fr["slf"] = ms_
        m = red(DEN[:, 0, :], GX[:, :, 0:E], ex, fr.get("den"))
        m2 = ts(V, DEN[:, 1, :], GX[:, :, E + 4], 1.0, ALU.add, ex, fr.get("den"))
        m = rcp(DEN[:, :, :], DEN[:, :, :], m, m2)
        m3 = cp(V, SIG[:, 4 * ch:4 * ch + 4], DEN[:, 1, :], m)
        sig_ok[ch] = m3
        wk = WKF[:, 4 * ch:4 * ch + 4, :]
        m1 = tt(V, wk, GX[:, :, E:E + 4], DEN[:, 0, :].unsqueeze(2).to_broadcast([128, 4, TOPK]), ALU.mult, m)
        fr["gx"], fr["den"] = m1, [m1, m3]
        m1 = cp(V, ROWS[:, :, :, C + 1], wk, m1, rows_free)
        m2 = cp(V, ROWS[:, :, :, C], DID[:, 4 * ch:4 * ch + 4, :], d_c, rows_free)
        yield
        for t in range(4):
            for q in range(TOPK):
                o = SLI[ch % 2][:, TOPK * t + q:TOPK * t + q + 1]
                src = ROWS[:, t, q, :]
                ms2 = G.dma(D("sc"), lambda e, o=o, src=src: e.indirect_dma_start(
                    XS[:, :], bass.IndirectOffsetOnAxis(ap=o, axis=0), src, None,
                    bounds_check=E * SLOTS - 1, oob_is_err=False), ms_, m1, m2, d_pf)
            yield
        fr["sli", ch % 2] = ms2
        tk = Y.dma(D("tok"), lambda e: e.dma_start(
            TOK.rearrange("(n p) c -> p n c", p=128)[:, 4 * ch:4 * ch + 4, :], ROWS[:, :, 0, 0:C]), [rows[tc] for tc in range(4)])
        rows_free[:] = [ms2, tk]
        sc_ok[ch] = ms2

    sc_ok, sp_ok = {}, []

    if upto >= 2:
        attention(1, chain([post(0, V)] + [p1(i, True, V, G) for i in range(8, 12)]))
        attention(2, chain([post(1, V)] + [later(i, V, G) for i in range(12, 16)]))
        p1_done = [q.last() for q in (PE, V, S, G)]
        attention(3, chain([post(2, V, p1_done)]))

    ov = out.rearrange("(n p) c -> p n c", p=128)
    fence = lambda: [q.last() for q in (PE, V, S, G)] + [(c, c.n) for c in dctr.values()]
    if upto >= 2:
        drain([post(3, S, p1_done)])
    if upto == 2:
        Y.dma(D("out"), lambda e: e.dma_start(ov, X[:, :, :]), fence())

    if upto >= 3:
        att_done = fence()
        W1 = Region(nc, a0, top)
        S1H, S1L = W1("S1H", [128, 2, 2 * ISH], F32R), W1("S1L", [128, 2, 2 * ISH], F32R)
        S2H, S2L = W1("S2H", [128, 6, C], F32R), W1("S2L", [128, 6, C], F32R)
        SSG = [W1(f"SSG{i}", [128, 256], F32) for i in range(2)]
        SHF = [W1(f"SHF{i}", [128, 256], F32) for i in range(2)]
        SHH = [W1(f"SHH{i}", [128, 256], F32R) for i in range(2)]
        SHL = [W1(f"SHL{i}", [128, 256], F32R) for i in range(2)]
        STT = W1("STT", [128, 256], F32R)
        a2 = W1.at
        SRW = W1("SRW", [128, 2 * 2 * ISH], F32)
        r1 = SRW[:, :].rearrange("p (c n) -> p c n", c=2)
        m = Y.dma(D("s1"), lambda e: e.dma_start(r1, wsh1.rearrange("(c p) n -> p c n", p=128)), att_done)
        m_s1 = split(S1H[:, :, :], S1L[:, :, :], r1, [m] + att_done)
        r2 = SRW[:, 0:6 * C].rearrange("p (f n) -> p f n", f=6)
        m = Y.dma(D("s1"), lambda e: e.dma_start(r2, wsh2.rearrange("(f p) n -> p f n", p=128)), m_s1)
        m_s2 = split(S2H[:, :, :], S2L[:, :, :], r2, m)
        shb = Turns(bank[0:4])
        sha = bank[4:6]
        shared_free = {}

        def shared(uu):
            ch, hf = divmod(uu, 2)
            w = [xt_ok[ch], m_s1]
            pend = None

            def down(f, h, l):
                wd = [m_s2]
                for t in range(2):
                    o, cs = sha[t].ap[:, 0:C], slice(128 * t, 128 * t + 128)
                    if f < 5:
                        mm(o, SHH[f % 2][:, cs], S2H[:, f, :], f == 0, False, h, wd, sha[t].free)
                        mm(o, SHH[f % 2][:, cs], S2L[:, f, :], False, False)
                        m = mm(o, SHL[f % 2][:, cs], S2H[:, f, :], False, False, l)
                    else:
                        mm(o, STT[:, cs], S2H[:, f, :], False, False, h, l)
                        m = mm(o, STT[:, cs], S2L[:, f, :], False, True)
                return m

            for f in range(6):
                k, p = shb(), f % 2
                for part in range(2 if f < 5 else 1):
                    n, c0 = 0, 256 * f + 128 * part
                    for l, r in ((S1H, XTH), (S1L, XTH), (S1H, XTL)):
                        for c in range(2):
                            mk = mm(k.ap[:, 256 * part:256 * part + 256], l[:, c, c0:c0 + 128],
                                    r[:, ch, c, 256 * hf:256 * hf + 256], n == 0, n == 5, w, k.free)
                            n += 1
                    yield
                if f < 5:
                    s_ = act(SSG[p][:, :], k.ap[:, 0:256], ACT.Silu, mk, shared_free.get(("sg", p)), att_done)
                    m = tt(V, SHF[p][:, :], SSG[p][:, :], k.ap[:, 256:512], ALU.mult, s_, shared_free.get(("hf", p)), att_done)
                    k.free, shared_free["sg", p] = [m], m
                    h = cp(S, SHH[p][:, :], SHF[p][:, :], m, shared_free.get(("hh", p)), att_done)
                    l = tt(V, SHL[p][:, :], SHF[p][:, :], f32(SHH[p][:, :]), ALU.subtract, h, shared_free.get(("hh", p)), att_done)
                else:
                    s_ = act(SSG[p][0:64, :], k.ap[0:64, 0:256], ACT.Silu, mk, shared_free.get(("sg", p)))
                    m = tt(V, SHF[p][0:64, :], SSG[p][0:64, :], k.ap[64:128, 0:256], ALU.mult, s_, shared_free.get(("hf", p)))
                    k.free, shared_free["sg", p] = [m], m
                    h = cp(S, STT[0:64, :], SHF[p][0:64, :], m, shared_free.get("tt"), att_done)
                    l = tt(V, STT[64:128, :], SHF[p][0:64, :], f32(STT[0:64, :]), ALU.subtract, h, shared_free.get("tt"), att_done)
                shared_free["hf", p] = l
                if pend:
                    m = down(*pend)
                    shared_free["hh", pend[0] % 2] = m
                    yield
                pend = (f, h, l)
            m = down(*pend)
            shared_free["tt"] = m
            for t in range(2):
                i = 4 * ch + 2 * hf + t
                x1_ok[i] = stt(X[:, i, :], sha[t].ap[:, 0:C], SIG[:, i:i + 1], X[:, i, :], ALU.mult, ALU.add, m, sig_ok[ch])
                sha[t].free = [x1_ok[i]]
            yield

        drain([shared(uu) for uu in range(8)])
        if upto == 3:
            Y.dma(D("out"), lambda e: e.dma_start(ov, X[:, :, :]), fence())

    if upto >= 4:
        post_done = fence()
        W3 = Region(nc, a2, top)
        W5 = Region(nc, r0, r1_)
        NW = 4
        WR = [W3(f"WR{i}", [128, 2, WPK], F32) for i in range(NW)]
        XB = [W3(f"XB{i}", [128, 3, ROW], F32) for i in range(NW)]
        YI = [W3(f"YI{i}", [128, 3], I32) for i in range(NW)]
        W13H = [W3(f"W13H{i}", [128, 2, 4 * I], F32R) for i in range(2)]
        W13L = [W3(f"W13L{i}", [128, 2, 4 * I], F32R) for i in range(2)]
        W6, W7 = Region(nc, xt0, xt0 + 8192), Region(nc, xt0 + 16384, xt0 + 24576)
        W2H = [W6(f"W2H{i}", [128, 2, 2, C], F32R) for i in range(2)]
        W2L = [W7(f"W2L{i}", [128, 2, 2, C], F32R) for i in range(2)]
        XBH = [W3(f"XBH{i}", [128, 2, 2, 128], F32R) for i in range(2)]
        XBL = [W3(f"XBL{i}", [128, 2, 2, 128], F32R) for i in range(2)]
        XBC = [W3(f"XBC{i}", [128, 2, 128], F32) for i in range(2)]
        SGE = W5("SGE", [128, 3, I], F32)
        HE = [W5(f"HE{i}", [128, 3, I], F32) for i in range(2)]
        HMH = [W3(f"HMH{i}", [128, 2, 128], F32R) for i in range(2)]
        HML = [W3(f"HML{i}", [128, 2, 128], F32R) for i in range(2)]
        HMC = [W5(f"HMC{i}", [128, 128], F32) for i in range(2)]
        HTT = [W5(f"HTT{i}", [112, 2, 128], F32R) for i in range(2)]
        HTC = [W5(f"HTC{i}", [TAIL, 128], F32) for i in range(2)]
        YB = [W5(f"YB{i}", [128, 3, C], F32) for i in range(2)]
        guab, guc = Bank(PS[0].rearrange("p (j n) -> p j n", j=2)), bank[2]
        xab, mix, hab, ya, yb = bank[3], bank[4], bank[5], bank[6], bank[7]
        xc, hc = Bank(mix.ap[:, 0:256]), Bank(mix.ap[0:TAIL, 256:512].rearrange("p (j n) -> p j n", j=2))
        for k in (guab, guc, xab, xc, hc, hab, ya, yb):
            k.free = post_done
        ef = {}
        free = lambda *key: ef.get(key, post_done)
        m_tt = [ms(V, f32(HTT[i][32:64, :, :]), 0.0, post_done) for i in range(2)]
        wl, xl, mk_ = {}, {}, {}

        ones = [((n,), False) for n in range(FULL)]
        threes = [((n, n + 1), True) for n in range(FULL, PART, 2)]
        twos = [((n, n + 1), False) for n in range(PART, E, 2)]
        jobs, short = [], [v for pair in zip(ones + ones, twos) for v in pair]
        short = ones + twos
        for n, job in enumerate(threes):
            jobs.append(job)
            jobs += short[n * len(short) // len(threes):(n + 1) * len(short) // len(threes)]
        JOBS = len(jobs)
        assert sorted(n for g, _ in jobs for n in g) == list(range(E))
        expert = {}

        def number(n):
            def do(e):
                expert[n] = e.value_load(ORD[0:1, n:n + 1], min_val=0, max_val=E - 1)
            Y.wait(sp_ok)
            Y.prog.append(do)

        def load_w(i):
            b, f = i % NW, free("wr", i % NW)
            for j, n in enumerate(jobs[i][0]):
                number(n)
                wl[i] = Y.dma(D(f"w{b}"), lambda q, j=j, n=n: q.dma_start(
                    WR[b][:, j, :], wpk[bass.ds(expert[n], 1)].rearrange("e p n -> (e p) n")), f)

        def load_x(i):
            b, f = i % NW, [free("xb", i % NW), list(sc_ok.values())]
            g, three = jobs[i]
            parts = [(XB[b][:, j, :], n, 0, 128) for j, n in enumerate(g)]
            if len(g) == 1:
                parts.append((XB[b][:, 1, :], g[0], 128, 128))
            if three:
                parts += [(XB[b][64 * j:64 * j + 64, 2, :], n, 128, 64) for j, n in enumerate(g)]
            for part in parts:
                xl[i] = Y.dma(D(f"xe{b}"), lambda q, part=part: q.dma_start(
                    part[0], XS[bass.ds(expert[part[1]] * SLOTS + part[2], part[3]), :]), f)

        def split13(i, j):
            p, r = i % 2, WR[i % NW][:, j, 0:4 * I]
            h = cp(S, W13H[p][:, j, :], r, wl[i], free("w13", p))
            mk_["w13", i, j] = tt(V, W13L[p][:, j, :], r, f32(W13H[p][:, j, :]), ALU.subtract, h, free("w13", p))

        def split2(i):
            p, ng = i % 2, len(jobs[i][0])
            r = WR[i % NW][:, 0:ng, 4 * I:].rearrange("p j (c n) -> p j c n", c=2)
            h = cp(V, W2H[p][:, 0:ng], r, wl[i], free("w2", p))
            mk_["w2", i] = [tt(G, W2L[p][:, j], r[:, j], f32(W2H[p][:, j]), ALU.subtract, h, free("w2", p)) for j in range(ng)]

        def xt_pe(i):
            x_ = XB[i % NW]
            for j in range(2):
                for c in range(2):
                    q = 256 * j + 128 * c
                    mk_["xt", i] = tr(xab.ap[:, q:q + 128], x_[:, j, 128 * c:128 * c + 128], IDF, xl[i], xab.free)
            if jobs[i][1]:
                for c in range(2):
                    mk_["xt", i] = mk_["xtc", i] = tr(xc.ap[:, 128 * c:128 * c + 128], x_[:, 2, 128 * c:128 * c + 128], IDF,
                                                      xl[i], xc.free, hc.free)

        def xt_split(i):
            p, b, nt = i % 2, i % NW, 3 if jobs[i][1] else 2
            v = xab.ap.rearrange("p (j c n) -> p j c n", j=2, c=2)
            h = cp(S, XBH[p][:, :, :, :], v, mk_["xt", i], free("xbh", p))
            if nt == 3:
                m = cp(V, XBC[p][:, :, :], xc.ap.rearrange("p (c n) -> p c n", c=2), mk_["xtc", i], free("xbc", p))
                xc.free = [m]
                mk_["xbc", i] = m
            mk_["yi", i] = cp(V, YI[b][:, 0:nt], XB[b][:, 0:nt, C], xl[i], free("yi", b))
            m = tt(V, XBL[p][:, :, :, :], v, f32(XBH[p][:, :, :, :]), ALU.subtract, h, free("xbh", p))
            xab.free = [m]
            mk_["xbl", i] = m

        def up(i):
            p, w, ng = i % 2, WR[i % NW], len(jobs[i][0])
            for j in range(2):
                wj = j % ng
                n, r3 = 0, [t[p][:, wj, :].rearrange("p (c n) -> p c n", c=2) for t in (W13H, W13L, W13H)]
                for l, r in zip((XBH, XBH, XBL), r3):
                    for c in range(2):
                        m = mm(guab.ap[:, j, 0:2 * I], l[p][:, j, c, :], r[:, c, :], n == 0, n == 5,
                               mk_["xbl", i], mk_["w13", i, wj], guab.free)
                        n += 1
            mk_["up", i] = m
            ef["w13", p] = ef["xbh", p] = [m]
            if jobs[i][1]:
                for c in range(2):
                    for j in range(2):
                        m = mm(guc.ap[64 * j:64 * j + 64, 0:2 * I], XBC[p][:, c, 64 * j:64 * j + 64],
                               w[:, j, 2 * I * c:2 * I * c + 2 * I], c == 0, c == 1, mk_["xbc", i], wl[i], guc.free)
                mk_["upc", i] = m
                ef["xbc", p] = [m]

        def gated(i, shared_tile):
            p = i % 2
            if not shared_tile:
                v = guab.ap
                s_ = act(SGE[:, 0:2, :], v[:, :, 0:I], ACT.Silu, mk_["up", i], free("sge", 0))
                m = tt(V, HE[p][:, 0:2, :], SGE[:, 0:2, :], v[:, :, I:2 * I], ALU.mult, s_, free("he", p))
                ef["sge", 0] = guab.free = [m]
                mk_["he", i] = m
            else:
                v = guc.ap
                s_ = act(SGE[:, 2, :], v[:, 0:I], ACT.Silu, mk_["upc", i], free("sge", 1))
                m = tt(V, HE[p][:, 2, :], SGE[:, 2, :], v[:, I:2 * I], ALU.mult, s_, free("he", p))
                ef["sge", 1] = guc.free = [m]
                mk_["hec", i] = m

        def ht_pe(i):
            h_ = HE[i % 2]
            for j in range(2):
                tr(hab.ap[:, 128 * j:128 * j + 128], h_[:, j, 0:128], IDF, mk_["he", i], hab.free)
            for j in range(2):
                m = tr(hc.ap[:, j, :], h_[:, j, 128:I], IDF, hc.free, xc.free)
            if jobs[i][1]:
                tr(hab.ap[:, 256:384], h_[:, 2, 0:128], IDF, mk_["hec", i])
                m = tr(hab.ap[0:TAIL, 384:512], h_[:, 2, 128:I], IDF)
            mk_["ht", i] = m
            ef["he", i % 2] = [m]

        def ht_split(i):
            p = i % 2
            v = hab.ap[:, 0:256].rearrange("p (j n) -> p j n", j=2)
            h1 = cp(S, HMH[p][:, :, :], v, mk_["ht", i], free("hm", p))
            h2 = cp(S, HTT[p][0:TAIL, :, :], hc.ap, mk_["ht", i], free("hm", p), m_tt[p])
            m = [h2]
            if jobs[i][1]:
                cp(S, HMC[p][:, :], hab.ap[:, 256:384], mk_["ht", i], free("hm", p))
                m.append(cp(S, HTC[p][:, :], hab.ap[0:TAIL, 384:512]))
            m1 = tt(V, HML[p][:, :, :], v, f32(HMH[p][:, :, :]), ALU.subtract, h1, m, free("hm", p))
            m2 = tt(V, HTT[p][64:64 + TAIL, :, :], hc.ap, f32(HTT[p][0:TAIL, :, :]), ALU.subtract, h2, free("hm", p))
            hab.free, hc.free = [m1] + m, [m2]
            mk_["hl", i] = [m1, m2] + m

        def down(i):
            p, w, ng = i % 2, WR[i % NW], len(jobs[i][0])
            k2 = TAIL + 64
            for j in range(2):
                o, h, l = (ya, yb)[j].ap[:, 0:C], W2H[p][:, j % ng], W2L[p][:, j % ng]
                mm(o, HMH[p][:, j, :], h[:, 0, :], True, False, mk_["hl", i], mk_["w2", i], ya.free, yb.free)
                mm(o, HMH[p][:, j, :], l[:, 0, :], False, False)
                mm(o, HML[p][:, j, :], h[:, 0, :], False, False)
                mm(o, HTT[p][0:k2, j, :], h[0:k2, 1, :], False, False)
                m = mm(o, HTT[p][0:k2, j, :], l[0:k2, 1, :], False, True)
            if jobs[i][1]:
                o = ya.ap[:, C:2 * C]
                for c, h in enumerate((HMC[p][:, :], HTC[p][:, :])):
                    for j in range(2):
                        q, w0 = slice(64 * j, 64 * j + 64), 4 * I + C * c
                        m = mm(o[q, :], h[:, q], w[0:h.shape[0], j, w0:w0 + C], c == 0, c == 1)
            mk_["y", i] = m
            ef["hm", p] = ef["w2", p] = [m]
            ef["wr", i % NW] = [m, mk_["w2", i]]

        def give(i):
            p, b = i % 2, i % NW
            ms_ = {}
            for j, en, o in ((0, S, ya.ap[:, 0:C]), (2, S, ya.ap[:, C:2 * C]), (1, V, yb.ap[:, 0:C])):
                if j < 2 or jobs[i][1]:
                    ms_[j] = scaled(en, YB[p][:, j, :], o, XB[b][:, j, C + 1:C + 2], mk_["y", i], free("yb", p))
            ya.free = yb.free = list(ms_.values())
            for j in ms_:
                m = G.dma(D(f"so{p}"), lambda q, j=j: q.indirect_dma_start(
                    YS[:, :], bass.IndirectOffsetOnAxis(ap=YI[b][:, j:j + 1], axis=0), YB[p][:, j, :], None,
                    bounds_check=NPAIR - 1, oob_is_err=False), ms_[j], mk_["yi", i], d_pf)
            ef["yb", p] = ef["yi", b] = [m]
            ef["xb", b] = list(ms_.values()) + [mk_["yi", i], mk_["xt", i]]

        for i in range(NW):
            load_w(i)
        for i in range(NW):
            load_x(i)
        for j in range(len(jobs[0][0])):
            split13(0, j)
        xt_pe(0)
        xt_split(0)
        for i in range(JOBS + 1):
            if i:
                ht_split(i - 1)
            if i < JOBS:
                up(i)
                if i + 1 < JOBS:
                    xt_pe(i + 1)
            if i:
                down(i - 1)
            if i < JOBS:
                ng = len(jobs[i + 1][0]) if i + 1 < JOBS else 0
                if ng:
                    split13(i + 1, 0)
                split2(i)
                gated(i, False)
                if ng == 2:
                    split13(i + 1, 1)
                if jobs[i][1]:
                    gated(i, True)
                if ng:
                    xt_split(i + 1)
                ht_pe(i)
            if i:
                give(i - 1)
                if i + NW - 1 < JOBS:
                    load_w(i + NW - 1)
                    load_x(i + NW - 1)

    if upto >= 5:
        moe_done = fence()
        W4 = Region(nc, a2, top)
        FB = [Bank(W4(f"FB{i}", [128, TOPK, C], F32)) for i in range(8)]
        FO = [Bank(W4(f"FO{i}", [128, C], F32)) for i in range(4)]
        yv = YS.rearrange("(n p k) c -> n p k c", p=128, k=TOPK)
        ok = {}

        def fetch(i):
            k = FB[i % 8]
            ok[i] = Y.dma(D(f"fb{i % 8}"), lambda q: q.dma_start(k.ap[:, :, :], yv[i]), moe_done if i < 8 else k.free)

        for i in range(8):
            fetch(i)
        for i in range(NT):
            k, o = FB[i % 8], FO[i % 4]
            m = red(o.ap[:, :], k.ap[:, :, :].rearrange("p k c -> p c k"), ok[i], moe_done, o.free)
            k.free = [m]
            m = tt(V, o.ap[:, :], o.ap[:, :], X[:, i, :], ALU.add, m, x1_ok[i])
            o.free = [S.dma(D(f"fo{i % 4}"), lambda q, i=i, o=o: q.dma_start(ov[:, i, :], o.ap[:, :]), m)]
            if i + 8 < NT:
                fetch(i + 8)

    for c in dctr.values():
        Y.wait((c, c.n))

    with nc.Block() as block:

        @block.sync
        def _(e):
            Y.run(e)

        @block.tensor
        def _(e):
            PE.run(e)

        @block.vector
        def _(e):
            V.run(e)

        @block.scalar
        def _(e):
            S.run(e)

        @block.gpsimd
        def _(e):
            G.run(e)

    if upto >= 5:
        overflow(nc, wpk, TOK, YS, ov, X, CST, CNT, ORD, RKF, EXF, WKF, a0, top, PS)
    ctx.close()


def overflow(nc, wpk, TOK, YS, ov, X, CST, CNT, ORD, RKF, EXF, WKF, a0, top, PS):
    ctx = ExitStack()
    sems = [ctx.enter_context(nc.semaphore(f"o{i}")) for i in range(7)]
    every = range(sems[0].num, sems[0].num + 7)
    s_w, s_g, s_v, s_t, s_c, s_q, s_p = sems
    assert [q.num for q in sems] == list(every)
    WTS = nc.dram_tensor("wts_scratch", [NPAIR, 1], F32, kind="Internal").ap()
    IDS = nc.dram_tensor("ids_scratch", [E * CAP, 1], I32, kind="Internal").ap()
    M = Region(nc, a0, top)
    NONE = M("NONE", [128, E * CAP // 128], I32)
    OSF, OSL = M("OSF", [128, NT, TOPK], F32), M("OSL", [128, NT * TOPK], I32)
    ODI = M("ODI", [128, NT * TOPK], I32)
    OID, OTK = M("OID", [128, 1], I32), M("OTK", [128, 1], I32)
    OWT = M("OWT", [128, 1], F32)
    OW = M("OW", [128, WPK], F32)
    OX = M("OX", [128, C], F32)
    OXT = M("OXT", [128, C], F32)
    OSG, OH_ = M("OSG", [128, I], F32), M("OH_", [128, I], F32)
    OHT = M("OHT", [128, 2, 128], F32)
    OY = M("OY", [128, C], F32)
    OF, OO = M("OF", [128, TOPK, C], F32), M("OO", [128, C], F32)
    IDF = CST[:, C_ID:C_ID + 128]
    p0, p1, p2, p3 = (PS[i][:, 0:512] for i in range(4))

    left = nc.values_load(ORD[0:1, E:E + 1], min_val=0, max_val=E)
    everyone = (nc.sync, nc.tensor, nc.vector, nc.scalar, nc.gpsimd)
    with nc.If(left > 0):
        for e in everyone:
            e.nop()
        with nc.Block() as block:

            @block.vector
            def _(v):
                v.memset(NONE[:, :], NPAIR).then_inc(s_v, 1)
                v.scalar_tensor_tensor(OSF[:, :, :], EXF[:, :, :], float(CAP), RKF[:, :, :], ALU.mult, ALU.add).then_inc(s_v, 1)
                v.wait_ge(s_v, 2)
                v.tensor_copy(OSL[:, :], OSF[:, :, :].rearrange("p t k -> p (t k)")).then_inc(s_v, 1)
                v.tensor_copy(ODI[:, :], CST[:, C_DID:C_DID + NT * TOPK]).then_inc(s_v, 1)

            @block.gpsimd
            def _(g):
                g.dma_start(WTS.rearrange("(t p k) w -> p t (k w)", p=128, k=TOPK), WKF[:, :, :]).then_inc(s_q, 16)
                g.wait_ge(s_v, 4)
                g.dma_start(IDS.rearrange("(p n) w -> p (n w)", p=128), NONE[:, :]).then_inc(s_q, 16)
                g.wait_ge(s_q, 32)
                for i in range(NT * TOPK):
                    g.indirect_dma_start(IDS[:, :], bass.IndirectOffsetOnAxis(ap=OSL[:, i:i + 1], axis=0), ODI[:, i:i + 1], None,
                                         bounds_check=E * CAP - 1, oob_is_err=False).then_inc(s_q, 16)
                g.wait_ge(s_q, 16 * (2 + NT * TOPK))
                g.dma_reset(every)

        nc.all_engine_barrier(sems_to_clear=every)
        with nc.Fori(0, E) as ex:
            have = nc.values_load(CNT[0:1, bass.ds(ex, 1)], min_val=0, max_val=CAP)
            with nc.Fori(0, NMORE) as j:
                with nc.If(have > j * 128 + 128):
                    for e in everyone:
                        e.nop()
                    with nc.Block() as block:

                        @block.sync
                        def _(y):
                            y.dma_start(OID[:, :], IDS[bass.ds(ex * CAP + j * 128 + 128, 128), :]).then_inc(s_p, 16)
                            y.dma_start(OW[:, :], wpk[bass.ds(ex, 1), :, :].rearrange("a p n -> (a p) n")).then_inc(s_w, 16)
                            y.wait_ge(s_w, 16)

                        @block.gpsimd
                        def _(g):
                            g.wait_ge(s_v, 3)
                            g.indirect_dma_start(OX[:, :], None, TOK[:, :], bass.IndirectOffsetOnAxis(ap=OTK[:, :], axis=0),
                                                 bounds_check=B * T - 1, oob_is_err=False).then_inc(s_g, 16)
                            g.indirect_dma_start(OWT[:, :], None, WTS[:, :], bass.IndirectOffsetOnAxis(ap=OID[:, :], axis=0),
                                                 bounds_check=NPAIR - 1, oob_is_err=False).then_inc(s_g, 16)
                            g.wait_ge(s_v, 8)
                            g.indirect_dma_start(YS[:, :], bass.IndirectOffsetOnAxis(ap=OID[:, :], axis=0), OY[:, :], None,
                                                 bounds_check=NPAIR - 1, oob_is_err=False).then_inc(s_q, 16)
                            g.wait_ge(s_q, 16)
                            g.dma_reset(every)

                        @block.vector
                        def _(v):
                            v.memset(OX[:, :], 0.0).then_inc(s_v, 1)
                            v.memset(OWT[:, :], 0.0).then_inc(s_v, 1)
                            v.wait_ge(s_p, 16)
                            v.tensor_scalar(OTK[:, :], OID[:, :], 2, None, ALU.logical_shift_right).then_inc(s_v, 1)
                            v.wait_ge(s_t, 1)
                            v.tensor_copy(OXT[:, :], p0[:, 0:C]).then_inc(s_v, 1)
                            v.wait_ge(s_c, 1)
                            v.tensor_tensor(OH_[:, :], OSG[:, :], p1[:, I:2 * I], ALU.mult).then_inc(s_v, 1)
                            v.wait_ge(s_t, 3)
                            v.tensor_copy(OHT[:, 0, :], p2[:, 0:128]).then_inc(s_v, 1)
                            v.tensor_copy(OHT[0:48, 1, :], p2[0:48, 128:256]).then_inc(s_v, 1)
                            v.wait_ge(s_t, 4)
                            v.tensor_scalar(OY[:, :], p3[:, 0:C], OWT[:, 0:1], None, ALU.mult).then_inc(s_v, 1)

                        @block.scalar
                        def _(a):
                            a.wait_ge(s_t, 2)
                            a.activation(OSG[:, :], p1[:, 0:I], ACT.Silu).then_inc(s_c, 1)

                        @block.tensor
                        def _(t):
                            t.wait_ge(s_g, 32)
                            t.transpose(p0[:, 0:128], OX[:, 0:128], IDF)
                            t.transpose(p0[:, 128:256], OX[:, 128:256], IDF).then_inc(s_t, 1)
                            t.wait_ge(s_w, 16)
                            t.wait_ge(s_v, 4)
                            t.matmul(p1[:, 0:2 * I], OXT[:, 0:128], OW[:, 0:2 * I], start=True, stop=False)
                            t.matmul(p1[:, 0:2 * I], OXT[:, 128:256], OW[:, 2 * I:4 * I], start=False, stop=True).then_inc(s_t, 1)
                            t.wait_ge(s_v, 5)
                            t.transpose(p2[:, 0:128], OH_[:, 0:128], IDF)
                            t.transpose(p2[0:48, 128:256], OH_[:, 128:I], IDF).then_inc(s_t, 1)
                            t.wait_ge(s_v, 7)
                            t.matmul(p3[:, 0:C], OHT[:, 0, :], OW[:, 4 * I:4 * I + C], start=True, stop=False)
                            t.matmul(p3[:, 0:C], OHT[0:48, 1, :], OW[0:48, 4 * I + C:], start=False, stop=True).then_inc(s_t, 1)

                    nc.all_engine_barrier(sems_to_clear=every)

        with nc.Block() as block:
            yv = YS.rearrange("(n p k) c -> n p k c", p=128, k=TOPK)

            @block.sync
            def _(y):
                for i in range(NT):
                    if i:
                        y.wait_ge(s_v, 2 * i - 1)
                    y.dma_start(OF[:, :, :], yv[i]).then_inc(s_w, 16)
                    y.wait_ge(s_v, 2 * i + 2)
                    y.dma_start(ov[:, i, :], OO[:, :]).then_inc(s_p, 16)
                    y.wait_ge(s_p, 16 * i + 16)

            @block.vector
            def _(v):
                for i in range(NT):
                    v.wait_ge(s_w, 16 * i + 16)
                    if i:
                        v.wait_ge(s_p, 16 * i)
                    v.tensor_reduce(OO[:, :], OF[:, :, :].rearrange("p k c -> p c k"), AX.X, ALU.add).then_inc(s_v, 1)
                    v.wait_ge(s_v, 2 * i + 1)
                    v.tensor_tensor(OO[:, :], OO[:, :], X[:, i, :], ALU.add).then_inc(s_v, 1)
    ctx.close()


def layout(x, wq, wk, wv, wo, gate, sgate, w13, w2, sgu, sdn):
    wqkv = np.concatenate([wq, wk, wv], 1)
    wo5 = wo.reshape(NKV, 4, 1, HD, C)
    wos = np.concatenate([wo5, wo5], 2).reshape(NKV * 128, C)
    gw = np.concatenate([gate, sgate, np.zeros((3, C), gate.dtype)], 0).T
    g, u = sgu[:ISH], sgu[ISH:]
    order = [w[f:min(f + 128, ISH)] for f in range(0, ISH, 128) for w in (g, u)]
    wsh1 = np.concatenate(order, 0).T
    sdt = sdn.T
    wsh2 = np.concatenate([sdt, sdt[640:]], 0)
    a = w13.transpose(0, 2, 1).reshape(E, 2, 128, 2 * I).transpose(0, 2, 1, 3).reshape(E, 128, 4 * I)
    w2t = w2.transpose(0, 2, 1)
    z = np.zeros((E, 16, C), w2.dtype)
    tail = np.concatenate([w2t[:, 128:], z, w2t[:, 128:], z], 1)
    wpk = np.concatenate([a, w2t[:, :128], tail], 2)
    flat = dict(x=x.reshape(B * T, C), wqkv=wqkv, wos=wos, gw=gw, wsh1=wsh1, wsh2=wsh2, wpk=wpk, cst=constants())
    return {k: np.ascontiguousarray(v) for k, v in flat.items()}


def kernel(L0_attn_x, L0_attn_q_kernel, L0_attn_k_kernel, L0_attn_v_kernel, L0_attn_out_kernel, L0_ffn_gate_w,
           L0_ffn_shared_gate_w, L0_ffn_w13, L0_ffn_w2, L0_ffn_se_gate_up_w, L0_ffn_se_down_w):
    import concourse.bacc as _bacc
    from concourse.bass_utils import run_bass_kernel_spmd as _run

    given = [np.asarray(a) for a in (
        L0_attn_x, L0_attn_q_kernel, L0_attn_k_kernel, L0_attn_v_kernel, L0_attn_out_kernel, L0_ffn_gate_w,
        L0_ffn_shared_gate_w, L0_ffn_w13, L0_ffn_w2, L0_ffn_se_gate_up_w, L0_ffn_se_down_w)]
    nc = _bacc.Bacc("TRN2", target_bir_lowering=False, num_devices=1)
    arrays, args = {}, []
    for name, a in layout(*given).items():
        arrays[f"in_{name}"] = a
        args.append(nc.dram_tensor(f"in_{name}", a.shape, mybir.dt.from_np(a.dtype), kind="ExternalInput").ap())
    args.append(nc.dram_tensor("out_0_dram", (B * T, C), F32, kind="ExternalOutput").ap())
    moe_block_kernel(nc, *args)
    r = _run(nc, [arrays], core_ids=[0])
    return r.results[0]["out_0_dram"].reshape(B, T, C)
```

```python
from contextlib import ExitStack

import numpy as np

import concourse.bass as bass
from concourse import mybir

ACT = mybir.ActivationFunctionType
ALU = mybir.AluOpType
AX = mybir.AxisListType
F32 = mybir.dt.float32
F32R = mybir.dt.float32r
BF16 = mybir.dt.bfloat16
I32 = mybir.dt.int32
U32 = mybir.dt.uint32

B, T, C = 2, 1024, 256
NH, NKV, HD = 16, 4, 16
NT = B * T // 128
E, I, TOPK = 60, 176, 4
ISH = 704
CAP = B * T
SLOTS = 256
FULL, PART, SOME = 2, 18, 38
ROWS_AT = [208, 192]
for _n, _r in ((2, (192, 184, 180, 176, 172, 172, 168, 160)), (4, (156, 152, 148, 140, 134)),
               (2, (128, 128, 128, 124, 122, 118, 116, 114, 108, 102, 96))):
    ROWS_AT += [r for r in _r for _ in range(_n)]
LOW = min(ROWS_AT)
ORDER = "31513252325232523252323232"
BATCH, FIRST = 8, 40
AWAY = 1 << 20
ROW = 260
NPAIR = B * T * TOPK
IA, IB = 112, 64
WPK = 2 * 2 * I + C

NMORE = -(-(CAP - LOW) // 128)
IDROWS = CAP + 128
C_ID, C_TRI, C_COS, C_SIN, C_IOTA, C_DID, C_ROW, C_ONE, C_CAP, C_PLACE = np.cumsum([0, 128, 128, 128, 128, 60, 64, 1, 1, 60]).tolist()
NCST = C_PLACE + E


def plan():
    ones = [[((n,), 128)] for n in range(FULL)]
    twos = [[((n, n + 1), 128)] for n in range(SOME, E, 2)]
    threes = [[((n, n + 1), 192)] for n in range(FULL, PART, 2)]
    fives = [[((n, n + 1), 160), ((n + 2, n + 3), 160)] for n in range(PART, SOME, 4)]
    jobs, extra = [], []
    for c in ORDER:
        block = {"1": ones, "2": twos, "3": threes, "5": fives}[c].pop(0)
        if block[0][1] > 128:
            extra.append(([(v, 128, r - 128) for g, r in block for v in g], len(jobs), len(jobs) + len(block) - 1))
        jobs += block
    return jobs, extra


def constants():
    c = np.zeros((128, NCST), np.float32)
    p = np.arange(128)
    c[:, C_ID:C_ID + 128] = np.eye(128)
    c[:, C_TRI:C_TRI + 128] = p[:, None] < p[None, :]
    frac = np.arange(0, HD, 2, dtype=np.float32) / np.float32(HD)
    inv = np.float32(1.0) / np.power(np.float32(10000.0), frac, dtype=np.float32)
    ang = np.arange(T, dtype=np.float32)[:, None] * inv[None, :]
    cos, sin = np.cos(ang.astype(np.float64)), np.sin(ang.astype(np.float64))
    cos = np.concatenate([cos, cos], 1).reshape(T // 128, 128, HD)
    sin = np.concatenate([-sin, sin], 1).reshape(T // 128, 128, HD)
    c[:, C_COS:C_COS + 128] = cos.transpose(1, 0, 2).reshape(128, -1)
    c[:, C_SIN:C_SIN + 128] = sin.transpose(1, 0, 2).reshape(128, -1)
    c[:, C_IOTA:C_IOTA + E] = np.arange(E)
    tok = np.arange(NT)[None, :, None] * 128 + p[:, None, None]
    c[:, C_DID:C_DID + NT * TOPK] = (tok * TOPK + np.arange(TOPK)).reshape(128, -1)
    c[:, C_ROW] = p
    c[:, C_ONE] = 1.0
    places = [n for g, _ in plan()[0] for n in g]
    c[:, C_PLACE:C_PLACE + E] = places
    c[:, C_CAP:C_CAP + E] = [64.0 * ROWS_AT[n] for n in places]
    return c


class Ctr:

    def __init__(self, sem):
        self.sem, self.n, self.when = sem, 0, {}


def latest(*marks):
    t = 0.0
    for m in marks:
        if isinstance(m, list):
            t = max(t, latest(*m))
        elif m is not None:
            t = max(t, m[0].when.get(m[1], 0.0))
    return t


class Eng:
    bus = 0.0

    def __init__(self, sem, lat):
        self.ctr, self.prog, self.met, self.at, self.lat = Ctr(sem), [], {}, 600.0, lat

    def wait(self, *marks):
        for m in marks:
            if m is None:
                continue
            if isinstance(m, list):
                self.wait(*m)
                continue
            c, v = m
            if self.met.get(id(c), 0) < v:
                self.met[id(c)] = v
                self.prog.append(lambda e, c=c, v=v: e.wait_ge(c.sem, v))

    def __call__(self, fn, *marks, ns=200.0):
        self.wait(*marks)
        c = self.ctr
        c.n += 1
        self.at = max(self.at, latest(*marks)) + ns
        c.when[c.n] = self.at + self.lat
        self.prog.append(lambda e: fn(e).then_inc(c.sem, 1))
        return (c, c.n)

    def dma(self, c, fn, *marks, ns=50.0, size=0):
        self.wait(*marks)
        c.n += 16
        self.at = max(self.at, latest(*marks)) + ns
        if size:
            Eng.bus = max(Eng.bus, self.at + 1000.0) + size / 360.0
            c.when[c.n] = Eng.bus + 1100.0
        else:
            c.when[c.n] = self.at + 2500.0
        self.prog.append(lambda e: fn(e).then_inc(c.sem, 16))
        return (c, c.n)

    def last(self):
        return (self.ctr, self.ctr.n) if self.ctr.n else None

    def run(self, eng):
        for f in self.prog:
            f(eng)


class Bank:

    def __init__(self, ap):
        self.ap, self.free, self.taken = ap, [], False

    def leave(self, *marks):
        self.free, self.taken = list(marks), False


class Turns:

    def __init__(self, items):
        self.items, self.i = items, -1

    def __call__(self):
        self.i += 1
        return self.items[self.i % len(self.items)]


class Region:

    def __init__(self, nc, base, end):
        self.nc, self.at, self.end = nc, base, end

    def __call__(self, name, shape, dt):
        n = int(np.prod(shape[1:])) * (2 if dt == BF16 else 4)
        t = self.nc.alloc_sbuf_tensor_at(name, shape, dt, offset=self.at)
        self.at += -(-n // 32) * 32
        assert self.at <= self.end, (name, self.at, self.end)
        return t


def moe_block_kernel(nc, x, wqkv, wos, gw, wsh1, wsh2, wpk, wtl, cst, out):
    ctx = ExitStack()
    sem = lambda name: ctx.enter_context(nc.semaphore(name))
    PE, V, S, G, Y = (Eng(sem(n), lat) for n, lat in
                      (("s_pe", 200.0), ("s_dve", 130.0), ("s_act", 170.0), ("s_pool", 150.0), ("s_sp", 150.0)))
    dctr = {}

    def D(name):
        if name not in dctr:
            dctr[name] = Ctr(sem("d_" + name))
        return dctr[name]

    base, top = -(-nc.sbuf_base // 64) * 64, nc.sbuf_top
    P_ = Region(nc, base, top)
    X = P_("X", [128, NT, C], F32)
    xt0 = P_.at
    XTH = P_("XTH", [128, 4, 2, 512], F32R)
    XTL = P_("XTL", [128, 4, 2, 512], F32R)
    R0 = [Region(nc, xt0 + q, xt0 + q + 8192) for q in (8192, 24576, 0, 16384)]
    CST = P_("CST", [128, NCST], F32)
    IDB = P_("IDB", [128, 128], BF16)
    TRI = P_("TRI", [128, 128], BF16)
    ONE = P_("ONE", [128, 128], BF16)
    MAC = P_("MAC", [128, 4, E], BF16)
    r0 = P_.at
    ROWS = P_("ROWS", [128, 4, TOPK, ROW], F32)
    pf0 = P_.at
    PF = P_("PF", [128, 2, ROW], F32)
    r1_ = P_.at
    SIG = P_("SIG", [128, NT], F32)
    CNT = P_("CNT", [128, 64], I32)
    CNF = P_("CNF", [128, 64], F32)
    ORD = P_("ORD", [1, 64], I32)
    KEY = P_("KEY", [128, 64], F32)
    KEG = P_("KEG", [128, 64], F32)
    MH = P_("MH", [128, 2], F32)
    KES = P_("KES", [128, 4], F32)
    RKF = P_("RKF", [128, NT, TOPK], F32)
    EXF = P_("EXF", [128, NT, TOPK], F32)
    WKF = P_("WKF", [128, NT, TOPK], F32)
    ST = [P_(f"ST{i}", [128, 10], F32) for i in range(4)]
    SP = [P_(f"SP{i}", [128, 10], F32) for i in range(4)]
    SQ = [P_(f"SQ{i}", [128, 8], F32) for i in range(4)]
    a0 = P_.at
    R1 = Region(nc, a0, top)
    QT, KT, VS = [None, None], [None, None], [None, None]
    QT[0] = R1("QT0", [128, NH, 512], BF16)
    KT[0] = R1("KT0", [128, NKV, T], BF16)
    VS[0] = R1("VS0", [128, 8, NKV, 32], F32)
    WQH = R1("WQH", [128, 2, 384], F32R)
    WQL = R1("WQL", [128, 2, 384], F32R)
    QS = [R1(f"QS{i}", [128, 20, 16], F32) for i in range(8)]
    XN, XNH, XNL, RT, RU, EX = [], [], [], [], [], []
    for i in range(4):
        r_ = Region(nc, R0[i].at, R0[i].end)
        RT.append(r_(f"RT{i}", [128, 20, 16], F32))
        RU.append(r_(f"RU{i}", [128, 20, 16], F32))
        XN.append(R0[i](f"XN{i}", [128, C], F32))
        XNH.append(R0[i](f"XNH{i}", [128, C], F32R))
        XNL.append(R0[i](f"XNL{i}", [128, C], F32R))
        EX.append(R0[i](f"EX{i}", [128, 20, 8, 16], BF16))
    a1 = R1.at
    R2 = Region(nc, a1, top)
    QT[1] = R2("QT1", [128, NH, 512], BF16)
    KT[1] = R2("KT1", [128, NKV, T], BF16)
    VS[1] = R2("VS1", [128, 8, NKV, 32], F32)
    NP = 6
    PB = [R2(f"PB{i}", [128, 1024], F32) for i in range(NP)]
    ET = [R2(f"ET{i}", [128, 16, 32], F32) for i in range(2)]
    EM = R2("EM", [128, 16, 16], F32)
    ERC = R2("ERC", [128, 16, 1], F32)
    EHR = R2("EHR", [128, 16, 16], F32R)
    EU = R2("EU", [128, 16, 32], F32)
    EL = R2("EL", [128, 16, 32], F32)
    HALF = Region(nc, R2.at, top)("HALF", [128, NKV, 512], F32)
    ENC = R2("ENC", [128, 2, 2, 512], F32R)
    WOH = R2("WOH", [128, 2, C], F32R)
    WOL = R2("WOL", [128, 2, C], F32R)
    GW = R2("GW", [128, 2, 2, 64], F32R)
    GL = R2("GL", [128, 512], F32)
    LG = R2("LG", [128, 4, 64], F32)
    GX = R2("GX", [128, 4, 65], F32)
    DEN = R2("DEN", [128, 2, 4], F32)
    MX = R2("MX", [128, 4, 8], F32)
    MI = R2("MI", [128, 4, 8], U32)
    OH = R2("OH", [128, 4, TOPK, E], BF16)
    PR = R2("PR", [128, 4, TOPK, E], F32)
    MB = R2("MB", [128, 4, E], BF16)
    MS = R2("MS", [128, E], F32)
    SLF = R2("SLF", [128, 4, TOPK], F32)
    sli0 = R2.at
    SLI = [R2(f"SLI{i}", [128, 4 * TOPK], I32) for i in range(2)]

    PS = [ctx.enter_context(nc.psum_tensor(f"ps{i}", [128, 1024], F32)) for i in range(4)]
    half = lambda i: PS[i // 2][:, 512 * (i % 2):512 * (i % 2) + 512]
    bank = [Bank(half(i)) for i in range(8)]
    unit = [Bank(PS[i][:, :]) for i in range(2)]
    pvb = Turns(bank[4:6])

    XS = nc.dram_tensor("xs_scratch", [E * SLOTS, ROW], F32, kind="Internal").ap()
    TOK = nc.dram_tensor("tok_scratch", [B * T, C], F32, kind="Internal").ap()
    YS = nc.dram_tensor("ys_scratch", [NPAIR, C], F32, kind="Internal").ap()

    table = [None]

    def size(o):
        return int(np.prod(o.shape[1:]))

    def cost(en, o, *srcs):
        n = max(size(a) for a in (o,) + srcs)
        if en is S:
            return 50 + 0.84 * n
        if en is G:
            return 60 + 2.4 * n
        slow = len(srcs) > 1 or "PSUM" in str(srcs[0].space)
        return 65 + (1.04 if slow else 0.52) * (0.5 if o.dtype == srcs[0].dtype == BF16 else 1.0) * n

    def mm(o, l, r, st, sp, *w, ns=None):
        if ns is None:
            ns = 5.0 + size(r) * 1.665 if r.dtype == F32 else 2.5 + max(107.0 if r.dtype == F32R else 25.0, size(r) * 0.4165)
        return PE(lambda e: e.matmul(o, l, r, start=st, stop=sp), *w, ns=ns)

    def tr(o, i, ident, *w):
        return PE(lambda e: e.transpose(o, i, ident), *w, ns=56.0 if i.dtype == BF16 else 109.5)

    def cp(en, o, i, *w):
        if en is S:
            return act(o, i, ACT.Copy, *w)
        return en(lambda e: e.tensor_copy(o, i), *w, ns=cost(en, o, i))

    def act(o, i, f, *w, scale=1.0):
        ns = cost(S, o) + (0 if isinstance(scale, float) else 95)
        if f != ACT.Copy and f != table[0]:
            table[0], ns = f, ns + 1300.0
        return S(lambda e: e.activation(o, i, f, scale=scale), *w, ns=ns)

    def tt(en, o, a, b, op, *w):
        ns = 300.0 + 164.0 * size(o) if op == ALU.pow else cost(en, o, a, b)
        return en(lambda e: e.tensor_tensor(o, a, b, op), *w, ns=ns)

    def ts(en, o, a, s1, o1, *w):
        return en(lambda e: e.tensor_scalar(o, a, s1, None, o1), *w, ns=cost(en, o, a) + (0 if isinstance(s1, float) else 62))

    def ts2(en, o, a, s1, s2, o1, o2, *w):
        return en(lambda e: e.tensor_scalar(o, a, s1, s2, o1, o2), *w, ns=cost(en, o, a) + (0 if isinstance(s1, float) else 125))

    def stt(o, a, s, b, o1, o2, *w):
        return V(lambda e: e.scalar_tensor_tensor(o, a, s, b, o1, o2), *w, ns=cost(V, o, a, b) + (0 if isinstance(s, float) else 62))

    def red(o, a, *w):
        return V(lambda e: e.tensor_reduce(o, a, AX.X, ALU.add), *w, ns=65 + 1.04 * size(a))

    def count(o, a, *w):
        def do(e):
            with nc.allow_low_precision("a sum of four zeros and ones"):
                return e.tensor_reduce(o, a, AX.X, ALU.add)
        return V(do, *w, ns=65 + 1.04 * size(a))

    def bns(o, i, *w):
        return V(lambda e: e.bn_stats(o, i), *w, ns=cost(V, i, i, i))

    def bna(o, i, *w):
        return V(lambda e: e.bn_aggr(o, i), *w, ns=75.0)

    def vtr(o, i, *w):
        return V(lambda e: e.transpose(o, i), *w, ns=600.0)

    def rcp(o, i, *w):
        return V(lambda e: e.reciprocal(o, i), *w, ns=170.0)

    def ms(en, o, v, *w):
        return en(lambda e: e.memset(o, v), *w, ns=60 + 0.8 * size(o) if en is G else cost(en, o, o))

    def sums(o, i, acc, scale, *w):
        return S(lambda e: e.activation(o, i, ACT.Square, scale=scale, accum_out=acc), *w, ns=cost(S, o) + 93)

    def f32(t):
        return t.bitcast(F32)

    def scaled(en, o, i, s, *w):
        if en is S:
            return act(o, i, ACT.Copy, *w, scale=s)
        return ts(en, o, i, s, ALU.mult, *w)

    xv = x.rearrange("(n p) c -> p n c", p=128)
    d_x = [None] * NT

    def load_x0(en, i0, i1):
        m = en.dma(D(f"x{i0}"), lambda e: e.dma_start(X[:, i0:i1, :], xv[:, i0:i1, :]), size=(i1 - i0) * 128 * C * 4)
        for i in range(i0, i1):
            d_x[i] = m

    raw = ROWS[:, :, :, :].rearrange("p t k w -> p (t k w)")
    WQR = raw[:, 0:768].rearrange("p (c n) -> p c n", c=2)
    WOR = raw[:, 768:1280].rearrange("p (g n) -> p g n", g=2)
    GWR = raw[:, 1280:1408].rearrange("p (c n) -> p c n", c=2)
    load_x0(Y, 0, 2)
    d_c = S.dma(D("cst"), lambda e: e.dma_start(CST[:, :], cst), size=128 * NCST * 4)
    d_wq = Y.dma(D("wq"), lambda e: e.dma_start(WQR, wqkv.rearrange("(c p) n -> p c n", p=128)), size=C * 384 * 4)
    load_x0(Y, 2, 4)
    load_x0(Y, 4, 8)
    d_wo = Y.dma(D("wo"), lambda e: e.dma_start(WOR, wos.rearrange("(g p) n -> p g n", p=128)), size=C * C * 4)
    d_gw = Y.dma(D("gw"), lambda e: e.dma_start(GWR, gw.rearrange("(c p) n -> p c n", p=128)), size=C * 64 * 4)
    load_x0(Y, 8, 16)

    IDF = CST[:, C_ID:C_ID + 128]
    m_mh = ms(G, MH[:, :], -0.5)
    m_vs1 = [ms(G, VS[b][:, :, :, 16:32], 1.0) for b in range(B)]
    m_pf = ms(G, PF[:, :, :], 0.0)
    m_pf2 = ms(G, PF[:, :, 256:257], float(NPAIR), m_pf)
    m_tri = m_rows = m_wo = m_gw = None
    m_mac = [None]

    def split(hi, lo, raw, w, e_hi=S, e_lo=V):
        h = cp(e_hi, hi, raw, w)
        return tt(e_lo, lo, raw, f32(hi), ALU.subtract, h)

    cosT = CST[:, C_COS:C_COS + 128].rearrange("p (t d) -> p t d", d=16)
    sinT = CST[:, C_SIN:C_SIN + 128].rearrange("p (t d) -> p t d", d=16)
    fr = {}
    kt_ok, vs_ok = {}, {}
    qt_ok = {}
    qs_ok = {}
    qt_free = {}

    def ln(src, st, key, *w):
        m = bns(st[:, 0:6], src, *w, fr.get(key))
        m = bna(st[:, 6:8], st[:, 0:6], m)
        m = ts(V, st[:, 9:10], st[:, 7:8], 1e-5, ALU.add, m)
        return tt(G, st[:, 8:9], st[:, 9:10], MH[:, 0:1], ALU.pow, m, m_mh)

    def norm(src, st, key, calm, *w):
        yield from calm(V, [*w, fr.get(key)])
        m = bns(st[:, 0:6], src, *w, fr.get(key))
        yield from calm(V, m)
        m = bna(st[:, 6:8], st[:, 0:6], m)
        yield from calm(V, m)
        m = ts(V, st[:, 9:10], st[:, 7:8], 1e-5, ALU.add, m)
        yield from calm(G, m)
        return tt(G, st[:, 8:9], st[:, 9:10], MH[:, 0:1], ALU.pow, m, m_mh)

    def grab(banks, calm):
        while all(k.taken for k in banks):
            yield
        k = min((k for k in banks if not k.taken), key=lambda k: latest(k.free))
        k.taken = True
        yield from calm(PE, k.free)
        return k

    def tile(i, s, bk, h1, calm, e_hi, pick):
        b, t = divmod(i, 8)
        st, sq, qs = ST[s], SQ[s], QS[i % 8]
        m = yield from norm(X[:, i, :], st, ("st", s), calm, d_x[i])
        yield from calm(V, m)
        m = ts2(V, XN[s][:, :], X[:, i, :], st[:, 6:7], st[:, 8:9], ALU.subtract, ALU.mult, m, fr.get(("rt", s)))
        fr["st", s] = m
        yield from calm(PE, m)
        k = yield from grab(bk, calm)
        tr(k.ap[:, 0:128], XN[s][:, 0:128], IDF, m, k.free, d_c)
        m = tr(k.ap[:, 128:256], XN[s][:, 128:256], IDF)
        yield from calm(e_hi, m)
        h = cp(e_hi, XNH[s][:, :], k.ap[:, 0:256], m)
        m = tt(V, XNL[s][:, :], k.ap[:, 0:256], f32(XNH[s][:, :]), ALU.subtract, h)
        k.leave(m)
        yield from calm(PE, m)
        k = yield from grab(bk, calm)
        while m_wq is None or len(m_wq) < 2:
            yield
        n = 0
        for l, r, w in ((XNH, WQH, m_wqh), (XNL, WQH, m_wqh), (XNH, WQL, list(m_wq))):
            for c in range(2):
                mk = mm(k.ap[:, 0:384], l[s][:, 128 * c:128 * c + 128], r[:, c, :], n == 0, n == 5, m, w, k.free)
                n += 1
        yield from calm(S, mk)
        junk = XN[s][:, :]
        m1 = sums(junk[:, 0:64], k.ap[:, 0:64], sq[:, 0:1], 0.125, mk, fr.get(("sq", s)))
        m2 = sums(junk, k.ap[:, 64:320], sq[:, 1:2], 0.0625, m1)
        mv = cp(S, VS[b][:, t, :, 0:16], k.ap[:, 320:384].rearrange("p (g d) -> p g d", d=16), mk)
        yield from calm(V, m2)
        m = ts(V, sq[:, 2:4], sq[:, 0:2], 1e-6, ALU.add, m2)
        yield from calm(G, m)
        m = tt(G, sq[:, 4:6], sq[:, 2:4], MH[:, :], ALU.pow, m, m_mh)
        yield from calm(S, m)
        w = fr.get(("qs", i % 8))
        scaled(S, qs[:, 0:4, :], k.ap[:, 0:64].rearrange("p (h d) -> p h d", d=16), sq[:, 4:5], m, w)
        m = scaled(S, qs[:, 4:20, :], k.ap[:, 64:320].rearrange("p (h d) -> p h d", d=16), sq[:, 5:6], m, w)
        k.leave(m)
        fr["sq", s] = m
        vs_ok[i] = [mv, m_vs1[b]]
        qs_ok[i] = m
        yield from rope(i, s, bk, 0, h1, calm, pick)

    def rope(i, s, bk, h0, h1, calm, pick):
        (b, t), nh, ch, tc = divmod(i, 8), h1 - h0, i // 4, i % 4
        rt, ru, ex, src = RT[s][:, h0:h1, :], RU[s][:, h0:h1, :], EX[s], QS[i % 8][:, h0:h1, :]
        q0 = max(h0, 4)
        co = cosT[:, t:t + 1, :].to_broadcast([128, nh, 16])
        si = sinT[:, t:t + 1, :].to_broadcast([128, nh, 16])
        side = G if nh > 4 else V
        m, w = [qs_ok[i], d_c], fr.get(("rt", s))
        yield from calm(V, m)
        m1 = tt(pick(rt, m, side, V), rt, src, co, ALU.mult, m, w)
        m2 = tt(pick(ru[:, :, 0:8], m, V, G), ru[:, :, 0:8], src[:, :, 8:16], si[:, :, 0:8], ALU.mult, m, w)
        m3 = tt(pick(ru[:, :, 0:8], m, V, G), ru[:, :, 8:16], src[:, :, 0:8], si[:, :, 8:16], ALU.mult, m, w)
        fr["qs", i % 8] = [m1, m2, m3]
        en = pick(rt, [m1, m2, m3], V, G)
        yield from calm(en, [m1, m2, m3])
        m = tt(en, rt, rt, ru, ALU.add, m1, m2, m3)
        en = pick(rt, m, V, S)
        yield from calm(en, m)
        a1 = cp(en, ex[:, h0:h1, 0, :], rt, m, fr.get(("ex", s)))
        en = pick(rt, a1, V, G)
        yield from calm(en, a1)
        m = tt(en, ru, rt, ex[:, h0:h1, 0, :], ALU.subtract, m, a1)
        en = pick(rt, m, V, S)
        yield from calm(en, m)
        a2 = cp(en, ex[:, h0:h1, 1, :], ru, m, fr.get(("ex", s)))
        en = pick(rt, a2, side, V)
        yield from calm(en, a2)
        m = tt(en, rt, ru, ex[:, h0:h1, 1, :], ALU.subtract, m, a2)
        done = [a1, a2, m]
        if h0 == 0:
            o = ex[:, 0:4, 2:6, :].rearrange("p h (r s) d -> p h r s d", r=2)
            done.append(cp(pick(o, a2, V, S), o, ex[:, 0:4, 0:2, :].unsqueeze(2).to_broadcast([128, 4, 2, 2, 16]), a1, a2))
        if h1 > 4:
            o = ex[:, q0:h1, 6:8, :]
            done.append(cp(pick(o, a2, V, S), o, ex[:, q0:h1, 0:2, :], a1, a2))
        en = pick(rt, m, V, S)
        yield from calm(en, m)
        if h0 == 0:
            o = ex[:, 0:4, 6:8, :]
            done.append(cp(pick(o, m, V, S), o, rt[:, 0:4, :].unsqueeze(2).to_broadcast([128, 4, 2, 16]), m))
        if h1 > 4:
            a3 = cp(pick(o, m, V, S), ex[:, q0:h1, 2, :], rt[:, q0 - h0:, :], m)
            o = ex[:, q0:h1, 3:6, :]
            en = pick(o, a3, V, S)
            yield from calm(en, a3)
            done += [a3, cp(en, o, ex[:, q0:h1, 0:3, :], a1, a2, a3)]
        fr["rt", s] = done
        cuts = [c for c in (0, 4, 8, 12, 16, 20) if h0 <= c <= h1 and (c not in (8, 16) or c in (h0, h1))]
        for g0, g1 in zip(cuts, cuts[1:]):
            while m_id is None:
                yield
            yield from calm(PE, done)
            if g0:
                while ch > 1 and ch - 2 not in qt_free:
                    yield
            k = yield from grab(bk, calm)
            kb = k.ap.bitcast(BF16).rearrange("p (h n) -> p h n", n=128)
            for h in range(g0, g1):
                m = tr(kb[:, h - g0, :], ex[:, h, :, :].rearrange("p s d -> p (s d)"), IDB[:, :], done, m_id, k.free)
            o = QT[ch % 2][:, g0 - 4:g1 - 4, 128 * tc:128 * tc + 128] if g0 else KT[b][:, :, 128 * t:128 * t + 128]
            en = pick(o, m, V, S)
            yield from calm(en, m)
            if g0:
                m2 = cp(en, o, kb[:, 0:g1 - g0, :], m, qt_free.get(ch - 2))
                for g in range(g0 // 4 - 1, g1 // 4 - 1):
                    qt_ok[i, g] = m2
            else:
                m2 = cp(en, o, kb[:, 0:4, :], m)
                kt_ok[i] = m2
            k.leave(m2)
        fr["ex", s] = m

    exp_m, pv_m, s_m = {}, {}, {}
    enc_ok = {}
    units = [(0, g, kt, hf) for k0 in (0, 4) for g in range(NKV) for kt in range(k0, k0 + 4) for hf in range(2)]
    units += [(ch, g, kt, hf) for ch in range(1, 4) for g in range(NKV) for kt in range(8) for hf in range(2)]

    def scores(n):
        ch, g, kt, hf = units[n]
        b = ch // 2
        u = unit[n % 2]
        need(lambda: ready(n))
        w = [kt_ok[8 * b + kt]] + [qt_ok[4 * ch + i, g] for i in range(4)]
        for j in range(2):
            s_m[n] = mm(u.ap[:, 512 * j:512 * j + 512], KT[b][:, g, 128 * kt:128 * kt + 128],
                        QT[ch % 2][:, 4 * g + 2 * hf + j, :], True, True, w, exp_m.get(n - 2), *([bk.free for bk in bank[0:4]] if n < 2 else []))
        if n % 64 == 63:
            qt_free[ch] = s_m[n]

    def exponent(n):
        exp_m[n] = act(PB[n % NP][:, :], unit[n % 2].ap, ACT.Exp, s_m[n], pv_m.get(n - NP), scale=0.25)
        turn[1] = S.at

    def values(n, c0, c1):
        ch, g, kt, _ = units[n]
        b = ch // 2
        first, last = (kt % 4 == 0, kt % 4 == 3) if ch == 0 else (kt == 0, kt == 7)
        if first and c0 == 0:
            pv_bank[ch, g] = pvb()
            need(lambda: not pv_bank[ch, g].taken)
            pv_bank[ch, g].taken = True
        k = pv_bank[ch, g]
        for j in range(4):
            m = mm(k.ap[32 * j:32 * j + 32, c0:c1], VS[b][:, kt, g, :],
                   PB[(n + j // 2) % NP][:, 512 * (j % 2) + c0:512 * (j % 2) + c1],
                   first and c0 == 0, last and c1 == 512, exp_m[n], exp_m[n + 1], vs_ok[8 * b + kt], k.free,
                   ns=1.68 * (c1 - c0) if j == 3 else 27.0)
        if c1 == 512:
            pv_m[n] = pv_m[n + 1] = m
            if last and kt == 3:
                norms.append(lambda lane: keep(g, m))
            elif last:
                norms.append(lambda lane: normalise(ch, g, m))

    pv_bank, enc_used, half_ok, pair_ok = {}, [], {}, {}

    def keep(g, m):
        k = pv_bank[0, g]
        yield from calm(V, m)
        half_ok[g] = vtr(HALF[:, g, :], k.ap, m)
        k.leave(half_ok[g])

    def normalise(ch, g, m):
        k, p = pv_bank[ch, g], g % 2
        yield from calm(V, m)
        m = vtr(ET[p][:, :, :].rearrange("p a b -> p (a b)"), k.ap, m, fr.get(("et", p)))
        k.leave(m)
        yield
        if ch == 0:
            v = ET[p][:, :, :].rearrange("p a b -> p (a b)")
            m = tt(V, v, v, HALF[:, g, :], ALU.add, m, half_ok[g])
            yield
        m = rcp(ERC[:, :, :], ET[p][:, :, 16:17], m, fr.get("em"))
        m = tt(V, EM[:, :, :], ET[p][:, :, 0:16], ERC[:, :, :].to_broadcast([128, 16, 16]), ALU.mult, m)
        fr["et", p] = m
        yield
        h = cp(V, EHR[:, :, :], EM[:, :, :], m, fr.get("ehr"))
        m = tt(V, EL[:, :, 16 * p:16 * p + 16], EM[:, :, :], f32(EHR[:, :, :]), ALU.subtract, h, fr.get("el"))
        h = cp(V, EU[:, :, 16 * p:16 * p + 16], f32(EHR[:, :, :]), h, fr.get("eu"))
        fr["em"], fr["ehr"] = m, [m, h]
        pair_ok[g] = [m, h]
        if p == 0:
            return
        yield
        done = []
        for key, src, q in (("el", EL, 1), ("eu", EU, 0)):
            et = ET[q][:, :, :].rearrange("p a b -> p (a b)")
            m = fr[key] = vtr(et, src[:, :, :].rearrange("p a b -> p (a b)"), pair_ok[g - 1], pair_ok[g], fr["et", q])
            yield
            while ch and ch - 1 not in enc_used:
                yield
            m = fr["et", q] = cp(V, ENC[:, g // 2, q, :], et, m, fr.get("enc"))
            done.append(m)
        enc_ok[ch, g // 2] = done

    class Lane:

        def __init__(self, s, tasks):
            self.s, self.tasks, self.now = s, tasks, None

        def step(self):
            if self.now is None and self.tasks:
                self.now = self.tasks.pop(0)(self)
            if self.now is not None and next(self.now, "end") == "end":
                self.now = None

    tasks, posts, norms = [], [], []
    lanes = [Lane(None, norms), Lane(None, posts)] + [Lane(i, tasks) for i in range(4)]
    turn = [0.0, 0.0]
    BURST = (500.0, 500.0)
    side = bank[6:8]

    def step():
        turn[0] = PE.at
        for l in lanes:
            l.step()

    def need(ready):
        left = 4000
        while not ready():
            left -= 1
            assert left
            t = PE.at
            turn[1] = S.at
            step()
            PE.at = max(PE.at, t + 200.0)
            S.at = max(S.at, PE.at - 500.0)

    def idle():
        return not tasks and not posts and not norms and all(l.now is None for l in lanes)

    def soonest(en, m):
        yield max(latest(m), en.at)

    def calm(en, m):
        while latest(m) > (en.at if en is S else max(en.at, PE.at)) or en is PE and PE.at > turn[0] + BURST[0] or en is S and S.at > turn[1] + BURST[1]:
            yield

    def given(o, m, en, *others):
        return en

    def whichever(o, m, *engines):
        return min(engines, key=lambda en: max(en.at, latest(m)) + cost(en, o, o, o) + en.lat)

    def start_tile(i):
        return tile(i, i, bank[2 * i:2 * i + 2], 8, soonest, S, whichever)

    def keys_of(i):
        return lambda lane: tile(i, lane.s, side, 4, calm, V, given)

    def rest_of(i, h0):
        return lambda lane: rope(i, lane.s, side, h0, 20, calm, given)

    WARM = 6800.0
    m_one = ms(V, ONE[:, :], 1.0)

    def warm(until):
        while True:
            ns = 427.0 if PE.at < WARM else 216.0
            k = [k for k in bank if not k.taken and latest(k.free) <= PE.at]
            if not k or PE.at + ns > until:
                return
            mm(k[-1].ap, ONE[:, :], ONE[:, :].unsqueeze(1).to_broadcast([128, 4, 128]), True, True, m_one, k[-1].free, ns=ns)

    PE.at = 1000.0
    m_id = m_wqh = m_wq = None
    n_e, n_s, n_v = 4, 6, 0
    BLOCKED, OVER = 8e8, 9e8

    def ready(n):
        ch, g, kt, _ = units[n]
        return 8 * (ch // 2) + kt in kt_ok and all((4 * ch + i, g) in qt_ok for i in range(4))

    def weights():
        nonlocal m_wqh, m_wq
        yield from soonest(S, d_wq)
        m_wqh = cp(S, WQH[:, :, :], WQR, d_wq)
        m_wq = []
        for c in range(2):
            en = whichever(WQL[:, c, :], m_wqh, V, G)
            yield from soonest(en, m_wqh)
            m_wq.append(tt(en, WQL[:, c, :], WQR[:, c, :], f32(WQH[:, c, :]), ALU.subtract, m_wqh))

    def identity():
        nonlocal m_id
        yield from soonest(V, d_c)
        m_id = cp(V, IDB[:, :], IDF, d_c)

    def more_heads(i):
        while min(at[:4]) < OVER:
            yield
        yield from rope(i, i, bank[4:8], 8, 12, soonest, whichever)

    def first_scores():
        for n in range(n_s):
            while not ready(n) or n >= 2 and n - 2 not in exp_m:
                yield
            yield from soonest(PE, [[kt_ok[units[n][2]]] + [qt_ok[i, 0] for i in range(4)], exp_m.get(n - 2)])
            for k in bank[0:4]:
                k.taken = True
            scores(n)

    def first_exponents():
        for n in range(n_e):
            while n not in s_m:
                yield
            yield from soonest(S, s_m[n])
            exponent(n)

    first = [start_tile(i) for i in range(4)] + [identity(), weights(), first_scores(), first_exponents()] + [more_heads(i) for i in range(4)]
    at = [BLOCKED] * len(first)
    go_on = lambda f: (lambda t: BLOCKED if t is None else t)(next(f, OVER))
    while min(at) < OVER:
        at = [go_on(f) if t == BLOCKED else t for f, t in zip(first, at)]
        i = at.index(min(at))
        if at[i] < BLOCKED:
            warm(at[i])
        if at[i] < BLOCKED:
            at[i] = go_on(first[i])
    start_done = [q.last() for q in (PE, V, S, G)]

    xsv = XS.rearrange("(e p r) w -> p e (r w)", e=E, p=128)
    for q in range(4):
        Y.dma(D("pf"), lambda e, q=q: e.dma_start(
            xsv[:, 15 * q:15 * q + 15, :], PF[:, :, :].rearrange("p j w -> p (j w)").unsqueeze(1).to_broadcast([128, 15, 2 * ROW])),
            m_pf2, d_x[15], d_gw)
    d_pf = Y.dma(D("pf"), lambda e: e.dma_start(
        YS.rearrange("(p r) c -> p r c", p=128),
        PF[:, 0, 0:C].unsqueeze(1).to_broadcast([128, NPAIR // 128, C])), m_pf2)

    def prepare(lane):
        nonlocal m_wo, m_gw, m_tri, m_rows
        m_wo = split(WOH[:, :, :], WOL[:, :, :], WOR, d_wo, V, V)
        yield
        m_gw = split(GW[:, :, 0, :], GW[:, :, 1, :], GWR, d_gw, V, V)
        m_tri = cp(V, TRI[:, :], CST[:, C_TRI:C_TRI + 128], d_c)
        yield
        m_mac[0] = ms(V, MAC[:, 0, :], 0.0)
        m_rows = ms(V, ROWS[:, :, :, 258:260], 0.0, m_wo, m_gw, m_wq)
        rows_free.append(m_rows)
        yield

    rows_free = []

    AHEAD, TURN, WHOLE, STOCK, SOON, HURRY = 0.0, 600.0, 4, 4, 16, 300.0

    def attention(ch, more):
        nonlocal n_e, n_s, n_v
        tasks.extend(more)
        end, beside = 64 * ch + 64, PE.at
        while n_e < end or ch == 3 and n_v < 256:
            may = n_e < min(end, n_s) and (n_e < NP or n_e - NP in pv_m)
            if may and latest(s_m[n_e]) <= max(S.at, PE.at) and S.at <= PE.at + AHEAD:
                exponent(n_e)
                n_e += 1
                continue
            late = n_s + SOON < 256 and not ready(n_s + SOON)
            if PE.at >= beside + (TURN if not late else HURRY):
                beside = PE.at
                step()
            v = n_v // 2 * 2
            t_s = latest(exp_m[n_s - 2]) if n_s < 256 and n_s - 2 in exp_m and ready(n_s) else 1e9
            t_v = latest(exp_m[v], exp_m[v + 1]) if v + 1 in exp_m else 1e9
            if min(t_s, t_v) > PE.at or t_s > PE.at and n_e - n_v < STOCK:
                beside = PE.at
                step()
                if PE.at > beside:
                    continue
            if t_s <= max(PE.at, t_v) and t_s < 1e9:
                scores(n_s)
                n_s += 1
            elif t_v < 1e9:
                whole = n_v % 2 == 0 and n_e - n_v >= WHOLE
                values(v, 256 * (n_v % 2), 512 if whole else 256 * (n_v % 2) + 256)
                n_v += 2 if whole else 1
            elif may:
                exponent(n_e)
                n_e += 1
            else:
                turn[1] = S.at
                PE.at += 200.0
                S.at = max(S.at, PE.at - 500.0)

    attention(0, [rest_of(i, 12) for i in range(4)] + [keys_of(i) for i in range(4, 8)] + [rest_of(i, 4) for i in range(4, 8)]
              + [prepare] + [keys_of(i) for i in range(8, 12)])

    IOTA = CST[:, C_IOTA:C_IOTA + E]
    DID = CST[:, C_DID:C_DID + NT * TOPK].rearrange("p (t k) -> p t k", k=TOPK)
    x1_ok, sig_ok, xt_ok = {}, {}, {}

    def post(ch, bk, e1, quiet, calm, brief):
        while not all((ch, g) in enc_ok for g in range(2)):
            yield
        w, rows, pw = [enc_ok[ch, g] for g in range(2)], {}, {}
        yield from calm(PE, [w, m_wo])
        for tc in range(4):
            i, n, k = 4 * ch + tc, 0, (yield from grab(bk, calm))
            for l, r in ((0, WOH), (0, WOL), (1, WOH)):
                for g in range(2):
                    mk = mm(k.ap[:, 0:256], ENC[:, g, l, 128 * tc:128 * tc + 128], r[:, g, :], n == 0, n == 5, w, m_wo, k.free)
                    n += 1
                yield
            m = tt(V, X[:, i, :], X[:, i, :], k.ap[:, 0:256], ALU.add, mk)
            k.leave(m)
            pw[tc] = ln(X[:, i, :], SP[tc], ("sp", tc), m)
            yield
        fr["enc"] = mk
        enc_used.append(ch)
        while ch and ch - 1 not in sc_ok:
            yield
        for tc in range(4):
            yield from calm(V, pw[tc])
            copies = TOPK if e1 is V else 1
            rows[tc] = ts2(V, ROWS[:, tc, 0:copies, 0:C], X[:, 4 * ch + tc:4 * ch + tc + 1, :].to_broadcast([128, copies, C]),
                           SP[tc][:, 6:7], SP[tc][:, 8:9], ALU.subtract, ALU.mult, pw[tc], rows_free)
            fr["sp", tc] = rows[tc]
            row_ok[ch, tc] = rows[tc]
            yield
        while any(l.now for l in quiet):
            yield
        xt_free = [q.last() for q in (PE, V, S, G)] if quiet else []
        for tc in range(4):
            yield from calm(PE, rows[tc])
            k, m = (yield from grab(bk, calm)), rows[tc]
            tr(k.ap[:, 0:128], ROWS[:, tc, 0, 0:128], IDF, m, k.free)
            m = tr(k.ap[:, 128:256], ROWS[:, tc, 0, 128:256], IDF)
            yield from calm(e1, m)
            kv = k.ap[:, 0:256].rearrange("p (c n) -> p c n", c=2)
            th, tl = XTH[:, ch, :, 128 * tc:128 * tc + 128], XTL[:, ch, :, 128 * tc:128 * tc + 128]
            h = cp(e1, th, kv, m, *xt_free)
            yield from brief(V, h)
            m = tt(V, tl, kv, f32(th), ALU.subtract, h, *xt_free)
            k.leave(m)
        yield from calm(PE, m)
        xt_ok[ch] = m
        k, n = (yield from grab(bk, calm)), 0
        for r in (XTH, XTL):
            for c in range(2):
                mk = mm(k.ap, GW[:, c, :, :].rearrange("p s e -> p (s e)"), r[:, ch, c, :], n == 0, n == 3, m, m_gw, k.free)
                n += 1
            yield
        yield from brief(e1, mk)
        m = cp(e1, GL[:, :], k.ap, mk, fr.get("gl"))
        k.leave(m)
        yield from calm(PE, m)
        k = yield from grab(bk, calm)
        for t in range(4):
            mk = tr(k.ap[:, 128 * t:128 * t + 128], GL[:, 128 * t:128 * t + 128], IDF, m, k.free)
        fr["gl"] = mk
        yield
        yield from brief(V, mk)
        m = red(LG[:, :, :], k.ap.rearrange("p (t s e) -> p t e s", t=4, s=2), mk, fr.get("lg"))
        k.leave(m)
        yield from brief(V, m)
        for t in range(4):
            m1 = V(lambda e, t=t: e.max(MX[:, t, :], LG[:, t, 0:E]), m, fr.get("mx"))
        for t in range(4):
            m2 = V(lambda e, t=t: e.max_index(MI[:, t, :], MX[:, t, :], LG[:, t, 0:E]), m1, fr.get("mi"))
        g1 = tt(V, GX[:, :, 0:E], LG[:, :, 0:E], MX[:, :, 0:1].to_broadcast([128, 4, E]), ALU.subtract, m1, fr.get("gx"))
        g2 = tt(V, GX[:, :, E:E + 4], MX[:, :, 0:4], MX[:, :, 0:1].to_broadcast([128, 4, 4]), ALU.subtract, m1, fr.get("gx"))
        g3 = ts(V, GX[:, :, E + 4:E + 5], LG[:, :, E:E + 1], -1.0, ALU.mult, m, fr.get("gx"))
        fr["lg"] = [m2, g1, g3]
        mfv = EXF[:, 4 * ch:4 * ch + 4, :]
        mf = cp(V, mfv, MI[:, :, 0:TOPK], m2)
        fr["mx"], fr["mi"] = [m2, g2], mf
        mo = tt(V, OH[:, :, :, :], IOTA.unsqueeze(1).unsqueeze(1).to_broadcast([128, 4, TOPK, E]),
                mfv.unsqueeze(3).to_broadcast([128, 4, TOPK, E]), ALU.is_equal, mf, fr.get("oh"))
        yield from calm(S, [g1, g2, g3])
        ex = act(GX[:, :, :], GX[:, :, :], ACT.Exp, g1, g2, g3)
        mb = count(MB[:, :, :], OH[:, :, :, :].rearrange("p t k e -> p t e k"), mo, fr.get("mb"))
        yield from calm(PE, mb)
        k = yield from grab(bk, calm)
        for t in range(4):
            o = k.ap[:, 64 * t:64 * t + E]
            mk = mm(o, TRI[:, :], MB[:, t, :], True, False, mb, m_tri, k.free)
            for s_ in range(t):
                mk = mm(o, ONE[:, :], MB[:, s_, :], False, False, m_one)
            mk = mm(o, ONE[:, :], MAC[:, ch, :], False, True, m_mac[ch], m_one)
        m = red(MS[:, :], MB[:, :, :].rearrange("p t e -> p e t"), mb, fr.get("ms"))
        m_mac.append(tt(V, MAC[:, (ch + 1) % 4, :], MAC[:, ch, :], MS[:, :], ALU.add, m, mk if ch == 3 else None))
        fr["ms"], fr["mb"] = m_mac[-1], [m, mk]
        if ch == 3:
            yield from calm(PE, m_mac[-1])
            mc = mm(k.ap[:, 256:256 + E], ONE[:, :], MAC[:, 0, :], True, True, m_mac[-1], m_one)
            m = cp(V, CNF[:, 0:E], k.ap[:, 256:256 + E], mc)
            mc = cp(V, CNT[:, 0:E], CNF[:, 0:E], m)
            m = stt(KEY[:, 0:E], CNF[:, 0:E], 64.0, IOTA, ALU.mult, ALU.subtract, m)
            m1 = tt(V, KEG[0:E, 0:E], KEY[0:E, 0:E], CST[0:E, C_ID:C_ID + E], ALU.mult, m)
            m1 = red(KES[0:E, 0:1], KEG[0:E, 0:E], m1)
            m = ts(V, KEG[0:E, 0:E], KEY[0:E, 0:E], KES[0:E, 0:1], ALU.is_gt, m1)
            m = red(KES[0:E, 1:2], KEG[0:E, 0:E], m)
            m1 = ts(V, KEG[0:E, 0:E], CST[0:E, C_PLACE:C_PLACE + E], KES[0:E, 1:2], ALU.is_equal, m)
            m2 = tt(V, KEY[0:E, 0:E], KEG[0:E, 0:E], CST[0:E, C_CAP:C_CAP + E], ALU.mult, m1)
            m2 = red(KES[0:E, 2:3], KEY[0:E, 0:E], m2)
            m2 = tt(V, KES[0:E, 3:4], KES[0:E, 0:1], KES[0:E, 2:3], ALU.is_gt, m2)
            yield from calm(PE, m2)
            mm(k.ap[0:1, 320:320 + E], CST[0:E, C_ROW:C_ROW + 1], KEG[0:E, 0:E], True, True, m1)
            m = mm(k.ap[0:1, 320 + E:321 + E], KES[0:E, 3:4], CST[0:E, C_ONE:C_ONE + 1], True, True, m2)
            sp_ok.append(cp(V, ORD[0:1, 0:E + 1], k.ap[0:1, 320:321 + E], m))
        yield
        kr = k.ap[:, 0:256].rearrange("p (t e) -> p t e", t=4)[:, :, 0:E]
        m = tt(V, PR[:, :, :, :], OH[:, :, :, :], kr.unsqueeze(2).to_broadcast([128, 4, TOPK, E]), ALU.mult, mk, fr.get("pr"))
        fr["oh"] = m
        k.leave(m)
        yield from brief(V, m)
        rk = RKF[:, 4 * ch:4 * ch + 4, :]
        m = red(rk, PR[:, :, :, :], m)
        fr["pr"] = m
        yield from brief(V, m)
        m1 = ts2(V, SLF[:, :, :], rk, float(SLOTS), float(AWAY), ALU.is_ge, ALU.mult, m, fr.get("slf"))
        yield from brief(V, m1)
        m1 = tt(V, SLF[:, :, :], SLF[:, :, :], rk, ALU.add, m1)
        yield from brief(V, m1)
        m1 = stt(SLF[:, :, :], mfv, float(SLOTS), SLF[:, :, :], ALU.mult, ALU.add, m1)
        yield from brief(V, m1)
        sl = SLI[ch % 2]
        ms_ = cp(V, sl[:, :], SLF[:, :, :].rearrange("p t k -> p (t k)"), m1, fr.get(("sli", ch % 2)))
        fr["slf"] = ms_
        m = red(DEN[:, 0, :], GX[:, :, 0:E], ex, fr.get("den"))
        m2 = ts(V, DEN[:, 1, :], GX[:, :, E + 4], 1.0, ALU.add, ex, fr.get("den"))
        yield from brief(V, m2)
        m = rcp(DEN[:, :, :], DEN[:, :, :], m, m2)
        yield from brief(V, m)
        m3 = cp(V, SIG[:, 4 * ch:4 * ch + 4], DEN[:, 1, :], m)
        sig_ok[ch] = m3
        wk = WKF[:, 4 * ch:4 * ch + 4, :]
        m1 = tt(V, wk, GX[:, :, E:E + 4], DEN[:, 0, :].unsqueeze(2).to_broadcast([128, 4, TOPK]), ALU.mult, m)
        fr["gx"], fr["den"] = m1, [m1, m3]
        yield from brief(V, m1)
        m1 = cp(V, ROWS[:, :, :, C + 1], wk, m1, rows_free)
        m2 = cp(V, ROWS[:, :, :, C], DID[:, 4 * ch:4 * ch + 4, :], d_c, rows_free)
        yield
        for t in range(4):
            while e1 is S and t not in copied:
                yield
            for q in range(TOPK):
                o = SLI[ch % 2][:, TOPK * t + q:TOPK * t + q + 1]
                src = ROWS[:, t, q, :]
                ms2 = G.dma(D("sc"), lambda e, o=o, src=src: e.indirect_dma_start(
                    XS[:, :], bass.IndirectOffsetOnAxis(ap=o, axis=0), src, None,
                    bounds_check=E * SLOTS - 1, oob_is_err=False), ms_, m1, m2, copied.get(t), d_pf, ns=1040.0, size=128 * ROW * 4)
                yield
        fr["sli", ch % 2] = ms2
        tk = Y.dma(D("tok"), lambda e: e.dma_start(
            TOK.rearrange("(n p) c -> p n c", p=128)[:, 4 * ch:4 * ch + 4, :], ROWS[:, :, 0, 0:C]), [rows[tc] for tc in range(4)])
        rows_free[:] = [ms2, tk]
        toks.append(tk)
        sc_ok[ch] = ms2

    sc_ok, sp_ok, toks, row_ok, copied = {}, [], [], {}, {}

    def copy_rows(ch):
        for t in range(4):
            while (ch, t) not in row_ok:
                yield None
            o, i = ROWS[:, t, 1:TOPK, 0:C], ROWS[:, t, 0:1, 0:C].to_broadcast([128, TOPK - 1, C])
            en = yield from any_of(o, o, [row_ok[ch, t]], S, G)
            copied[t] = cp(en, o, i, row_ok[ch, t])

    def post_of(ch, quiet=(), e1=V, banks=side):
        return lambda lane: post(ch, banks, e1, quiet, calm, lambda en, m: ())

    ov = out.rearrange("(n p) c -> p n c", p=128)
    fence = lambda: [q.last() for q in (PE, V, S, G)] + [(dctr[n], dctr[n].n) for n in ("sc", "tok", "pf")]
    for l in lanes[4:6]:
        l.tasks = []
    posts.append(post_of(0, lanes[4:6]))
    attention(1, [rest_of(i, 4) for i in range(8, 12)] + [keys_of(i) for i in range(12, 16)])
    posts.append(post_of(1))
    attention(2, [rest_of(i, 4) for i in range(12, 16)])
    posts.append(post_of(2, lanes[2:4]))

    W1 = Region(nc, a0, a1)
    S1H, S1L = W1("S1H", [128, 2, 2 * ISH], F32R), W1("S1L", [128, 2, 2 * ISH], F32R)
    S2H, S2L = W1("S2H", [128, 6, C], F32R), W1("S2L", [128, 6, C], F32R)
    W1b = Region(nc, W1.at, a1)
    SRW = W1b("SRW", [128, 6 * C], F32)
    SSG = [W1(f"SSG{i}", [128, 256], F32) for i in range(2)]
    SHF = [W1(f"SHF{i}", [128, 256], F32) for i in range(2)]
    W1c = Region(nc, pf0, r1_)
    SHH = [(W1 if i < 3 else W1c)(f"SHH{i}", [128, 256], F32R) for i in range(4)]
    SHL = [(W1 if i < 3 else W1c)(f"SHL{i}", [128, 256], F32R) for i in range(4)]
    W3 = Region(nc, a1, top)
    STT = W3("STT", [128, 256], F32R)
    sh_w = []

    def shared_weights(lane):
        w = [q.last() for q in (PE, V, S, G)]
        v1, v2 = wsh1.rearrange("(c p) n -> c p n", p=128), wsh2.rearrange("(f p) n -> p f n", p=128)
        m = w
        for c in range(3):
            if c < 2:
                src, dst, n, hi, lo = v1[c], SRW[:, 0:2 * ISH], 2 * ISH, S1H[:, c, :], S1L[:, c, :]
            else:
                src, dst, n = v2, SRW[:, :].rearrange("p (f n) -> p f n", f=6), 6 * C
                hi, lo = (t[:, :, :].rearrange("p f n -> p (f n)") for t in (S2H, S2L))
            d = Y.dma(D("sw"), lambda e, src=src, dst=dst: e.dma_start(dst, src), m, size=128 * n * 4)
            m = []
            for c0 in range(0, n, n // 2):
                sl = slice(c0, c0 + n // 2)
                yield from calm(V, d)
                h = cp(V, hi[:, sl], SRW[:, sl], d, w)
                yield from calm(G, h)
                m.append(tt(G, lo[:, sl], SRW[:, sl], f32(hi[:, sl]), ALU.subtract, h, w))
                yield
        sh_w.extend(m)

    lanes[2].tasks = [shared_weights]
    attention(3, [])
    att_done = [q.last() for q in (PE, V, S)]
    for k in bank[0:4]:
        k.free, k.taken = [exp_m[254], exp_m[255]], False

    jobs, extra = plan()
    JOBS = len(jobs)
    assert sorted(n for g, _ in jobs for n in g) == list(range(E))
    where = {n: (i, j) for i, (g, _) in enumerate(jobs) for j, n in enumerate(g)}
    begins, ends = {i: q for q, (_, i, _) in enumerate(extra)}, {i: q for q, (_, _, i) in enumerate(extra)}
    shares = {i: q for q, (_, i0, i1) in enumerate(extra) for i in range(i0, i1 + 1)}

    W5, W6, W7 = Region(nc, r0, pf0), Region(nc, xt0, xt0 + 8192), Region(nc, xt0 + 16384, xt0 + 24576)
    w3 = W3.at
    NW, NX, NY, NH_, N2 = 5, 5, 6, 3, 2
    WR = [W3(f"WR{i}", [128, 2, WPK + C], F32) for i in range(NW)]
    XB = [W3(f"XB{i}", [128, 2, ROW], F32) for i in range(NX)]
    XC = [W3(f"XC{i}", [128, ROW], F32) for i in range(3)]
    YI = [W3(f"YI{i}", [128, 2], I32) for i in range(NY)]
    YW = [W3(f"YW{i}", [128, 2], F32) for i in range(NY)]
    YJ = [W3(f"YJ{i}", [128, 1], I32) for i in range(3)]
    YV = [W3(f"YV{i}", [128, 1], F32) for i in range(3)]
    XT = [W3(f"XT{i}", [128, 2, 384], F32) for i in range(3)]
    HX = [W3(f"HX{i}", [IA, 2, 384], F32) for i in range(NH_)]
    W2H = [W6(f"W2H{i}", [128, 2, 2, C], F32R) for i in range(N2)]
    W2L = [W7(f"W2L{i}", [IA, 2, C], F32R) for i in range(N2)]
    HMH = [W7(f"HMH{i}", [IA, 2, 128], F32R) for i in range(2)]
    HML = [W7(f"HML{i}", [IA, 2, 128], F32R) for i in range(2)]
    assert W3.at <= sli0
    SGE = [W5(f"SGE{i}", [IA, 2, 384], F32) for i in range(2)]
    HTT = [W5(f"HTT{i}", [128, 2, 128], F32R) for i in range(2)]
    HTL = [W5(f"HTL{i}", [IB, 2, 128], F32R) for i in range(2)]
    YB = [W5(f"YB{i}", [128, 2, C], F32) for i in range(2)]
    YC = [W5(f"YC{i}", [128, C], F32) for i in range(2)]
    gb, ub, tb, xab, xcb, ya, yb = bank[0], bank[1], bank[2], bank[3], bank[4], bank[6], bank[7]
    mk_, expert = {}, {}

    def tile_rows(i):
        return min(128, ROWS_AT[jobs[i][0][0]])

    def mains(t, i):
        g, w = jobs[i]
        return t[:, 0:2 * w].rearrange("p (j n) -> p j n", j=2)[:, :, 0:tile_rows(i)]

    def computed(t, i):
        g, w = jobs[i]
        return t[:, 0:2 * w].rearrange("p (j n) -> p j n", j=2)[:, :, 0:ROWS_AT[g[0]]] if len(g) == 2 else t[:, 0:ROWS_AT[g[0]]]

    def begun():
        return [att_done, list(sc_ok.values()), toks, x1_ok[7]] if len(sc_ok) == 4 and 7 in x1_ok else None

    def after(*keys):
        keys = [k for k in keys if k[1] is not None]
        while any(k not in mk_ if k[1] >= 0 else not begun() for k in keys):
            yield None
        return [mk_[k] if k[1] >= 0 else begun() for k in keys]

    def one(en, *marks):
        yield [(en, 0.0)], list(marks)

    def any_of(o, i, marks, *engines):
        return (yield [(en, cost(en, o, i)) for en in engines], list(marks)) or engines[0]

    places = [n for g, _ in jobs for n in g]

    def number(*group):
        while any(n not in expert for n in group):
            k = len(expert)
            names = places[k:k + BATCH]
            expert.update((n, None) for n in names)

            def do(e, k=k, names=names):
                _, values = nc.values_load_multi_w_load_instructions(ORD[0:1, k:k + len(names)], engines=[e.engine], min_val=0, max_val=E - 1)
                expert.update(zip(names, values))
            Y.wait(sp_ok)
            Y.prog.append(do)
            Y.at += 250.0 * len(names)

    def loads_w(i):
        b, k = i % NW, i - NW
        while not sp_ok:
            yield None
        f = (yield from after(("up", k), ("w2", k), ("y3", shares.get(k)))) if k >= 0 else att_done
        yield from one(Y, f)
        number(*jobs[i][0])
        for j, n in enumerate(jobs[i][0]):
            Y.dma(D(f"w{b}"), lambda q, j=j, n=n: q.dma_start(
                WR[b][:, j, 0:WPK], wpk[bass.ds(expert[n], 1)].rearrange("e p n -> (e p) n")), f, ns=560.0, size=128 * WPK * 4)
            m = Y.dma(D(f"w{b}"), lambda q, j=j, n=n: q.dma_start(
                WR[b][0:IB, j, WPK:], wtl[bass.ds(expert[n], 1)].rearrange("e p n -> (e p) n")), f, ns=740.0, size=IB * C * 4)
            yield from one(Y)
        mk_["w", i] = m
        if i + 1 == NW:
            number(*places[0:FIRST])

    def loads_x(i):
        b, k, (g, _), rt = i % NX, i - NX, jobs[i], tile_rows(i)
        while len(sc_ok) < 4:
            yield None
        f = (yield from after(("yi", k), ("xt", k))) if k >= 0 else att_done
        number(*g)
        yield from one(Y, f)
        for j in range(2):
            n, r = (g[j], 0) if len(g) == 2 else (g[0], 128 * j)
            m = Y.dma(D(f"xe{b}"), lambda q, j=j, n=n, r=r: q.dma_start(
                XB[b][0:rt, j, :], XS[bass.ds(expert[n] * SLOTS + r, rt), :]), f, list(sc_ok.values()), ns=560.0, size=rt * ROW * 4)
        mk_["x", i] = m
        if i in begins:
            q3 = begins[i]
            f = (yield from after(("xt3", q3 - 3), ("yj", q3 - 3))) if q3 >= 3 else att_done
            yield from one(Y, f)
            number(*[n for n, _, _ in extra[q3][0]])
            for j, (n, r, k) in enumerate(extra[q3][0]):
                m = Y.dma(D(f"xc{q3 % 3}"), lambda q, j=j, n=n, r=r, k=k: q.dma_start(
                    XC[q3 % 3][k * j:k * j + k, :], XS[bass.ds(expert[n] * SLOTS + r, k), :]), f, list(sc_ok.values()), ns=740.0 if k == 64 else 580.0, size=k * ROW * 4)
            mk_["x3", q3] = m

    def turned(i):
        b, p, (g, r), rt = i % NX, i % 3, jobs[i], tile_rows(i)
        x, f = yield from after(("x", i), ("up", i - 3))
        while xab.taken:
            yield None
        xab.taken = True
        yield from one(PE, x, xab.free)
        for j in range(2):
            for c in range(2):
                m = tr(xab.ap[:, 256 * c + 128 * j:256 * c + 128 * j + rt], XB[b][0:rt, j, 128 * c:128 * c + 128], IDF[0:rt, 0:rt], x, xab.free)
        mk_["xt", i] = m
        o = XT[p][:, :, 0:2 * r].rearrange("p c (j n) -> p c j n", j=2)[:, :, :, 0:rt]
        v = xab.ap.rearrange("p (c j n) -> p c j n", c=2, j=2)[:, :, :, 0:rt]
        en = yield from any_of(o, v, [m, f], S, V)
        m = cp(en, o, v, m, f)
        xab.leave(m)
        done = [m]
        m = yield from after(("out", i - NY), ("give", i - NY))
        yield from one(V, x, m)
        mk_["yi", i] = [cp(V, YI[i % NY][0:rt, :], XB[b][0:rt, :, C], x, m), cp(V, YW[i % NY][0:rt, :], XB[b][0:rt, :, C + 1], x, m)]
        if i in begins:
            q3 = begins[i]
            last = extra[q3][2]
            xc, src = XC[q3 % 3], xcb.ap[:, 0:256].rearrange("p (c j n) -> p c j n", c=2, n=r - 128)
            w = yield from after(("x3", q3), ("up", last - 3))
            while xcb.taken:
                yield None
            xcb.taken = True
            yield from one(PE, w[0], xcb.free)
            for c in range(2):
                m = tr(xcb.ap[:, 128 * c:128 * c + 128], xc[:, 128 * c:128 * c + 128], IDF, w[0], xcb.free)
            mk_["xt3", q3] = m
            left = []
            for i_ in range(i, last + 1):
                o = XT[i_ % 3][:, :, 0:2 * r].rearrange("p c (j n) -> p c j n", j=2)[:, :, :, 128:r]
                v = src[:, :, 2 * (i_ - i):2 * (i_ - i) + 2, :]
                if i_ == i:
                    en = yield from any_of(o, v, [m, w], S, V)
                left.append(cp(en, o, v, m, w))
                mk_["xe", i_] = left[-1]
            xcb.leave(*left)
            m = yield from after(("out3", q3 - 3), ("give3", q3 - 3))
            yield from one(V, w[0], m)
            mk_["yj", q3] = [cp(V, YJ[q3 % 3][:, :], xc[:, C:C + 1], w[0], m), cp(V, YV[q3 % 3][:, :], xc[:, C + 1:C + 2], w[0], m)]
        mk_["xin", i] = done + ([mk_["xe", i]] if i in shares else [])

    def split2(i):
        p, ng = i % N2, len(jobs[i][0])
        r = WR[i % NW][:, 0:ng, 4 * I:].rearrange("p j (c n) -> p j c n", c=2)
        hi, lo = W2H[p][:, 0:ng], W2L[p][:, 0:ng]
        w, f = yield from after(("w", i), ("y", i - N2))
        en = yield from any_of(hi[0:IA, :, 0], r[0:IA, :, 0], [w, f], V, S)
        h = cp(en, hi[0:IA, :, 0], r[0:IA, :, 0], w, f)
        en = yield from any_of(hi[0:IB, :, 1], r[0:IB, :, 1], [w, f], S, V)
        g = cp(en, hi[0:IB, :, 1], r[0:IB, :, 1], w, f)
        en = yield from any_of(lo, lo, [h, f], G, V)
        m1 = tt(en, lo, r[0:IA, :, 0], f32(hi[0:IA, :, 0]), ALU.subtract, h, f)
        yield from one(V, g)
        m2 = tt(V, hi[IB:2 * IB, :, 1], r[0:IB, :, 1], f32(hi[0:IB, :, 1]), ALU.subtract, g, f)
        mk_["w2", i] = [m1, m2]

    def ups(i):
        (g, s_), w_ = jobs[i], WR[i % NW]
        r = ROWS_AT[g[0]]
        w, x = yield from after(("w", i), ("xin", i))
        for key, k, c0, n in (("g", gb, 0, IA), ("u", ub, IA, IA), ("t", tb, 2 * IA, 2 * IB)):
            while k.taken:
                yield None
            k.taken = True
            yield from one(PE, w, x, k.free)
            for j in range(len(g)):
                for c in range(2):
                    m = mm(k.ap[0:n, s_ * j:s_ * j + r], w_[:, j, 2 * I * c + c0:2 * I * c + c0 + n], XT[i % 3][:, c, s_ * j:s_ * j + r],
                           c == 0, c == 1, w, x, k.free)
            mk_[key, i] = m
        mk_["up", i] = m

    def gated(i):
        p, q = i % 2, i % NH_
        sa, sb, ha, hb = (computed(t, i) for t in (SGE[p][:, 0, :], SGE[p][0:IB, 1, :], HX[q][:, 0, :], HX[q][0:IB, 1, :]))
        m, f = yield from after(("g", i), ("he", i - 2))
        yield from one(S, m, f)
        s_ = act(sa, computed(gb.ap[0:IA, :], i), ACT.Silu, m, f)
        gb.leave(s_)
        m, *f = yield from after(("u", i), ("hl", i - NH_), ("y3", shares.get(i - NH_)))
        yield from one(V, m, s_, f)
        he = tt(V, ha, sa, computed(ub.ap[0:IA, :], i), ALU.mult, m, s_, f)
        ub.leave(he)
        m, = yield from after(("t", i))
        yield from one(S, m)
        s_ = act(sb, computed(tb.ap[0:IB, :], i), ACT.Silu, m, f)
        yield from one(V, m, s_)
        ht = tt(V, hb, sb, computed(tb.ap[IB:2 * IB, :], i), ALU.mult, s_)
        tb.leave(ht)
        mk_["he", i] = [he, ht]

    def split_h(i):
        p, q, rt = i % 2, i % NH_, tile_rows(i)
        va, vb = mains(HX[q][:, 0, :], i), mains(HX[q][0:IB, 1, :], i)
        hh, hl, th, td, tl = (t[:, :, 0:rt] for t in (HMH[p], HML[p], HTT[p][0:IB], HTT[p][IB:2 * IB], HTL[p]))
        (he, ht), f = yield from after(("he", i), ("y", i - 2))
        en = yield from any_of(hh, va, [he, f], S, V)
        h1 = cp(en, hh, va, he, f)
        en = yield from any_of(th, vb, [ht, f], S, V)
        h2 = cp(en, th, vb, ht, f)
        en = yield from any_of(td, vb, [ht, f], V, S)
        h3 = cp(en, td, vb, ht, f)
        en = yield from any_of(hl, hl, [h1, f], V, G)
        m1 = tt(en, hl, va, f32(hh), ALU.subtract, h1, f)
        en = yield from any_of(tl, tl, [h2, f], V, G)
        m2 = tt(en, tl, vb, f32(th), ALU.subtract, h2, f)
        mk_["hl", i] = [m1, m2, h3]

    def down(i):
        p, w, ng, rt = i % 2, i % N2, len(jobs[i][0]), tile_rows(i)
        m, mw = yield from after(("hl", i), ("w2", i))
        for j, k in enumerate((ya, yb)):
            while k.taken:
                yield None
            k.taken = True
            yield from one(PE, m, mw, k.free)
            o, h, l = k.ap[0:rt, 0:C], W2H[w][:, j % ng], W2L[w][:, j % ng]
            mm(o, HMH[p][:, j, 0:rt], h[0:IA, 0, :], True, False, m, mw, k.free)
            mm(o, HML[p][:, j, 0:rt], h[0:IA, 0, :], False, False)
            mm(o, HMH[p][:, j, 0:rt], l, False, False)
            mm(o, HTL[p][:, j, 0:rt], h[0:IB, 1, :], False, False)
            mk_["y" + "ab"[j], i] = y = mm(o, HTT[p][:, j, 0:rt], h[:, 1, :], False, True)
        mk_["y", i] = y
        if i in ends:
            q3 = ends[i]
            rows = extra[q3][0]
            k = xcb
            while k.taken:
                yield None
            k.taken = True
            yield from one(PE, mk_["he", i], k.free)
            for c, n_ in enumerate((IA, IB)):
                for j, (n, _, r) in enumerate(rows):
                    i_, j_ = where[n]
                    a = jobs[i_][1] * j_ + 128
                    y = mm(k.ap[r * j:r * j + r, 256:512], HX[i_ % NH_][0:n_, c, a:a + r], WR[i_ % NW][0:n_, j_, 4 * I + C * c:4 * I + C * c + C],
                           c == 0, c == 1, mk_["he", i], k.free, ns=430.0 if j + 1 == len(rows) else 20.0)
            mk_["y3", q3] = y

    def give(i):
        p, b, rt = i % 2, i % NY, tile_rows(i)
        mi, f = yield from after(("yi", i), ("out", i - 2))
        left = []
        for j, k in enumerate((ya, yb)):
            m, = yield from after(("y" + "ab"[j], i))
            en = yield from any_of(YB[p][0:rt, j, :], k.ap[0:rt, 0:C], [m, mi, f], S, V)
            left.append(scaled(en, YB[p][0:rt, j, :], k.ap[0:rt, 0:C], YW[b][0:rt, j:j + 1], m, mi, f))
            k.leave(left[j])
        mk_["give", i] = left
        if i in ends:
            q3 = ends[i]
            m, *f = yield from after(("y3", q3), ("yj", q3), ("out3", q3 - 2))
            o, v = YC[q3 % 2][:, :], xcb.ap[:, 256:512]
            en = yield from any_of(o, v, [m, f], S, V)
            m = scaled(en, o, v, YV[q3 % 3][:, :], m, f)
            xcb.leave(m)
            mk_["give3", q3] = m

    def scatter(i):
        p, b, rt = i % 2, i % NY, tile_rows(i)
        m, mi = yield from after(("give", i), ("yi", i))
        for j in range(2):
            yield from one(G, m[j], mi)
            out_ = G.dma(D(f"so{p}"), lambda q, j=j: q.indirect_dma_start(
                YS[:, :], bass.IndirectOffsetOnAxis(ap=YI[b][0:rt, j:j + 1], axis=0), YB[p][0:rt, j, :], None,
                bounds_check=NPAIR - 1, oob_is_err=False), m[j], mi, d_pf, ns=1040.0, size=rt * C * 4)
        mk_["out", i] = out_
        if i in ends:
            q3 = ends[i]
            m, mi = yield from after(("give3", q3), ("yj", q3))
            yield from one(G, m, mi)
            mk_["out3", q3] = G.dma(D(f"sox{q3 % 2}"), lambda q: q.indirect_dma_start(
                YS[:, :], bass.IndirectOffsetOnAxis(ap=YJ[q3 % 3][:, :], axis=0), YC[q3 % 2][:, :], None,
                bounds_check=NPAIR - 1, oob_is_err=False), m, mi, d_pf, ns=1040.0, size=128 * C * 4)

    LATE = 5
    steps = [(uu, f) for uu in range(8) for f in range(6)]
    early = lambda n: n < 6 * LATE
    shb, sha = ([bank[0], bank[1], ya, xcb], [bank[0], bank[1], bank[2], bank[4]]), ([bank[5], yb], [bank[5], xab])
    sh_bank = {}

    def before(n, key, depth):
        return (yield from after((key, n - depth))) if n >= depth else [att_done, sh_w, d_pf]

    def sh_up(n):
        (uu, f), banks = steps[n], shb[0 if early(n) else 1]
        ch, hf = divmod(uu, 2)
        while ch not in sig_ok or not early(n) and ("up", JOBS - 1) not in mk_:
            yield None
        while all(k.taken for k in banks):
            yield None
        k = sh_bank[n] = min((k for k in banks if not k.taken), key=lambda k: latest(k.free))
        k.taken = True
        for part in range(2 if f < 5 else 1):
            yield from one(PE, xt_ok[ch], sh_w, k.free)
            m, c0 = 0, 256 * f + 128 * part
            for l, r in ((S1H, XTH), (S1L, XTH), (S1H, XTL)):
                for c in range(2):
                    mk = mm(k.ap[:, 256 * part:256 * part + 256], l[:, c, c0:c0 + 128],
                            r[:, ch, c, 256 * hf:256 * hf + 256], m == 0, m == 5, xt_ok[ch], sh_w, k.free)
                    m += 1
        mk_["sup", n] = mk

    def sh_gated(n):
        (uu, f), p = steps[n], n % 2
        nf = 128 if f < 5 else 64
        m, = yield from after(("sup", n))
        w = yield from before(n, "sg", 2)
        yield from one(S, m, w)
        k = sh_bank[n]
        up = k.ap[:, 256:512] if f < 5 else k.ap[64:128, 0:256]
        s_ = act(SSG[p][0:nf, :], k.ap[0:nf, 0:256], ACT.Silu, m, w)
        w = yield from before(n, "slo", 2)
        yield from one(V, s_, w)
        mk_["sg", n] = tt(V, SHF[p][0:nf, :], SSG[p][0:nf, :], up, ALU.mult, s_, w)
        k.leave(mk_["sg", n])

    def sh_split(n):
        (uu, f), p, q = steps[n], n % 2, n % 4
        nf = 128 if f < 5 else 64
        hi, lo = (SHH[q][:, :], SHL[q][:, :]) if f < 5 else (STT[0:64, :], STT[64:128, :])
        m, = yield from after(("sg", n))
        w = yield from before(n, "sdn", 4 if f < 5 else 6)
        yield from one(S, m, w)
        h = cp(S, hi, SHF[p][0:nf, :], m, w)
        en = (yield from any_of(lo, lo, [h, w], V, G)) if f < 5 else V
        mk_["slo", n] = [tt(en, lo, SHF[p][0:nf, :], f32(hi), ALU.subtract, h, w)]

    def sh_down(n):
        (uu, f), q = steps[n], n % 4
        ch, hf = divmod(uu, 2)
        k = sha[0 if early(n) else 1][uu % 2]
        m, = yield from after(("slo", n))
        if f == 0:
            while k.taken:
                yield None
            k.taken = True
        yield from one(PE, m, k.free)
        for t in range(2):
            o, cs = k.ap[:, C * t:C * t + C], slice(128 * t, 128 * t + 128)
            if f < 5:
                mm(o, SHH[q][:, cs], S2H[:, f, :], f == 0 and t == 0, False, m, sh_w, k.free)
                mm(o, SHH[q][:, cs], S2L[:, f, :], False, False)
                mk = mm(o, SHL[q][:, cs], S2H[:, f, :], False, False)
            else:
                mm(o, STT[:, cs], S2H[:, f, :], False, False, m)
                mk = mm(o, STT[:, cs], S2L[:, f, :], False, t == 1)
        mk_["sdn", n] = mk
        if f == 5:
            for t in range(2):
                i = 4 * ch + 2 * hf + t
                yield from one(V, mk, sig_ok[ch])
                x1_ok[i] = stt(X[:, i, :], k.ap[:, C * t:C * t + C], SIG[:, i:i + 1], X[:, i, :], ALU.mult, ALU.add, mk, sig_ok[ch])
            k.leave(x1_ok[i - 1], x1_ok[i])

    def clear():
        f = yield from after(("he", -1))
        for t in HX:
            yield from one(V, f)
            ms(V, t[:, :, :], 0.0, f)

    W4 = Region(nc, w3, top)
    FB = [W4(f"FB{i}", [128, TOPK, C], F32) for i in range(NT)]
    FO = [W4(f"FO{i}", [128, C], F32) for i in range(NT)]
    yv = YS.rearrange("(n p k) c -> n p k c", p=128, k=TOPK)
    fb_ok, left = {}, list(range(NT))

    def fetch():
        w = yield from after(("out", JOBS - 1), ("out", JOBS - 2), ("out3", len(extra) - 1), ("out3", len(extra) - 2))
        for i in range(NT):
            yield from one(Y, w)
            fb_ok[i] = Y.dma(D(f"fb{i}"), lambda q, i=i: q.dma_start(FB[i][:, :, :], yv[i]), w, ns=560.0, size=128 * TOPK * C * 4)

    def result():
        while left:
            i = left.pop(0)
            while i not in fb_ok:
                yield None
            b, o = FB[i], FO[i][:, :]
            en = (yield [(q, cost(q, o, o, o) * 3) for q in (V, G)], [fb_ok[i]]) or V
            m = tt(en, b[:, 0:2, :], b[:, 0:2, :], b[:, 2:4, :], ALU.add, fb_ok[i])
            yield from one(en, m)
            m = tt(en, o, b[:, 0, :], b[:, 1, :], ALU.add, m)
            while i not in x1_ok:
                yield None
            yield from one(en, m, x1_ok[i])
            m = tt(en, o, o, X[:, i, :], ALU.add, m, x1_ok[i])
            yield from one(Y, m)
            Y.dma(D(f"fo{i % 8}"), lambda q, i=i, o=o: q.dma_start(ov[:, i, :], o), m, ns=560.0, size=128 * C * 4)

    def chain(part, number):
        for i in range(number):
            yield from part(i)

    def weave(threads):
        want, stuck = [next(l, "end") for l in threads], 0
        while any(w != "end" for w in want):
            if not idle():
                turn[1] = S.at
                step()
            best = None
            for n, w in enumerate(want):
                if w is None:
                    w = want[n] = next(threads[n], "end")
                if w is None or w == "end":
                    continue
                t = latest(w[1])
                en = min((max(en.at, t) + ns, k) for k, (en, ns) in enumerate(w[0]))[1]
                at = max(w[0][en][0].at, t)
                if best is None or at < best[0] - 1.0:
                    best = at, n, w[0][en][0]
            if best is None:
                stuck += 1
                assert stuck < 1000, want
                PE.at += 100.0 if not idle() else 0.0
                continue
            stuck = 0
            try:
                want[best[1]] = threads[best[1]].send(best[2])
            except StopIteration:
                want[best[1]] = "end"

    jobs_of = lambda part: chain(part, JOBS)
    steps_of = lambda part: chain(part, len(steps))
    weave([post(3, bank[2:4], S, (), one, one), jobs_of(loads_w), jobs_of(loads_x), jobs_of(scatter), jobs_of(turned), clear(),
           jobs_of(gated), jobs_of(split_h), steps_of(sh_gated), steps_of(sh_split), jobs_of(give), steps_of(sh_down), jobs_of(down),
           jobs_of(ups), steps_of(sh_up), jobs_of(split2), copy_rows(3), fetch(), result(), result(), result()])

    for c in dctr.values():
        Y.wait((c, c.n))

    with nc.Block() as block:

        @block.sync
        def _(e):
            Y.run(e)

        @block.tensor
        def _(e):
            PE.run(e)

        @block.vector
        def _(e):
            V.run(e)

        @block.scalar
        def _(e):
            S.run(e)

        @block.gpsimd
        def _(e):
            G.run(e)

    overflow(nc, wpk, wtl, TOK, YS, ov, X, CST, CNT, ORD, RKF, EXF, WKF, a0, top, PS)
    ctx.close()


def overflow(nc, wpk, wtl, TOK, YS, ov, X, CST, CNT, ORD, RKF, EXF, WKF, a0, top, PS):
    ctx = ExitStack()
    sems = [ctx.enter_context(nc.semaphore(f"o{i}")) for i in range(7)]
    every = range(sems[0].num, sems[0].num + 7)
    s_w, s_g, s_v, s_t, s_c, s_q, s_p = sems
    assert [q.num for q in sems] == list(every)
    WTS = nc.dram_tensor("wts_scratch", [NPAIR, 1], F32, kind="Internal").ap()
    IDS = nc.dram_tensor("ids_scratch", [E * IDROWS, 1], I32, kind="Internal").ap()
    M = Region(nc, a0, top)
    NONE = M("NONE", [128, E * IDROWS // 128], I32)
    OSF, OSL = M("OSF", [128, NT, TOPK], F32), M("OSL", [128, NT * TOPK], I32)
    ODI = M("ODI", [128, NT * TOPK], I32)
    OID, OTK = M("OID", [128, 1], I32), M("OTK", [128, 1], I32)
    OWT = M("OWT", [128, 1], F32)
    OW = M("OW", [128, WPK + C], F32)
    OX = M("OX", [128, C], F32)
    OXT = M("OXT", [128, C], F32)
    OSG, OH_ = M("OSG", [128, I], F32), M("OH_", [128, I], F32)
    OHT = M("OHT", [128, 2, 128], F32)
    OY = M("OY", [128, C], F32)
    OF, OO = M("OF", [128, TOPK, C], F32), M("OO", [128, C], F32)
    IDF = CST[:, C_ID:C_ID + 128]
    p0, p1, p2, p3 = (PS[i][:, 0:512] for i in range(4))

    left = nc.values_load(ORD[0:1, E:E + 1], min_val=0, max_val=E)
    everyone = (nc.sync, nc.tensor, nc.vector, nc.scalar, nc.gpsimd)
    with nc.If(left > 0):
        for e in everyone:
            e.nop()
        with nc.Block() as block:

            @block.vector
            def _(v):
                v.memset(NONE[:, :], NPAIR).then_inc(s_v, 1)
                v.scalar_tensor_tensor(OSF[:, :, :], EXF[:, :, :], float(IDROWS), RKF[:, :, :], ALU.mult, ALU.add).then_inc(s_v, 1)
                v.wait_ge(s_v, 2)
                v.tensor_copy(OSL[:, :], OSF[:, :, :].rearrange("p t k -> p (t k)")).then_inc(s_v, 1)
                v.tensor_copy(ODI[:, :], CST[:, C_DID:C_DID + NT * TOPK]).then_inc(s_v, 1)

            @block.gpsimd
            def _(g):
                g.dma_start(WTS.rearrange("(t p k) w -> p t (k w)", p=128, k=TOPK), WKF[:, :, :]).then_inc(s_q, 16)
                g.wait_ge(s_v, 4)
                g.dma_start(IDS.rearrange("(p n) w -> p (n w)", p=128), NONE[:, :]).then_inc(s_q, 16)
                g.wait_ge(s_q, 32)
                for i in range(NT * TOPK):
                    g.indirect_dma_start(IDS[:, :], bass.IndirectOffsetOnAxis(ap=OSL[:, i:i + 1], axis=0), ODI[:, i:i + 1], None,
                                         bounds_check=E * IDROWS - 1, oob_is_err=False).then_inc(s_q, 16)
                g.wait_ge(s_q, 16 * (2 + NT * TOPK))
                g.dma_reset(every)

        nc.all_engine_barrier(sems_to_clear=every)
        with nc.Fori(0, E) as ex:
            have = nc.values_load(CNT[0:1, bass.ds(ex, 1)], min_val=0, max_val=CAP)
            with nc.Fori(0, NMORE) as j:
                with nc.If(have > j * 128 + LOW):
                    for e in everyone:
                        e.nop()
                    with nc.Block() as block:

                        @block.sync
                        def _(y):
                            y.dma_start(OID[:, :], IDS[bass.ds(ex * IDROWS + j * 128 + LOW, 128), :]).then_inc(s_p, 16)
                            y.dma_start(OW[:, 0:WPK], wpk[bass.ds(ex, 1), :, :].rearrange("a p n -> (a p) n")).then_inc(s_w, 16)
                            y.dma_start(OW[0:IB, WPK:], wtl[bass.ds(ex, 1), :, :].rearrange("a p n -> (a p) n")).then_inc(s_w, 16)
                            y.wait_ge(s_w, 32)

                        @block.gpsimd
                        def _(g):
                            g.wait_ge(s_v, 3)
                            g.indirect_dma_start(OX[:, :], None, TOK[:, :], bass.IndirectOffsetOnAxis(ap=OTK[:, :], axis=0),
                                                 bounds_check=B * T - 1, oob_is_err=False).then_inc(s_g, 16)
                            g.indirect_dma_start(OWT[:, :], None, WTS[:, :], bass.IndirectOffsetOnAxis(ap=OID[:, :], axis=0),
                                                 bounds_check=NPAIR - 1, oob_is_err=False).then_inc(s_g, 16)
                            g.wait_ge(s_v, 9)
                            g.indirect_dma_start(YS[:, :], bass.IndirectOffsetOnAxis(ap=OID[:, :], axis=0), OY[:, :], None,
                                                 bounds_check=NPAIR - 1, oob_is_err=False).then_inc(s_q, 16)
                            g.wait_ge(s_q, 16)
                            g.dma_reset(every)

                        @block.vector
                        def _(v):
                            v.memset(OX[:, :], 0.0).then_inc(s_v, 1)
                            v.memset(OWT[:, :], 0.0).then_inc(s_v, 1)
                            v.wait_ge(s_p, 16)
                            v.tensor_scalar(OTK[:, :], OID[:, :], 2, None, ALU.logical_shift_right).then_inc(s_v, 1)
                            v.wait_ge(s_t, 1)
                            v.tensor_copy(OXT[:, :], p0[:, 0:C]).then_inc(s_v, 1)
                            v.wait_ge(s_c, 2)
                            v.tensor_tensor(OH_[:, 0:IA], OSG[:, 0:IA], p1[:, IA:2 * IA], ALU.mult).then_inc(s_v, 1)
                            v.tensor_tensor(OH_[:, IA:I], OSG[:, IA:I], p1[:, I + IA:2 * I], ALU.mult).then_inc(s_v, 1)
                            v.wait_ge(s_t, 3)
                            v.tensor_copy(OHT[0:IA, 0, :], p2[0:IA, 0:128]).then_inc(s_v, 1)
                            v.tensor_copy(OHT[0:IB, 1, :], p2[0:IB, 128:256]).then_inc(s_v, 1)
                            v.wait_ge(s_t, 4)
                            v.tensor_scalar(OY[:, :], p3[:, 0:C], OWT[:, 0:1], None, ALU.mult).then_inc(s_v, 1)

                        @block.scalar
                        def _(a):
                            a.wait_ge(s_t, 2)
                            a.activation(OSG[:, 0:IA], p1[:, 0:IA], ACT.Silu).then_inc(s_c, 1)
                            a.activation(OSG[:, IA:I], p1[:, 2 * IA:I + IA], ACT.Silu).then_inc(s_c, 1)

                        @block.tensor
                        def _(t):
                            t.wait_ge(s_g, 32)
                            t.transpose(p0[:, 0:128], OX[:, 0:128], IDF)
                            t.transpose(p0[:, 128:256], OX[:, 128:256], IDF).then_inc(s_t, 1)
                            t.wait_ge(s_w, 32)
                            t.wait_ge(s_v, 4)
                            t.matmul(p1[:, 0:2 * I], OXT[:, 0:128], OW[:, 0:2 * I], start=True, stop=False)
                            t.matmul(p1[:, 0:2 * I], OXT[:, 128:256], OW[:, 2 * I:4 * I], start=False, stop=True).then_inc(s_t, 1)
                            t.wait_ge(s_v, 6)
                            t.transpose(p2[0:IA, 0:128], OH_[:, 0:IA], IDF)
                            t.transpose(p2[0:IB, 128:256], OH_[:, IA:I], IDF).then_inc(s_t, 1)
                            t.wait_ge(s_v, 8)
                            t.matmul(p3[:, 0:C], OHT[0:IA, 0, :], OW[0:IA, 4 * I:4 * I + C], start=True, stop=False)
                            t.matmul(p3[:, 0:C], OHT[0:IB, 1, :], OW[0:IB, 4 * I + C:], start=False, stop=True).then_inc(s_t, 1)

                    nc.all_engine_barrier(sems_to_clear=every)

        with nc.Block() as block:
            yv = YS.rearrange("(n p k) c -> n p k c", p=128, k=TOPK)

            @block.sync
            def _(y):
                for i in range(NT):
                    if i:
                        y.wait_ge(s_v, 2 * i - 1)
                    y.dma_start(OF[:, :, :], yv[i]).then_inc(s_w, 16)
                    y.wait_ge(s_v, 2 * i + 2)
                    y.dma_start(ov[:, i, :], OO[:, :]).then_inc(s_p, 16)
                    y.wait_ge(s_p, 16 * i + 16)

            @block.vector
            def _(v):
                for i in range(NT):
                    v.wait_ge(s_w, 16 * i + 16)
                    if i:
                        v.wait_ge(s_p, 16 * i)
                    v.tensor_reduce(OO[:, :], OF[:, :, :].rearrange("p k c -> p c k"), AX.X, ALU.add).then_inc(s_v, 1)
                    v.wait_ge(s_v, 2 * i + 1)
                    v.tensor_tensor(OO[:, :], OO[:, :], X[:, i, :], ALU.add).then_inc(s_v, 1)
    ctx.close()


def layout(x, wq, wk, wv, wo, gate, sgate, w13, w2, sgu, sdn):
    wqkv = np.concatenate([wk, wq, wv], 1)
    wos = wo.reshape(2, 2, 4, HD, C).transpose(0, 2, 1, 3, 4).reshape(C, C)
    gw = np.concatenate([gate, sgate, np.zeros((3, C), gate.dtype)], 0).T
    g, u = sgu[:ISH], sgu[ISH:]
    order = [w[f:min(f + 128, ISH)] for f in range(0, ISH, 128) for w in (g, u)]
    wsh1 = np.concatenate(order, 0).T
    sdt = sdn.T
    wsh2 = np.concatenate([sdt, sdt[640:]], 0)
    w13 = np.concatenate([w13[:, 0:IA], w13[:, I:I + IA], w13[:, IA:I], w13[:, I + IA:]], 1)
    a = w13.transpose(0, 2, 1).reshape(E, 2, 128, 2 * I).transpose(0, 2, 1, 3).reshape(E, 128, 4 * I)
    w2t = w2.transpose(0, 2, 1)
    wpk, wtl = np.concatenate([a, w2t[:, :128]], 2), w2t[:, IA:]
    flat = dict(x=x.reshape(B * T, C), wqkv=wqkv, wos=wos, gw=gw, wsh1=wsh1, wsh2=wsh2, wpk=wpk, wtl=wtl, cst=constants())
    return {k: np.ascontiguousarray(v) for k, v in flat.items()}


def kernel(L0_attn_x, L0_attn_q_kernel, L0_attn_k_kernel, L0_attn_v_kernel, L0_attn_out_kernel, L0_ffn_gate_w,
           L0_ffn_shared_gate_w, L0_ffn_w13, L0_ffn_w2, L0_ffn_se_gate_up_w, L0_ffn_se_down_w):
    import concourse.bacc as _bacc
    from concourse.bass_utils import run_bass_kernel_spmd as _run

    given = [np.asarray(a) for a in (
        L0_attn_x, L0_attn_q_kernel, L0_attn_k_kernel, L0_attn_v_kernel, L0_attn_out_kernel, L0_ffn_gate_w,
        L0_ffn_shared_gate_w, L0_ffn_w13, L0_ffn_w2, L0_ffn_se_gate_up_w, L0_ffn_se_down_w)]
    nc = _bacc.Bacc("TRN2", target_bir_lowering=False, num_devices=1)
    arrays, args = {}, []
    for name, a in layout(*given).items():
        arrays[f"in_{name}"] = a
        args.append(nc.dram_tensor(f"in_{name}", a.shape, mybir.dt.from_np(a.dtype), kind="ExternalInput").ap())
    args.append(nc.dram_tensor("out_0_dram", (B * T, C), F32, kind="ExternalOutput").ap())
    moe_block_kernel(nc, *args)
    r = _run(nc, [arrays], core_ids=[0])
    return r.results[0]["out_0_dram"].reshape(B, T, C)
```
